# Optimizing a Trainium2 kernel written in Bass

```python
import numpy as np
import jax
import jax.numpy as jnp

def _softmax(x, axis=-1):
    return jax.nn.softmax(x, axis=axis)

def _gelu(x):
    return jax.nn.gelu(x, approximate=True)

def _silu(x):
    return jax.nn.silu(x)

def _sigmoid(x):
    return jax.nn.sigmoid(x)

def _layernorm(x, axis=-1, eps=1e-05):
    m = jnp.mean(x, axis=axis, keepdims=True)
    v = jnp.var(x, axis=axis, keepdims=True)
    return (x - m) / jnp.sqrt(v + eps)

def _scatter_add(tgt, idx, src, axis=0):
    return tgt.at[idx].add(src)

def _segment_sum(src, seg, n):
    return jax.ops.segment_sum(src, seg, n)
kernel_name = 'mk_gps_d1_gnn_r8_110221'

def setup_inputs(seed: int=0):
    np.random.seed(seed)
    _w = jnp.asarray

    def _rec_inputs():
        import jax
        import jax.numpy as jnp
        _gk = jax.random.key(seed)
        x = -0.0003019 + 1 * jax.random.normal(jax.random.fold_in(_gk, 1), (1250, 1024), jnp.float32)
        src = jax.random.randint(jax.random.fold_in(_gk, 2), (20000,), 0, 1250, jnp.int32)
        dst = jax.random.randint(jax.random.fold_in(_gk, 3), (20000,), 0, 1250, jnp.int32)
        _o = jnp.argsort(dst, stable=True)
        src = src[_o]
        dst = dst[_o]
        return (x, src, dst)
    x, src, dst = _rec_inputs()

    def _L0_gnn_setup():
        import jax, jax.numpy as jnp
        import numpy as np
        N = 2500
        E = 40000
        D_IN = 1024
        D_OUT = 1024
        key = jax.random.key(seed)
        k1, k2, k3, k4 = jax.random.split(key, 4)
        x = jax.random.normal(k1, (N, D_IN), dtype=jnp.float32)
        edge_index = jax.random.randint(k2, (2, E), 0, N, dtype=jnp.int64)
        W = jax.random.normal(k3, (D_OUT, D_IN), dtype=jnp.float32) * (1.0 / np.sqrt(D_IN))
        b = jax.random.normal(k4, (D_OUT,), dtype=jnp.float32) * 0.01
        return {'x': x, 'edge_index': edge_index, 'W': W, 'b': b}
    _L0_gnn_all = _L0_gnn_setup()
    _L0_gnn_in = {k: v for k, v in _L0_gnn_all.items() if k in ('W', 'b')}
    del _L0_gnn_all

    def _L0_mix_setup():
        import jax, jax.numpy as jnp
        import numpy as np
        D_MODEL = 1024
        N_HEADS = 16
        D_K = 64
        key = jax.random.key(seed)
        k0, k1, k2, k3, k4 = jax.random.split(key, 5)
        B, S = (4, 512)
        std = 0.02
        x = jax.random.normal(k0, (B, S, D_MODEL), dtype=jnp.float32)
        W_q = std * jax.random.normal(k1, (N_HEADS * D_K, D_MODEL), dtype=jnp.float32)
        W_k = std * jax.random.normal(k2, (N_HEADS * D_K, D_MODEL), dtype=jnp.float32)
        W_v = std * jax.random.normal(k3, (N_HEADS * D_K, D_MODEL), dtype=jnp.float32)
        W_o = std * jax.random.normal(k4, (D_MODEL, N_HEADS * D_K), dtype=jnp.float32)
        return {'x': x, 'W_q': W_q, 'W_k': W_k, 'W_v': W_v, 'W_o': W_o}
    _L0_mix_all = _L0_mix_setup()
    _L0_mix_in = {k: v for k, v in _L0_mix_all.items() if k in ('W_q', 'W_k', 'W_v', 'W_o')}
    del _L0_mix_all

    def _L0_ffn_setup():
        import jax, jax.numpy as jnp
        import numpy as np
        K = 4
        ROUTED_SCALING = 1.0
        NORM_TOPK = True

        def _gate(hidden_states, router_w, router_bias):
            logits = jnp.einsum('bsh,he->bse', hidden_states, router_w).astype(jnp.float32)
            scores = jax.nn.softmax(logits, axis=-1)
            corrected = scores + router_bias
            _, top_k_indices = jax.lax.top_k(corrected, K)
            top_k_weights = jnp.take_along_axis(scores, top_k_indices, axis=-1)
            if NORM_TOPK:
                top_k_weights = top_k_weights / (top_k_weights.sum(-1, keepdims=True) + 1e-20)
            top_k_weights = top_k_weights * ROUTED_SCALING
            return (top_k_weights.astype(hidden_states.dtype), top_k_indices)
        key = jax.random.key(seed)
        ks = jax.random.split(key, 9)
        B, S, H, E, I, IS = (2, 1024, 1024, 8, 512, 256)
        sc = 0.02
        return {'hidden_states': jax.random.normal(ks[0], (B, S, H), jnp.float32), 'router_w': jax.random.normal(ks[1], (H, E), jnp.float32) * sc, 'router_bias': jnp.zeros((), jnp.float32), 'gate_w': jax.random.normal(ks[2], (E, H, I), jnp.float32) * sc, 'up_w': jax.random.normal(ks[3], (E, H, I), jnp.float32) * sc, 'down_w': jax.random.normal(ks[4], (E, I, H), jnp.float32) * sc, 's_gate_w': jax.random.normal(ks[5], (H, IS), jnp.float32) * sc, 's_up_w': jax.random.normal(ks[6], (H, IS), jnp.float32) * sc, 's_down_w': jax.random.normal(ks[7], (IS, H), jnp.float32) * sc}
    _L0_ffn_all = _L0_ffn_setup()
    _L0_ffn_in = {k: v for k, v in _L0_ffn_all.items() if k in ('router_w', 'router_bias', 'gate_w', 'up_w', 'down_w', 's_gate_w', 's_up_w', 's_down_w')}
    del _L0_ffn_all
    return {'x': x, 'src': src, 'dst': dst, 'L0_gnn_W': _L0_gnn_in['W'], 'L0_gnn_b': _L0_gnn_in['b'], 'L0_mix_W_q': _L0_mix_in['W_q'], 'L0_mix_W_k': _L0_mix_in['W_k'], 'L0_mix_W_v': _L0_mix_in['W_v'], 'L0_mix_W_o': _L0_mix_in['W_o'], 'L0_ffn_router_w': _L0_ffn_in['router_w'], 'L0_ffn_router_bias': _L0_ffn_in['router_bias'], 'L0_ffn_gate_w': _L0_ffn_in['gate_w'], 'L0_ffn_up_w': _L0_ffn_in['up_w'], 'L0_ffn_down_w': _L0_ffn_in['down_w'], 'L0_ffn_s_gate_w': _L0_ffn_in['s_gate_w'], 'L0_ffn_s_up_w': _L0_ffn_in['s_up_w'], 'L0_ffn_s_down_w': _L0_ffn_in['s_down_w']}

def reference(x, src, dst, L0_gnn_W, L0_gnn_b, L0_mix_W_q, L0_mix_W_k, L0_mix_W_v, L0_mix_W_o, L0_ffn_router_w, L0_ffn_router_bias, L0_ffn_gate_w, L0_ffn_up_w, L0_ffn_down_w, L0_ffn_s_gate_w, L0_ffn_s_up_w, L0_ffn_s_down_w):
    import jax
    import jax.numpy as jnp

    def _L0_gnn_ref(x, edge_index, W, b):
        import jax, jax.numpy as jnp
        import numpy as np
        N = 2500
        E = 40000
        D_IN = 1024
        D_OUT = 1024
        num_nodes = x.shape[0]
        self_idx = jnp.arange(num_nodes, dtype=edge_index.dtype)
        ei = jnp.concatenate([edge_index, jnp.stack([self_idx, self_idx], axis=0)], axis=1)
        row, col = (ei[0], ei[1])
        h = jnp.einsum('nd,od->no', x, W) + b
        deg = jnp.zeros((num_nodes,), dtype=h.dtype).at[row].add(1.0)
        deg_inv_sqrt = deg ** (-0.5)
        norm = deg_inv_sqrt[row] * deg_inv_sqrt[col]
        msg = norm[:, None] * h[col]
        out = jax.ops.segment_sum(msg, row, num_segments=num_nodes)
        return out

    def _L0_mix_ref(x, W_q, W_k, W_v, W_o):
        import jax, jax.numpy as jnp
        import numpy as np
        D_MODEL = 1024
        N_HEADS = 16
        D_K = 64
        B, S, _ = x.shape
        H, Dk = (N_HEADS, D_K)
        q = (x @ W_q.T).reshape(B, S, H, Dk)
        k = (x @ W_k.T).reshape(B, S, H, Dk)
        v = (x @ W_v.T).reshape(B, S, H, Dk)
        scale = 1.0 / jnp.sqrt(jnp.float32(Dk))
        kv = jnp.einsum('bshd,bshe->bhde', k, v)
        attn = jnp.einsum('bshd,bhde->bshe', q, kv) * scale
        out = attn.reshape(B, S, H * Dk) @ W_o.T
        return out

    def _L0_ffn_ref(hidden_states, router_w, router_bias, gate_w, up_w, down_w, s_gate_w, s_up_w, s_down_w):
        import jax, jax.numpy as jnp
        import numpy as np
        K = 4
        ROUTED_SCALING = 1.0
        NORM_TOPK = True

        def _gate(hidden_states, router_w, router_bias):
            logits = jnp.einsum('bsh,he->bse', hidden_states, router_w).astype(jnp.float32)
            scores = jax.nn.softmax(logits, axis=-1)
            corrected = scores + router_bias
            _, top_k_indices = jax.lax.top_k(corrected, K)
            top_k_weights = jnp.take_along_axis(scores, top_k_indices, axis=-1)
            if NORM_TOPK:
                top_k_weights = top_k_weights / (top_k_weights.sum(-1, keepdims=True) + 1e-20)
            top_k_weights = top_k_weights * ROUTED_SCALING
            return (top_k_weights.astype(hidden_states.dtype), top_k_indices)
        B, S, H = hidden_states.shape
        tk_w, tk_i = _gate(hidden_states, router_w, router_bias)
        hf = hidden_states.reshape(-1, H)
        tk_w = tk_w.reshape(-1, K)
        tk_i = tk_i.reshape(-1, K)
        gate_all = jnp.einsum('nh,ehi->nei', hf, gate_w)
        up_all = jnp.einsum('nh,ehi->nei', hf, up_w)
        act = jax.nn.silu(gate_all) * up_all
        down_all = jnp.einsum('nei,eih->neh', act, down_w)
        sel = jnp.take_along_axis(down_all, tk_i[:, :, None], axis=1)
        routed = (sel * tk_w[:, :, None]).sum(axis=1).reshape(B, S, H)
        g = jnp.einsum('bsh,hm->bsm', hidden_states, s_gate_w)
        u = jnp.einsum('bsh,hm->bsm', hidden_states, s_up_w)
        shared = jnp.einsum('bsm,mh->bsh', jax.nn.silu(g) * u, s_down_w)
        return routed + shared
    edge_index = jnp.stack([src, dst])
    xn = _layernorm(x, axis=-1)
    x = x + _L0_gnn_ref(xn, edge_index, L0_gnn_W, L0_gnn_b) + _L0_mix_ref(xn[None], L0_mix_W_q, L0_mix_W_k, L0_mix_W_v, L0_mix_W_o)[0]
    x = x + _L0_ffn_ref(_layernorm(x, axis=-1)[None], L0_ffn_router_w, L0_ffn_router_bias, L0_ffn_gate_w, L0_ffn_up_w, L0_ffn_down_w, L0_ffn_s_gate_w, L0_ffn_s_up_w, L0_ffn_s_down_w)[0]
    return x

_drawn_inputs = setup_inputs


def setup_inputs(seed=0):
    import zlib

    import numpy as np

    out = dict(_drawn_inputs(seed))
    spreads = {}
    factors = {'L0_gnn_W': 2.684,
     'L0_gnn_b': 42.131,
     'L0_ffn_router_w': 8.0,
     'L0_ffn_gate_w': 8.0,
     'L0_ffn_up_w': 8.0,
     'L0_ffn_down_w': 8.0,
     'L0_ffn_s_gate_w': 8.0,
     'L0_ffn_s_up_w': 8.0,
     'L0_ffn_s_down_w': 8.0}
    for name, (base, spread) in spreads.items():
        noise = np.random.default_rng([zlib.crc32(name.encode()), seed]).standard_normal(out[name].shape)
        drawn = base * np.exp(spread * noise) if base else spread * noise
        out[name] = jnp.asarray(drawn.astype(out[name].dtype))
    for name, factor in factors.items():
        out[name] = (out[name] * factor).astype(out[name].dtype)
    return out
```

```python
import concourse.bass as bass
from concourse import mybir
from contextlib import ExitStack

F32 = mybir.dt.float32
F32R = mybir.dt.float32r
BF16 = mybir.dt.bfloat16
F16 = mybir.dt.float16
I32 = mybir.dt.int32
U32 = mybir.dt.uint32
ALU = mybir.AluOpType
ACT = mybir.ActivationFunctionType
AX = mybir.AxisListType.X

N = 1250
D = 1024
P = 128
T = 125
NT = N // T
C = D // P
HALF = 512
EPS = 1e-5


class Phase(ExitStack):
    def __init__(self, nc):
        super().__init__()
        self.nc, self.sems = nc, []

    def sem(self, name):
        self.sems.append(self.nc.alloc_semaphore(name))
        return self.sems[-1]

    def block(self):
        self.opened = self.nc.Block()
        return self.opened.__enter__()

    def __exit__(self, *error):
        self.opened.__exit__(*error)
        if error[0] is None:
            self.clear()
        return super().__exit__(*error)

    def clear(self):
        with self.nc.Block() as block:
            @block.gpsimd
            def _(pool):
                for s in self.sems:
                    pool.sem_clear(s)
        for s in self.sems:
            self.nc.release_semaphore(s)


def hold(carrier, sem, value):
    carrier.eng.wait_ge(sem, value)
    if not isinstance(value, int):
        return carrier.issue()


class Carrier:
    def __init__(self, nc, scr, eng, on):
        self.nc, self.scr, self.eng, self.on = nc, scr, eng, on

    def issue(self):
        self.scr["spare_used"] += 1
        at = self.scr["spare"][0:1, self.scr["spare_used"]:self.scr["spare_used"] + 1]
        zero = self.scr["spare"][0:1, 0:1]
        if self.on == "scalar":
            return self.nc.scalar.copy(at, zero)
        if self.on == "gpsimd":
            return self.nc.gpsimd.tensor_tensor(at, zero, zero, ALU.add)
        return self.nc.vector.memset(at, 0.0)


def layernorm(nc, carrier, src, dst, stats, mv, small, step, base, var_ready, std_ready, normed, t):
    dve = carrier.eng
    for h in range(2):
        i = nc.vector.bn_stats(stats[:, h, :], src[:, h * HALF:(h + 1) * HALF])
    i.then_inc(step, 1)
    hold(carrier, step, base + 1)
    nc.vector.bn_aggr(mv[:, :], stats[:, :, :]).then_inc(step, 1)
    dve.wait_ge(step, base + 2)
    nc.vector.tensor_scalar_add(small[:, 0:1], mv[:, 1:2], EPS).then_inc(var_ready, 1)
    dve.wait_ge(std_ready, t + 1)
    inverse_root(nc, dve, small, step, base + 2)
    dve.wait_ge(step, base + 6)
    nc.vector.tensor_scalar(dst, src, mv[:, 0:1], small[:, 6:7], ALU.subtract, ALU.mult).then_inc(normed, 1)
    dve.wait_ge(normed, t + 1)
    nc.vector.memset(small[:, 7:8], 0.0).then_inc(step, 1)


def inverse_root(nc, dve, small, step, base):
    nc.vector.reciprocal(small[:, 2:3], small[:, 1:2]).then_inc(step, 1)
    dve.wait_ge(step, base + 1)
    nc.vector.scalar_tensor_tensor(small[:, 3:4], small[:, 2:3], small[:, 2:3], small[:, 0:1], ALU.mult, ALU.mult).then_inc(step, 1)
    dve.wait_ge(step, base + 2)
    nc.vector.tensor_scalar(small[:, 5:6], small[:, 3:4], -0.5, 1.5, ALU.mult, ALU.add).then_inc(step, 1)
    dve.wait_ge(step, base + 3)
    nc.vector.tensor_tensor(small[:, 6:7], small[:, 5:6], small[:, 2:3], ALU.mult).then_inc(step, 1)


def mm3(pe, out, lhs_hi, lhs_lo, rhs_hi, rhs_lo, start, stop):
    pe.matmul(out, lhs_lo, rhs_hi, start=start, stop=False)
    pe.matmul(out, lhs_hi, rhs_lo, start=False, stop=False)
    return pe.matmul(out, lhs_hi, rhs_hi, start=False, stop=stop)


def project_kv(nc, io, scr):
    with Phase(nc) as ctx:
        sb = lambda n, s, d: ctx.enter_context(nc.sbuf_tensor(n, s, d))
        ps = lambda n, s: ctx.enter_context(nc.psum_tensor(n, s, F32))
        sem = ctx.sem
        w_hi = sb("p1_w_hi", [P, 2, C, D], F32R)
        w_lo = sb("p1_w_lo", [P, 2, C, D], F32R)
        RAW = 4
        raw = sb("p1_raw", [P, RAW, D], F32)
        x = sb("p1_x", [T, 2, D], F32)
        xT_hi = sb("p1_xT_hi", [P, 2, C * T], F32R)
        xT_lo = sb("p1_xT_lo", [P, 2, C * T], F32R)
        kv_hi = sb("p1_kv_hi", [T, 4 * HALF], F32R)
        kv_lo = sb("p1_kv_lo", [T, 4 * HALF], F32R)
        stats = sb("p1_stats", [T, 2, 6], F32)
        mv = sb("p1_mv", [T, 2], F32)
        small = sb("p1_small", [T, 8], F32)
        kvT = scr["kvT"]
        ident = scr["ident"]
        xp = [ps(f"p1_xp{i}", [P, 4 * T]) for i in range(2)]
        pkv = [ps(f"p1_kv{i}", [T, HALF]) for i in range(4)]
        pT = [ps(f"p1_kvT{i}", [P, HALF]) for i in range(2)]

        s_raw = [sem(f"p1_raw_in{i}") for i in range(RAW)]
        w_hi_done, w_lo_done = sem("p1_w_hi_done"), sem("p1_w_lo_done")
        x_in = [sem(f"p1_x_in{i}") for i in range(2)]
        var_ready, std_ready, ln_step = sem("p1_var"), sem("p1_std"), sem("p1_ln_step")
        xn_ready, xT_mm, xT_hi_done, xT_lo_done = sem("p1_xn"), sem("p1_xT_mm"), sem("p1_xT_hi_done"), sem("p1_xT_lo_done")
        xT_out = [sem(f"p1_xT_out{i}") for i in range(2)]
        kv_mm, kv_hi_done, kv_lo_done = sem("p1_kv_mm"), sem("p1_kv_hi_done"), sem("p1_kv_lo_done")
        kvT_mm, kvT_added = sem("p1_kvT_mm"), sem("p1_kvT_added")

        x_dram = io["x"].rearrange("(t p) d -> t p d", p=T)
        w_dram = [io["wkT"].rearrange("(c p) n -> c p n", p=P), io["wvT"].rearrange("(c p) n -> c p n", p=P)]
        block = ctx.block()

        @block.sync
        def _(sp):
            def load_x(t, b, k):
                if k:
                    sp.wait_ge(xT_mm, 2 * (t - 1))
                sp.dma_start(x[:, b, :], x_dram[bass.ds(t, 1), :, :].rearrange("a p d -> (a p) d") if k else x_dram[t, :, :]).then_inc(x_in[b], 16)
            load_x(0, 0, False)
            for n in range(2 * C):
                if n >= RAW:
                    sp.wait_ge(w_lo_done, n - RAW + 1)
                sp.dma_start(raw[:, n % RAW, :], w_dram[n // C][n % C]).then_inc(s_raw[n % RAW], 16)
                if n == 1:
                    load_x(1, 1, False)

            def store_xT(t, b):
                sp.wait_ge(xT_hi_done, 2 * t + 2)
                sp.wait_ge(xT_lo_done, 2 * t + 2)
                sp.dma_start(scr["xT_hi"][bass.ds(t, 1), :, :].rearrange("a p d -> (a p) d"), xT_hi[:, b, :].bitcast(F32)).then_inc(xT_out[b], 16)
                sp.dma_start(scr["xT_lo"][bass.ds(t, 1), :, :].rearrange("a p d -> (a p) d"), xT_lo[:, b, :].bitcast(F32)).then_inc(xT_out[b], 16)
            with sp.Fori(0, NT // 2 - 1) as i:
                for b in range(2):
                    load_x(2 * i + 2 + b, b, True)
                    store_xT(2 * i + b, b)
            for b in range(2):
                store_xT(NT - 2 + b, b)
            for b in range(2):
                sp.wait_ge(xT_out[b], 32 * (NT // 2))

        def xT_halves(act, t, b, guard):
            if guard:
                act.wait_ge(kv_mm, 4 * t - 4)
                act.wait_ge(xT_out[b], 16 * (t - b))
            for h in range(2):
                act.wait_ge(xT_mm, 2 * t + h + 1)
                nc.scalar.copy(xT_hi[:, b, h * 4 * T:(h + 1) * 4 * T], xp[h][:, :]).then_inc(xT_hi_done, 1)

        def kv_half(act, t, q):
            if q == 0:
                act.wait_ge(kvT_mm, t)
            act.wait_ge(kv_mm, 4 * t + q + 1)
            nc.scalar.copy(kv_hi[:, q * HALF:(q + 1) * HALF], pkv[q][:, :]).then_inc(kv_hi_done, 1)

        @block.scalar
        def _(act):
            act_carrier = Carrier(nc, scr, act, "scalar")
            for n in range(2 * C):
                act.wait_ge(s_raw[n % RAW], 16 * (n // RAW + 1))
                nc.scalar.activation(w_hi[:, n // C, n % C, :], raw[:, n % RAW, :], ACT.Copy).then_inc(w_hi_done, 1)
                if n == 3:
                    act.wait_ge(var_ready, 1)
                    nc.scalar.activation(small[:, 1:2], small[:, 0:1], ACT.Sqrt).then_inc(std_ready, 1)
                if n == 5:
                    xT_halves(act, 0, 0, False)

            def tile(t, b, last=False):
                kv_half(act, t, 0)
                if not last:
                    hold(act_carrier, var_ready, t + 2)
                    nc.scalar.activation(small[:, 1:2], small[:, 0:1], ACT.Sqrt).then_inc(std_ready, 1)
                kv_half(act, t, 1)
                if not last:
                    xT_halves(act, t + 1, 1 - b, True)
                kv_half(act, t, 2)
                kv_half(act, t, 3)

            for b in range(2):
                tile(b, b)
            with act.Fori(1, NT // 2 - 1) as i:
                for b in range(2):
                    tile(2 * i + b, b)
            for b in range(2):
                tile(NT - 2 + b, b, last=b == 1)

        @block.vector
        def _(dve):
            dve_carrier = Carrier(nc, scr, dve, "vector")

            def norm(t, b):
                dve.wait_ge(x_in[b], 8 * (t - b) + 16)
                layernorm(nc, dve_carrier, x[:, b, :], x[:, b, :], stats, mv, small, ln_step, 7 * t, var_ready, std_ready, xn_ready, t)

            def xT_low(t, b):
                for h in range(2):
                    dve.wait_ge(xT_hi_done, 2 * t + h + 1)
                    at = slice(h * 4 * T, (h + 1) * 4 * T)
                    nc.vector.tensor_tensor(xT_lo[:, b, at], xp[h][:, :], xT_hi[:, b, at].bitcast(F32), ALU.subtract).then_inc(xT_lo_done, 1)

            def kv_low(t, q):
                dve.wait_ge(kv_hi_done, 4 * t + q + 1)
                at = slice(q * HALF, (q + 1) * HALF)
                nc.vector.tensor_tensor(kv_lo[:, at], pkv[q][:, :], kv_hi[:, at].bitcast(F32), ALU.subtract).then_inc(kv_lo_done, 1)

            def add_kvT(t):
                for h in range(2):
                    dve.wait_ge(kvT_mm, t + 1)
                    dve.wait_ge(kvT_added, 2 * t + h + 1)
                    at = slice(h * HALF, (h + 1) * HALF)
                    nc.vector.tensor_tensor(kvT[:, at], kvT[:, at], pT[h][:, :], ALU.add).then_inc(kvT_added, 1)

            def tile(t, b, first=False, last=False):
                if not first:
                    add_kvT(t - 1)
                kv_low(t, 0)
                if not last:
                    norm(t + 1, 1 - b)
                kv_low(t, 1)
                if not last:
                    xT_low(t + 1, 1 - b)
                kv_low(t, 2)
                kv_low(t, 3)

            for h in range(2):
                nc.vector.memset(kvT[:, h * HALF:(h + 1) * HALF], 0.0).then_inc(kvT_added, 1)
            for n in range(2 * C):
                dve.wait_ge(w_hi_done, n + 1)
                nc.vector.tensor_tensor(w_lo[:, n // C, n % C, :], raw[:, n % RAW, :], w_hi[:, n // C, n % C, :].bitcast(F32), ALU.subtract).then_inc(w_lo_done, 1)
                if n == 0:
                    norm(0, 0)
                if n == 5:
                    xT_low(0, 0)
            tile(0, 0, first=True)
            tile(1, 1)
            with dve.Fori(1, NT // 2 - 1) as i:
                for b in range(2):
                    tile(2 * i + b, b)
            for b in range(2):
                tile(NT - 2 + b, b, last=b == 1)
            add_kvT(NT - 1)

        @block.tensor
        def _(pe):
            def transposes(t, b):
                pe.wait_ge(xn_ready, t + 1)
                pe.wait_ge(xT_lo_done, 2 * t)
                for c in range(C):
                    i = pe.transpose(xp[c // 4][:, (c % 4) * T:(c % 4 + 1) * T], x[:, b, c * P:(c + 1) * P], ident[0:T, 0:T])
                    if c % 4 == 3:
                        i.then_inc(xT_mm, 1)

            def project(t, b, q, first):
                pe.wait_ge(xT_lo_done, 2 * t + 2)
                pe.wait_ge(kv_lo_done, 4 * t - 3 + q if not first else 0)
                for c in range(C):
                    if first and t == 0:
                        pe.wait_ge(w_lo_done, (q // 2) * C + c + 1)
                    at = slice(c * T, (c + 1) * T)
                    col = slice((q % 2) * HALF, (q % 2 + 1) * HALF)
                    i = mm3(pe, pkv[q][:, :], xT_hi[:, b, at], xT_lo[:, b, at],
                            w_hi[:, q // 2, c, col], w_lo[:, q // 2, c, col], c == 0, c == C - 1)
                i.then_inc(kv_mm, 1)

            def products(t):
                pe.wait_ge(kv_lo_done, 4 * t + 4)
                pe.wait_ge(kvT_added, 2 * t + 2)
                for j in range(C):
                    k, v = slice(j * P, (j + 1) * P), slice(D + j * P, D + (j + 1) * P)
                    i = mm3(pe, pT[j // 4][:, (j % 4) * P:(j % 4 + 1) * P], kv_hi[:, v], kv_lo[:, v], kv_hi[:, k], kv_lo[:, k], True, True)
                i.then_inc(kvT_mm, 1)

            def tile(t, b, first=False, last=False):
                project(t, b, 0, first)
                if not first:
                    products(t - 1)
                project(t, b, 1, first)
                if not last:
                    transposes(t + 1, 1 - b)
                project(t, b, 2, first)
                project(t, b, 3, first)

            pe.wait_ge(scr["go"], 1)
            transposes(0, 0)
            tile(0, 0, first=True)
            tile(1, 1)
            with pe.Fori(1, NT // 2 - 1) as i:
                for b in range(2):
                    tile(2 * i + b, b)
            for b in range(2):
                tile(NT - 2 + b, b, last=b == 1)
            products(NT - 1)


E = 20000
EC = 125
NCH = E // EC
NPAIR = NCH // 2
PIECES = ((0, 418), (418, 834), (834, 1250))


def adjacency(nc, io, scr):
    with Phase(nc) as ctx:
        sb = lambda n, s, d: ctx.enter_context(nc.sbuf_tensor(n, s, d))
        sem = ctx.sem
        src_i, dst_i = sb("p2_src_i", [EC, NCH], I32), sb("p2_dst_i", [EC, NCH], I32)
        src, dst = sb("p2_src", [EC, NCH], F32), sb("p2_dst", [EC, NCH], F32)
        nodes_i, nodes = sb("p2_nodes_i", [T, N], I32), sb("p2_nodes", [T, N], F16)
        own_i, own = sb("p2_own_i", [T, NT], I32), sb("p2_own", [T, NT], F32)
        at_least = sb("p2_at_least", [EC, NT + 1, NCH], F32)
        inside = sb("p2_inside", [EC, NT, NCH], BF16)
        ones, eye = sb("p2_ones", [EC, 1], BF16), sb("p2_eye", [T, T], BF16)
        up_i, up = sb("p2_up_i", [1, NPAIR, 2], I32), sb("p2_up", [1, NPAIR, 2], F32)
        down = sb("p2_down", [1, NPAIR, 2], F32)
        held, work = sb("p2_held", [1, NT, NCH], F32), sb("p2_work", [1, NT, NCH], F32)
        last, first = sb("p2_last", [1, NT], F32), sb("p2_first", [1, NT], F32)
        before = sb("p2_before", [1, NT], F32)
        bounds = sb("p2_bounds", [1, 2, NT], I32)
        row, col = sb("p2_row", [EC, 2, N], BF16), sb("p2_col", [EC, 2, T], BF16)
        self_row = sb("p2_self_row", [T, N], BF16)
        full, hi, lo = sb("p2_full", [T, 2, N], F32), sb("p2_hi", [T, 2, N], F32R), sb("p2_lo", [T, 2, N], F32R)
        acc = [[ctx.enter_context(nc.psum_tensor(f"p2_acc{a}{b}", [T, HALF], F32)) for b in range(3)] for a in range(2)]

        edges_in, step, counted, bounds_ready = sem("p2_edges_in"), sem("p2_step"), sem("p2_counted"), sem("p2_bounds_ready")
        iotas, inside_ready = sem("p2_iotas"), sem("p2_inside_ready")
        hot_ready, hot_used, self_ready, self_used = sem("p2_hot_ready"), sem("p2_hot_used"), sem("p2_self_ready"), sem("p2_self_used")
        acc_done, hi_done, full_done, lo_done = sem("p2_acc_done"), sem("p2_hi_done"), sem("p2_full_done"), sem("p2_lo_done")
        stored = [sem(f"p2_stored{b}") for b in range(2)]
        block = ctx.block()

        def pairs(eng, b):
            lo_ = eng.value_load(bounds[0:1, 0, bass.ds(b, 1)], min_val=0, max_val=NPAIR - 1)
            hi_ = eng.value_load(bounds[0:1, 1, bass.ds(b, 1)], min_val=1, max_val=NPAIR)
            return lo_, hi_

        @block.sync
        def _(sp):
            sp.dma_start(src_i[:, :], io["src"]).then_inc(edges_in, 16)
            sp.dma_start(dst_i[:, :], io["dst"]).then_inc(edges_in, 16)
            with sp.Fori(0, NT // 2) as i:
                for b in range(2):
                    for part, (name, t) in enumerate((("AT_hi", hi), ("AT_lo", lo))):
                        sp.wait_ge([hi_done, lo_done][part], 2 * i + b + 1 + part)
                        sp.dma_start(scr[name][:, :, bass.ds(2 * i + b, 1), :].rearrange("t p b i -> p t (b i)"),
                                     t[:, b, :].bitcast(F32).rearrange("p (t i) -> p t i", i=T)).then_inc(stored[b], 16)
            for b in range(2):
                sp.wait_ge(stored[b], 32 * (NT // 2) + 1)

        @block.gpsimd
        def _(pool):
            for s in (*stored, lo_done, full_done, self_used):
                pool.sem_inc(s, 1)
            nc.gpsimd.iota(nodes_i[:, :], pattern=[[1, N]], base=0, channel_multiplier=0).then_inc(iotas, 1)
            nc.gpsimd.iota(own_i[:, :], pattern=[[T, NT]], base=0, channel_multiplier=1).then_inc(iotas, 1)
            nc.gpsimd.iota(up_i[:, :, :], pattern=[[1, NPAIR], [0, 2]], base=1, channel_multiplier=0).then_inc(iotas, 1)
            with pool.Fori(0, NT // 2) as i:
                for b in range(2):
                    pool.wait_ge(hi_done, 2 * i + b + 1)
                    pool.wait_ge(full_done, 2 * i + b + 2)
                    pool.wait_ge(stored[b], 32 * i + 1)
                    nc.gpsimd.tensor_tensor(lo[:, b, :], full[:, b, :], hi[:, b, :].bitcast(F32), ALU.subtract).then_inc(lo_done, 1)

        @block.scalar
        def _(act):
            with act.Fori(0, NT // 2) as i:
                for b in range(2):
                    act.wait_ge(stored[b], 32 * i + 1)
                    act.wait_ge(lo_done, 2 * i + 1)
                    act.wait_ge(acc_done, 2 * i + b + 1)
                    for k, (a, z) in enumerate(PIECES):
                        s = nc.scalar.copy(hi[:, b, a:z], acc[b][k][:, 0:z - a])
                    s.then_inc(hi_done, 1)
                    for k, (a, z) in enumerate(PIECES):
                        s = nc.scalar.copy(full[:, b, a:z], acc[b][k][:, 0:z - a])
                    s.then_inc(full_done, 1)

        @block.vector
        def _(dve):
            n = [0]

            def link(ins):
                n[0] += 1
                ins.then_inc(step, 1)
                dve.wait_ge(step, n[0])

            nc.vector.memset(ones[:, :], 1.0)
            nc.vector.tensor_copy(eye[:, :], scr["ident"][0:T, 0:T])
            dve.wait_ge(iotas, 3)
            nc.vector.tensor_copy(nodes[:, :], nodes_i[:, :])
            nc.vector.tensor_copy(own[:, :], own_i[:, :])
            link(nc.vector.tensor_copy(up[:, :, :], up_i[:, :, :]))
            nc.vector.tensor_scalar(down[:, :, :], up[:, :, :], -1.0, NPAIR + 1.0, ALU.mult, ALU.add)
            dve.wait_ge(edges_in, 32)
            nc.vector.tensor_copy(src[:, :], src_i[:, :])
            link(nc.vector.tensor_copy(dst[:, :], dst_i[:, :]))
            for b in range(NT + 1):
                i = nc.vector.tensor_scalar(at_least[:, b, :], dst[:, :], float(b * T), None, ALU.is_ge)
            link(i)
            nc.vector.tensor_tensor(inside[:, :, :], at_least[:, 0:NT, :], at_least[:, 1:NT + 1, :], ALU.subtract).then_inc(inside_ready, 1)
            dve.wait_ge(counted, 1)
            for k in range(NT // 2):
                i = nc.vector.tensor_scalar(held[:, 2 * k:2 * k + 2, :], acc[k // 3][k % 3][0:1, 0:2 * NCH].rearrange("p (b c) -> p b c", c=NCH), 1.0, None, ALU.min)
            link(i)
            flat = lambda t: t[:, :, :].rearrange("p k j -> p (k j)").unsqueeze(1).to_broadcast([1, NT, NCH])
            link(nc.vector.tensor_tensor(work[:, :, :], held[:, :, :], flat(up), ALU.mult))
            link(nc.vector.tensor_reduce(last[:, :], work[:, :, :], AX, ALU.max))
            link(nc.vector.tensor_tensor(work[:, :, :], held[:, :, :], flat(down), ALU.mult))
            link(nc.vector.tensor_reduce(first[:, :], work[:, :, :], AX, ALU.max))
            link(nc.vector.tensor_scalar(last[:, :], last[:, :], 1.0, None, ALU.max))
            link(nc.vector.tensor_scalar(first[:, :], first[:, :], -1.0, float(NPAIR), ALU.mult, ALU.add))
            link(nc.vector.tensor_scalar(before[:, :], last[:, :], -1.0, None, ALU.add))
            link(nc.vector.tensor_tensor(first[:, :], first[:, :], before[:, :], ALU.min))
            link(nc.vector.tensor_copy(bounds[:, 0, :], first[:, :]))
            nc.vector.tensor_copy(bounds[:, 1, :], last[:, :]).then_inc(bounds_ready, 1)

            dve.wait_ge(bounds_ready, 1)
            with dve.register("p2_dve_taken") as taken:
                dve.reg_mov(taken, 0)
                with dve.Fori(0, NT // 2) as i:
                    for b in range(2):
                        blk = 2 * i + b
                        lo_, hi_ = pairs(dve, blk)
                        dve.wait_ge(self_used, blk + 1)
                        nc.vector.tensor_scalar(self_row[:, :], nodes[:, :], own[:, bass.ds(blk, 1)], None, ALU.is_equal).then_inc(self_ready, 1)
                        with dve.Fori(lo_, hi_) as p:
                            done = dve.snap(taken)
                            for j in range(2):
                                dve.wait_ge(hot_used, 2 * done + (j + 1))
                                nc.vector.tensor_scalar(col[:, j, :], nodes[:, bass.ds(blk * T, T)], dst[:, bass.ds(2 * p + j, 1)], None, ALU.is_equal)
                                nc.vector.tensor_scalar(row[:, j, :], nodes[:, :], src[:, bass.ds(2 * p + j, 1)], None, ALU.is_equal).then_inc(hot_ready, 1)
                            dve.reg_add(taken, taken, 1)

        @block.tensor
        def _(pe):
            pe.wait_ge(inside_ready, 1)
            for k in range(NT // 2):
                i = pe.matmul(acc[k // 3][k % 3][0:1, 0:2 * NCH], ones[:, :], inside[:, 2 * k:2 * k + 2, :].rearrange("p b c -> p (b c)"), start=True, stop=True)
            i.then_inc(counted, 1)
            pe.wait_ge(bounds_ready, 1)
            pe.sem_inc(hot_used, 2)
            with pe.register("p2_pe_taken") as taken:
                pe.reg_mov(taken, 0)
                with pe.Fori(0, NT // 2) as i:
                    for b in range(2):
                        blk = 2 * i + b
                        lo_, hi_ = pairs(pe, blk)
                        pe.wait_ge(full_done, 2 * i + 1)
                        pe.wait_ge(self_ready, blk + 1)
                        for k, (a, z) in enumerate(PIECES):
                            m = pe.matmul(acc[b][k][:, 0:z - a], eye[:, :], self_row[:, a:z], start=True, stop=False)
                        m.then_inc(self_used, 1)
                        with pe.Fori(lo_, hi_) as p:
                            done = pe.snap(taken)
                            for j in range(2):
                                pe.wait_ge(hot_ready, 2 * done + (j + 1))
                                for k, (a, z) in enumerate(PIECES):
                                    m = pe.matmul(acc[b][k][:, 0:z - a], col[:, j, :], row[:, j, a:z], start=False, stop=False)
                                m.then_inc(hot_used, 1)
                            pe.reg_add(taken, taken, 1)
                        for k in range(3):
                            m = pe.matmul(acc[b][k][0:T, 0:2], scr["zero"][0:T, 0:T], scr["zero"][0:T, 0:2], start=False, stop=True)
                        m.then_inc(acc_done, 1)


def split(nc, act, dve, raw, hi, lo, raw_in, raw_value, hi_done, lo_done, n):
    if act is not None:
        act.wait_ge(raw_in, raw_value)
        nc.scalar.copy(hi, raw).then_inc(hi_done, 1)
    if dve is not None:
        dve.wait_ge(hi_done, n + 1)
        nc.vector.tensor_tensor(lo, raw, hi.bitcast(F32), ALU.subtract).then_inc(lo_done, 1)


def mixing_matrix(nc, io, scr):
    with Phase(nc) as ctx:
        sb = lambda n, s, d: ctx.enter_context(nc.sbuf_tensor(n, s, d))
        sem = ctx.sem
        kv_hi, kv_lo = sb("p3_kv_hi", [P, D], F32R), sb("p3_kv_lo", [P, D], F32R)
        o_raw, o_hi, o_lo = sb("p3_o_raw", [P, 2, D], F32), sb("p3_o_hi", [P, 2, D], F32R), sb("p3_o_lo", [P, 2, D], F32R)
        q_raw, q_hi, q_lo = sb("p3_q_raw", [P, 2, C, P], F32), sb("p3_q_hi", [P, 2, C, P], F32R), sb("p3_q_lo", [P, 2, C, P], F32R)
        kvo_hi, kvo_lo = sb("p3_kvo_hi", [P, C, D], F32R), sb("p3_kvo_lo", [P, C, D], F32R)
        m_hi, m_lo = sb("p3_m_hi", [P, 2, D], F32R), sb("p3_m_lo", [P, 2, D], F32R)
        acc = [[ctx.enter_context(nc.psum_tensor(f"p3_acc{a}{b}", [P, HALF], F32)) for b in range(2)] for a in range(2)]
        o_in, q_in = [sem(f"p3_o_in{b}") for b in range(2)], [sem(f"p3_q_in{b}") for b in range(2)]
        kv_zero, kv_hi_done, kv_lo_done = sem("p3_kv_zero"), sem("p3_kv_hi_done"), sem("p3_kv_lo_done")
        o_hi_done, o_lo_done, q_hi_done, q_lo_done = sem("p3_o_hi_done"), sem("p3_o_lo_done"), sem("p3_q_hi_done"), sem("p3_q_lo_done")
        kvo_mm, kvo_hi_done, kvo_lo_done = sem("p3_kvo_mm"), sem("p3_kvo_hi_done"), sem("p3_kvo_lo_done")
        m_mm, m_hi_done, m_lo_done = sem("p3_m_mm"), sem("p3_m_hi_done"), sem("p3_m_lo_done")
        m_out = [sem(f"p3_m_out{b}") for b in range(2)]
        wo = io["woT"].rearrange("(c p) n -> c p n", p=P)
        wq = io["wq"].rearrange("(j p) c -> p j c", p=P)
        block = ctx.block()

        @block.sync
        def _(sp):
            def load_q(c, b):
                sp.dma_start(q_raw[:, b, :, :], wq[:, :, bass.ds(c * P, P)]).then_inc(q_in[b], 16)

            for j in range(C):
                if j >= 2:
                    sp.wait_ge(o_lo_done, j - 1)
                sp.dma_start(o_raw[:, j % 2, :], wo[j]).then_inc(o_in[j % 2], 16)
            for b in range(2):
                load_q(b, b)

            def store_m(c, b):
                for name, t, done, ahead in (("M_hi", m_hi, m_hi_done, 0), ("M_lo", m_lo, m_lo_done, 3)):
                    sp.wait_ge(done, 2 * c + 2 + ahead)
                    sp.dma_start(scr[name][bass.ds(c, 1), :, :].rearrange("a p n -> (a p) n"), t[:, b, :].bitcast(F32)).then_inc(m_out[b], 16)

            with sp.Fori(0, C // 2 - 1) as i:
                for b in range(2):
                    sp.wait_ge(q_lo_done, 2 * i + b + 1)
                    load_q(2 * i + 2 + b, b)
                    store_m(2 * i + b, b)
            for b in range(2):
                store_m(C - 2 + b, b)
            for b in range(2):
                sp.wait_ge(m_out[b], 16 * C + 1)

        @block.scalar
        def _(act):
            act.wait_ge(kv_zero, 2)
            for h in range(2):
                rows = slice(64 * h, 64 * h + 64)
                d = lambda t: t[rows, :].rearrange("p (j x) -> p j x", x=P)[:, :, 64 * h:64 * h + 64]
                i = nc.scalar.mul(d(kv_hi), d(scr["kvT"]), 0.125)
            i.then_inc(kv_hi_done, 1)

            def product_high(j):
                for h in range(2):
                    act.wait_ge(kvo_mm, 2 * j + h + 1)
                    nc.scalar.copy(kvo_hi[:, j, h * HALF:(h + 1) * HALF], acc[j % 2][h][:, :]).then_inc(kvo_hi_done, 1)

            for j in range(C):
                if j >= 2:
                    act.wait_ge(kvo_mm, 2 * (j - 1))
                split(nc, act, None, o_raw[:, j % 2, :], o_hi[:, j % 2, :], None, o_in[j % 2], 16 * (j // 2 + 1), o_hi_done, None, j)
                if j:
                    product_high(j - 1)
            product_high(C - 1)

            def q_split(c, b):
                split(nc, act, None, q_raw[:, b, :, :], q_hi[:, b, :, :], None, q_in[b], 8 * (c - b) + 16, q_hi_done, None, c)

            for b in range(2):
                q_split(b, b)

            def m_high(c, b):
                act.wait_ge(m_out[b], 16 * (c - b) + 1)
                for h in range(2):
                    act.wait_ge(m_mm, 2 * c + h + 1)
                    nc.scalar.copy(m_hi[:, b, h * HALF:(h + 1) * HALF], acc[b][h][:, :]).then_inc(m_hi_done, 1)

            with act.Fori(0, C // 2 - 1) as i:
                for b in range(2):
                    m_high(2 * i + b, b)
                    q_split(2 * i + 2 + b, b)
            for b in range(2):
                m_high(C - 2 + b, b)

        @block.vector
        def _(dve):
            nc.vector.memset(kv_hi[:, :].bitcast(F32), 0.0).then_inc(kv_zero, 1)
            nc.vector.memset(kv_lo[:, :].bitcast(F32), 0.0).then_inc(kv_zero, 1)
            dve.wait_ge(kv_zero, 2)
            dve.wait_ge(kv_hi_done, 1)
            for h in range(2):
                rows = slice(64 * h, 64 * h + 64)
                d = lambda t: t[rows, :].rearrange("p (j x) -> p j x", x=P)[:, :, 64 * h:64 * h + 64]
                i = nc.vector.scalar_tensor_tensor(d(kv_lo), d(scr["kvT"]), 0.125, d(kv_hi.bitcast(F32)), ALU.mult, ALU.subtract)
            i.then_inc(kv_lo_done, 1)

            def product_low(j):
                for h in range(2):
                    dve.wait_ge(kvo_hi_done, 2 * j + h + 1)
                    at = slice(h * HALF, (h + 1) * HALF)
                    nc.vector.tensor_tensor(kvo_lo[:, j, at], acc[j % 2][h][:, :], kvo_hi[:, j, at].bitcast(F32), ALU.subtract).then_inc(kvo_lo_done, 1)

            for j in range(C):
                split(nc, None, dve, o_raw[:, j % 2, :], o_hi[:, j % 2, :], o_lo[:, j % 2, :], None, 0, o_hi_done, o_lo_done, j)
                if j:
                    product_low(j - 1)
            product_low(C - 1)

            def q_split(c, b):
                split(nc, None, dve, q_raw[:, b, :, :], q_hi[:, b, :, :], q_lo[:, b, :, :], None, 0, q_hi_done, q_lo_done, c)

            for b in range(2):
                q_split(b, b)

            def m_low(c, b):
                for h in range(2):
                    dve.wait_ge(m_hi_done, 2 * c + h + 1)
                    at = slice(h * HALF, (h + 1) * HALF)
                    nc.vector.tensor_tensor(m_lo[:, b, at], acc[b][h][:, :], m_hi[:, b, at].bitcast(F32), ALU.subtract).then_inc(m_lo_done, 1)

            with dve.Fori(0, C // 2 - 1) as i:
                for b in range(2):
                    m_low(2 * i + b, b)
                    q_split(2 * i + 2 + b, b)
            for b in range(2):
                m_low(C - 2 + b, b)

        @block.tensor
        def _(pe):
            for s in m_out:
                pe.sem_inc(s, 1)
            pe.sem_inc(m_lo_done, 3)
            pe.wait_ge(kv_lo_done, 1)
            for j in range(C):
                pe.wait_ge(o_lo_done, j + 1)
                if j >= 2:
                    pe.wait_ge(kvo_lo_done, 2 * (j - 1))
                for h in range(2):
                    at, k = slice(h * HALF, (h + 1) * HALF), slice(j * P, (j + 1) * P)
                    mm3(pe, acc[j % 2][h][:, :], kv_hi[:, k], kv_lo[:, k], o_hi[:, j % 2, at], o_lo[:, j % 2, at], True, True).then_inc(kvo_mm, 1)
            pe.wait_ge(kvo_lo_done, 2 * C)

            with pe.Fori(0, C // 2) as i:
                for b in range(2):
                    pe.wait_ge(q_lo_done, 2 * i + b + 1)
                    pe.wait_ge(m_lo_done, 4 * i + 2 * b + 1)
                    for h in range(2):
                        at = slice(h * HALF, (h + 1) * HALF)
                        for j in range(C):
                            m = mm3(pe, acc[b][h][:, :], q_hi[:, b, j, :], q_lo[:, b, j, :], kvo_hi[:, j, at], kvo_lo[:, j, at], j == 0, j == C - 1)
                        m.then_inc(m_mm, 1)


def load_tile(sp, dst, dram, t, done, view=None):
    src = dram[bass.ds(t, 1)] if not isinstance(t, int) else dram[t:t + 1]
    names = "abc"[:len(dram.shape) - 2]
    sp.dma_start(dst, src.rearrange(f"o p {' '.join(names)} -> (o p) ({' '.join(names)})")).then_inc(done, 16)


def node_features(nc, io, scr):
    with Phase(nc) as ctx:
        sb = lambda n, s, d: ctx.enter_context(nc.sbuf_tensor(n, s, d))
        sem = ctx.sem
        RAW = 2
        w_raw = sb("p4_w_raw", [P, RAW, D], F32)
        w_hi, w_lo = sb("p4_w_hi", [P, C, D], F32R), sb("p4_w_lo", [P, C, D], F32R)
        xT_hi, xT_lo = sb("p4_xT_hi", [P, 2, C * T], F32R), sb("p4_xT_lo", [P, 2, C * T], F32R)
        at_hi, at_lo = sb("p4_at_hi", [T, NT * T], F32R), sb("p4_at_lo", [T, NT * T], F32R)
        bias, h_b = sb("p4_bias", [T, D], F32), sb("p4_h_b", [T, D], F32)
        ones = sb("p4_ones", [T, 2], F32R)
        small = sb("p4_small", [T, 8], F32)
        hs_hi, hs_lo, dinv = scr["hs_hi"], scr["hs_lo"], scr["dinv"]
        ph = [ctx.enter_context(nc.psum_tensor(f"p4_h{b}", [T, HALF], F32)) for b in range(4)]
        pdeg = ctx.enter_context(nc.psum_tensor("p4_deg", [T, 2], F32))
        w_in, x_in = [sem(f"p4_w_in{b}") for b in range(RAW)], [sem(f"p4_x_in{b}") for b in range(2)]
        at_in, bias_in, ones_ready = sem("p4_at_in"), sem("p4_bias_in"), sem("p4_ones")
        w_hi_done, w_lo_done = sem("p4_w_hi_done"), sem("p4_w_lo_done")
        deg_mm, deg_ready, root_ready, step, dinv_ready = sem("p4_deg_mm"), sem("p4_deg"), sem("p4_root"), sem("p4_step"), sem("p4_dinv")
        h_mm, hb_done, hi_done, lo_done = sem("p4_h_mm"), sem("p4_hb_done"), sem("p4_hi_done"), sem("p4_lo_done")
        block = ctx.block()
        wg = io["wgT"].rearrange("(c p) n -> c p n", p=P)

        @block.sync
        def _(sp):
            def loads(t, b):
                load_tile(sp, xT_hi[:, b, :].bitcast(F32), scr["xT_hi"], t, x_in[b])
                load_tile(sp, xT_lo[:, b, :].bitcast(F32), scr["xT_lo"], t, x_in[b])

            def load_at(t):
                load_tile(sp, at_hi[:, :].bitcast(F32), scr["AT_hi"], t, at_in)
                load_tile(sp, at_lo[:, :].bitcast(F32), scr["AT_lo"], t, at_in)

            sp.dma_start(bias[:, :], io["gb"].to_broadcast([T, D])).then_inc(bias_in, 16)
            load_at(0)
            loads(0, 0)
            for c in range(C):
                if c >= RAW:
                    sp.wait_ge(w_lo_done, c - RAW + 1)
                sp.dma_start(w_raw[:, c % RAW, :], wg[c]).then_inc(w_in[c % RAW], 16)
            loads(1, 1)
            sp.wait_ge(deg_mm, 1)
            load_at(1)
            with sp.Fori(1, NT // 2) as i:
                for b in range(2):
                    t = 2 * i + b
                    sp.wait_ge(h_mm, 2 * (t - 1))
                    loads(t, b)
                    sp.wait_ge(deg_mm, t)
                    load_at(t)

        @block.scalar
        def _(act):
            carrier = Carrier(nc, scr, act, "scalar")
            for c in range(C):
                split(nc, act, None, w_raw[:, c % RAW, :], w_hi[:, c, :], None, w_in[c % RAW], 16 * (c // RAW + 1), w_hi_done, None, c)

            def root(t):
                hold(carrier, deg_ready, t + 2)
                nc.scalar.activation(small[:, 1:2], small[:, 0:1], ACT.Sqrt).then_inc(root_ready, 1)

            def tile(t):
                for h in range(2):
                    hold(carrier, hb_done, 2 * t + h + 5)
                    nc.scalar.activation(hs_hi[:, bass.ds(t, 1), h * HALF:(h + 1) * HALF].rearrange("p o n -> p (o n)"),
                                         h_b[:, h * HALF:(h + 1) * HALF], ACT.Copy, scale=dinv[:, bass.ds(t, 1)]).then_inc(hi_done, 1)

            with act.Fori(0, NT) as t:
                root(t)
                tile(t)

        @block.vector
        def _(dve):
            for c in range(C):
                split(nc, None, dve, w_raw[:, c % RAW, :], w_hi[:, c, :], w_lo[:, c, :], None, 0, w_hi_done, w_lo_done, c)
            nc.vector.memset(ones[:, :].bitcast(F32), 1.0).then_inc(ones_ready, 1)
            dve.wait_ge(bias_in, 16)

            def tile(t, b):
                dve.wait_ge(deg_mm, t + 1)
                nc.vector.tensor_copy(small[:, 0:1], pdeg[:, 0:1]).then_inc(deg_ready, 1)
                dve.wait_ge(root_ready, t + 1)
                inverse_root(nc, dve, small, step, 4 * t)
                dve.wait_ge(step, 4 * t + 4)
                nc.vector.tensor_copy(dinv[:, bass.ds(t, 1)], small[:, 6:7]).then_inc(dinv_ready, 1)
                dve.wait_ge(dinv_ready, t + 1)
                for h in range(2):
                    at = slice(h * HALF, (h + 1) * HALF)
                    dve.wait_ge(h_mm, 2 * t + h + 1)
                    nc.vector.tensor_tensor(h_b[:, at], ph[2 * b + h][:, :], bias[:, at], ALU.add).then_inc(hb_done, 1)
                for h in range(2):
                    at = slice(h * HALF, (h + 1) * HALF)
                    dve.wait_ge(hi_done, 2 * t + h + 1)
                    flat = lambda x: x[:, bass.ds(t, 1), at].rearrange("p o n -> p (o n)")
                    nc.vector.scalar_tensor_tensor(flat(hs_lo), h_b[:, at], dinv[:, bass.ds(t, 1)], flat(hs_hi).bitcast(F32), ALU.mult, ALU.subtract).then_inc(lo_done, 1)

            with dve.Fori(0, NT // 2) as i:
                for b in range(2):
                    tile(2 * i + b, b)

        @block.tensor
        def _(pe):
            pe.sem_inc(hb_done, 4)
            pe.sem_inc(deg_ready, 1)
            pe.wait_ge(ones_ready, 1)

            def degree(t):
                pe.wait_ge(deg_ready, t + 1)
                pe.wait_ge(at_in, 32 * t + 32)
                for j in range(NT):
                    at = slice(j * T, (j + 1) * T)
                    pe.matmul(pdeg[:, :], at_lo[:, at], ones[:, :], start=j == 0, stop=False)
                    m = pe.matmul(pdeg[:, :], at_hi[:, at], ones[:, :], start=False, stop=j == NT - 1)
                m.then_inc(deg_mm, 1)

            pe.wait_ge(w_lo_done, C)
            with pe.Fori(0, NT // 2) as i:
                for b in range(2):
                    t = 2 * i + b
                    degree(t)
                    pe.wait_ge(x_in[b], 32 * i + 32)
                    for h in range(2):
                        pe.wait_ge(hb_done, 4 * i + 2 * b + h + 1)
                        col = slice(h * HALF, (h + 1) * HALF)
                        for c in range(C):
                            at = slice(c * T, (c + 1) * T)
                            m = mm3(pe, ph[2 * b + h][:, :], xT_hi[:, b, at], xT_lo[:, b, at], w_hi[:, c, col], w_lo[:, c, col], c == 0, c == C - 1)
                        m.then_inc(h_mm, 1)


EXPERTS = 8


def aggregate_and_mix(nc, io, scr):
    with Phase(nc) as ctx:
        sb = lambda n, s, d: ctx.enter_context(nc.sbuf_tensor(n, s, d))
        ps = lambda n, s: ctx.enter_context(nc.psum_tensor(n, s, F32))
        sem = ctx.sem
        m_hi, m_lo = sb("p5_m_hi", [P, C, D], F32R), sb("p5_m_lo", [P, C, D], F32R)
        at_hi, at_lo = sb("p5_at_hi", [T, 2, NT * T], F32R), sb("p5_at_lo", [T, NT * T], F32R)
        xT_hi, xT_lo = sb("p5_xT_hi", [P, 2, C * T], F32R), sb("p5_xT_lo", [P, C * T], F32R)
        x1, xn = sb("p5_x1", [T, 2, D], F32), sb("p5_xn", [T, D], F32)
        nT_hi, nT_lo = sb("p5_nT_hi", [P, C * T], F32R), sb("p5_nT_lo", [P, C * T], F32R)
        r_raw = sb("p5_r_raw", [P, C, EXPERTS], F32)
        r_parts = sb("p5_r_parts", [P, C, 2, EXPERTS], F32R)
        r_hi, r_lo = r_parts[:, :, 0, :], r_parts[:, :, 1, :]
        log_low = sb("p5_log_low", [T, EXPERTS], F32)
        stats, mv, small = sb("p5_stats", [T, 2, 6], F32), sb("p5_mv", [T, 2], F32), sb("p5_small", [T, 8], F32)
        hs_hi, hs_lo, dinv, logits = scr["hs_hi"], scr["hs_lo"], scr["dinv"], scr["logits"]
        pagg, pmix = [ps(f"p5_agg{h}", [T, HALF]) for h in range(2)], [ps(f"p5_mix{h}", [T, HALF]) for h in range(2)]
        pT = [ps(f"p5_T{h}", [P, 4 * T]) for h in range(2)]
        plog = ps("p5_log", [T, 2, EXPERTS])
        m_in, r_in = [sem(f"p5_m_in{h}") for h in range(2)], sem("p5_r_in")
        at_in, at_lo_in = [sem(f"p5_at_in{b}") for b in range(2)], sem("p5_at_lo_in")
        xT_in, xT_lo_in, x_in = [sem(f"p5_xT_in{b}") for b in range(2)], sem("p5_xT_lo_in"), [sem(f"p5_x_in{b}") for b in range(2)]
        agg_mm, mix_mm = sem("p5_agg_mm"), sem("p5_mix_mm")
        agg_added, mix_added, x1_stored = sem("p5_agg_added"), sem("p5_mix_added"), [sem(f"p5_x1_stored{b}") for b in range(2)]
        step, var_ready, std_ready, xn_ready, xn_stored = sem("p5_step"), sem("p5_var"), sem("p5_std"), sem("p5_xn"), sem("p5_xn_stored")
        nT_mm, nT_hi_done, nT_lo_done, nT_stored = sem("p5_nT_mm"), sem("p5_nT_hi_done"), sem("p5_nT_lo_done"), sem("p5_nT_stored")
        r_hi_done, r_lo_done, log_mm, log_done = sem("p5_r_hi_done"), sem("p5_r_lo_done"), sem("p5_log_mm"), sem("p5_log_done")
        low_taken = sem("p5_low_taken")
        block = ctx.block()
        x_dram = io["x"].rearrange("(t p) d -> t p d", p=T)

        @block.sync
        def _(sp):
            def load_hi(t, b):
                load_tile(sp, at_hi[:, b, :].bitcast(F32), scr["AT_hi"], t, at_in[b])
                load_tile(sp, xT_hi[:, b, :].bitcast(F32), scr["xT_hi"], t, xT_in[b])

            def load_x(t, b):
                load_tile(sp, x1[:, b, :], x_dram, t, x_in[b])

            load_hi(0, 0)
            load_tile(sp, at_lo[:, :].bitcast(F32), scr["AT_lo"], 0, at_lo_in)
            load_tile(sp, xT_lo[:, :].bitcast(F32), scr["xT_lo"], 0, xT_lo_in)
            for h in range(2):
                at = slice(h * HALF, (h + 1) * HALF)
                for t_, name in ((m_hi, "M_hi"), (m_lo, "M_lo")):
                    sp.dma_start(t_[:, :, at].bitcast(F32), scr[name][:, :, at].rearrange("c p n -> p c n")).then_inc(m_in[h], 16)
            load_x(0, 0)
            load_hi(1, 1)
            load_x(1, 1)

            def rest(t, b, more):
                sp.wait_ge(agg_mm, 2 * t + 2)
                if more >= 1:
                    load_tile(sp, at_lo[:, :].bitcast(F32), scr["AT_lo"], t + 1, at_lo_in)
                sp.wait_ge(mix_mm, 2 * t + 2)
                if more >= 1:
                    load_tile(sp, xT_lo[:, :].bitcast(F32), scr["xT_lo"], t + 1, xT_lo_in)
                if more >= 2:
                    load_hi(t + 2, b)
                sp.wait_ge(mix_added, 2 * t + 2)
                load_store = scr["x1"][bass.ds(t, 1), :, :].rearrange("o p d -> (o p) d")
                sp.dma_start(load_store, x1[:, b, :]).then_inc(x1_stored[b], 16)
                sp.wait_ge(xn_ready, t + 1)
                sp.dma_start(scr["xn2"][bass.ds(t * T, T), :], xn[:, :]).then_inc(xn_stored, 16)
                if more >= 2:
                    sp.wait_ge(x1_stored[b], 8 * (t - b) + 16)
                    load_x(t + 2, b)
                sp.wait_ge(nT_lo_done, 2 * t + 2)
                for name, t_ in (("nT_hi", nT_hi), ("nT_lo", nT_lo)):
                    sp.dma_start(scr[name][bass.ds(t, 1), :, :].rearrange("o p d -> (o p) d"), t_[:, :].bitcast(F32)).then_inc(nT_stored, 16)

            with sp.Fori(0, NT // 2 - 1) as i:
                for b in range(2):
                    rest(2 * i + b, b, 2)
            for b in range(2):
                rest(NT - 2 + b, b, 1 - b)
            for b in range(2):
                sp.wait_ge(x1_stored[b], 8 * NT)
            sp.wait_ge(xn_stored, 16 * NT)
            sp.wait_ge(nT_stored, 32 * NT)

        @block.gpsimd
        def _(pool):
            pool.dma_start(r_raw[:, :, :], io["router"].rearrange("(c p) e -> p c e", p=P)).then_inc(r_in, 16)

        @block.scalar
        def _(act):
            carrier = Carrier(nc, scr, act, "scalar")
            split(nc, act, None, r_raw[:, :, :], r_hi, None, r_in, 16, r_hi_done, None, 0)

            def tile(t, first=False):
                hold(carrier, var_ready, t + 1)
                nc.scalar.activation(small[:, 1:2], small[:, 0:1], ACT.Sqrt).then_inc(std_ready, 1)
                if not first:
                    act.wait_ge(nT_stored, 32 * t)
                    act.wait_ge(log_mm, t)
                for h in range(2):
                    act.wait_ge(nT_mm, 2 * t + h + 1)
                    nc.scalar.copy(nT_hi[:, h * 4 * T:(h + 1) * 4 * T], pT[h][:, :]).then_inc(nT_hi_done, 1)

            tile(0, True)
            with act.Fori(1, NT) as t:
                tile(t)

        @block.vector
        def _(dve):
            carrier = Carrier(nc, scr, dve, "vector")
            split(nc, None, dve, r_raw[:, :, :], r_hi, r_lo, None, 0, r_hi_done, r_lo_done, 0)

            def tile(t, b, first):
                dve.wait_ge(x_in[b], 8 * (t - b) + 16)
                for h in range(2):
                    at = slice(h * HALF, (h + 1) * HALF)
                    dve.wait_ge(agg_mm, 2 * t + h + 1)
                    nc.vector.scalar_tensor_tensor(x1[:, b, at], pagg[h][:, :], dinv[:, bass.ds(t, 1)], x1[:, b, at], ALU.mult, ALU.add).then_inc(agg_added, 1)
                for h in range(2):
                    at = slice(h * HALF, (h + 1) * HALF)
                    dve.wait_ge(agg_added, 2 * t + h + 1)
                    dve.wait_ge(mix_mm, 2 * t + h + 1)
                    nc.vector.tensor_tensor(x1[:, b, at], x1[:, b, at], pmix[h][:, :], ALU.add).then_inc(mix_added, 1)
                dve.wait_ge(mix_added, 2 * t + 2)
                if not first:
                    dve.wait_ge(xn_stored, 16 * t)
                    dve.wait_ge(nT_mm, 2 * t)
                layernorm(nc, carrier, x1[:, b, :], xn[:, :], stats, mv, small, step, 7 * t, var_ready, std_ready, xn_ready, t)
                for h in range(2):
                    dve.wait_ge(nT_hi_done, 2 * t + h + 1)
                    at = slice(h * 4 * T, (h + 1) * 4 * T)
                    nc.vector.tensor_tensor(nT_lo[:, at], pT[h][:, :], nT_hi[:, at].bitcast(F32), ALU.subtract).then_inc(nT_lo_done, 1)
                dve.wait_ge(log_mm, t + 1)
                nc.vector.tensor_copy(log_low[:, :], plog[:, 1, :]).then_inc(low_taken, 1)
                dve.wait_ge(low_taken, t + 1)
                nc.vector.tensor_tensor(logits[:, bass.ds(t, 1), :].rearrange("p o e -> p (o e)"), plog[:, 0, :], log_low[:, :], ALU.add).then_inc(log_done, 1)

            for b in range(2):
                tile(b, b, b == 0)
            with dve.Fori(1, NT // 2) as i:
                for b in range(2):
                    tile(2 * i + b, b, False)

        @block.tensor
        def _(pe):
            def aggregate(t, b, h):
                if h == 0:
                    pe.wait_ge(at_in[b], 8 * (t - b) + 16)
                    pe.wait_ge(at_lo_in, 16 * t + 16)
                col = slice(h * HALF, (h + 1) * HALF)
                if not (isinstance(t, int) and t == 0):
                    pe.wait_ge(agg_added, 2 * t - 1 + h)
                for j in range(NT):
                    at = slice(j * T, (j + 1) * T)
                    m = mm3(pe, pagg[h][:, :], at_hi[:, b, at], at_lo[:, at], hs_hi[:, j, col], hs_lo[:, j, col], j == 0, j == NT - 1)
                m.then_inc(agg_mm, 1)

            def mix(t, b, first=False):
                pe.wait_ge(xT_in[b], 8 * (t - b) + 16)
                pe.wait_ge(xT_lo_in, 16 * t + 16)
                for h in range(2):
                    col = slice(h * HALF, (h + 1) * HALF)
                    if first:
                        pe.wait_ge(m_in[h], 32)
                    else:
                        pe.wait_ge(mix_added, 2 * t - 1 + h)
                    for c in range(C):
                        at = slice(c * T, (c + 1) * T)
                        m = mm3(pe, pmix[h][:, :], xT_hi[:, b, at], xT_lo[:, at], m_hi[:, c, col], m_lo[:, c, col], c == 0, c == C - 1)
                    m.then_inc(mix_mm, 1)

            def turn(t, first=False):
                pe.wait_ge(xn_ready, t + 1)
                if not first:
                    pe.wait_ge(nT_lo_done, 2 * t)
                for c in range(C):
                    m = pe.transpose(pT[c // 4][:, (c % 4) * T:(c % 4 + 1) * T], xn[:, c * P:(c + 1) * P], scr["ident"][0:T, 0:T])
                    if c % 4 == 3:
                        m.then_inc(nT_mm, 1)

            def route(t, first=False):
                if not first:
                    pe.wait_ge(log_done, t)
                pe.wait_ge(nT_lo_done, 2 * t + 2)
                for c in range(C):
                    at = slice(c * T, (c + 1) * T)
                    both = r_parts[:, c, :, :].rearrange("p k e -> p (k e)")
                    pe.matmul(plog[:, :, :].rearrange("p k e -> p (k e)"), nT_lo[:, at], both, start=c == 0, stop=False)
                    m = pe.matmul(plog[:, :, :].rearrange("p k e -> p (k e)"), nT_hi[:, at], both, start=False, stop=c == C - 1)
                m.then_inc(log_mm, 1)

            pe.wait_ge(r_lo_done, 1)
            for h in range(2):
                aggregate(0, 0, h)
            mix(0, 0, first=True)
            aggregate(1, 1, 0)
            turn(0, first=True)
            aggregate(1, 1, 1)
            route(0, first=True)
            mix(1, 1)
            with pe.Fori(1, NT // 2) as i:
                for b in range(2):
                    t = 2 * i + b
                    aggregate(t, b, 0)
                    turn(t - 1)
                    aggregate(t, b, 1)
                    route(t - 1)
                    mix(t, b)
            turn(NT - 1)
            route(NT - 1)


TOP = 4
MOE = 512
SHARED = 256
SLOTS = 64
FAR = 1 << 20


def shared_and_routing(nc, io, scr, out):
    with Phase(nc) as ctx:
        sb = lambda n, s, d=F32: ctx.enter_context(nc.sbuf_tensor(n, s, d))
        ps = lambda n, s: ctx.enter_context(nc.psum_tensor(n, s, F32))
        sem = ctx.sem
        G = 2 * SHARED
        gu_raw, gu_hi, gu_lo = sb("p6_gu_raw", [P, C, G]), sb("p6_gu_hi", [P, C, G], F32R), sb("p6_gu_lo", [P, C, G], F32R)
        d_raw, d_hi, d_lo = sb("p6_d_raw", [P, 2, D]), sb("p6_d_hi", [P, 2, D], F32R), sb("p6_d_lo", [P, 2, D], F32R)
        nT_hi, nT_lo = sb("p6_nT_hi", [P, 2, C * T], F32R), sb("p6_nT_lo", [P, 2, C * T], F32R)
        y = sb("p6_y", [T, 2, D])
        sg, a = sb("p6_sg", [T, SHARED]), sb("p6_a", [T, SHARED])
        aT_hi, aT_lo = sb("p6_aT_hi", [P, 2 * T], F32R), sb("p6_aT_lo", [P, 2 * T], F32R)
        pgu, py = ps("p6_gu", [T, G]), [ps(f"p6_y{h}", [T, HALF]) for h in range(2)]
        paT = ps("p6_aT", [P, 2 * T])
        pcount = ps("p6_count", [T, 2, NT * EXPERTS])
        plist = ps("p6_list", [P, 2, SLOTS])
        gu_in, d_in = [sem(f"p6_gu_in{k}") for k in range(2)], sem("p6_d_in")
        nT_in, x1_in, stored = [sem(f"p6_nT_in{b}") for b in range(2)], [sem(f"p6_x1_in{b}") for b in range(2)], [sem(f"p6_stored{b}") for b in range(2)]
        gu_hi_done, gu_lo_done, d_hi_done, d_lo_done = sem("p6_gu_hi_done"), sem("p6_gu_lo_done"), sem("p6_d_hi_done"), sem("p6_d_lo_done")
        gu_mm, sg_done, a_done, aT_mm, aT_hi_done, aT_lo_done = sem("p6_gu_mm"), sem("p6_sg"), sem("p6_a"), sem("p6_aT_mm"), sem("p6_aT_hi_done"), sem("p6_aT_lo_done")
        y_mm, y_done = sem("p6_y_mm"), sem("p6_y_done")
        W = NT * EXPERTS
        sc, ez = sb("r_scores", [T, NT, EXPERTS]), sb("r_exp", [T, NT, EXPERTS])
        row_max, row_sum = sb("r_max", [T, NT]), sb("r_sum", [T, NT])
        bias = sb("r_bias", [T, 1])
        tri_i, tri = sb("r_tri_i", [T, EXPERTS, EXPERTS], I32), sb("r_tri", [T, EXPERTS, EXPERTS])
        full_i, full = sb("r_full_i", [T, EXPERTS, NT], I32), sb("r_full", [T, EXPERTS, NT])
        kth_i, kth = sb("r_kth_i", [T, TOP, EXPERTS], I32), sb("r_kth", [T, TOP, EXPERTS])
        below_i, below = sb("r_below_i", [T, T], I32), sb("r_below", [T, T], BF16)
        all_ones = sb("r_ones", [T, T], BF16)
        gt, eq = sb("r_gt", [T, NT, EXPERTS * EXPERTS]), sb("r_eq", [T, NT, EXPERTS * EXPERTS])
        rank, sel, sel_b = sb("r_rank", [T, NT, EXPERTS]), sb("r_sel", [T, NT, EXPERTS]), sb("r_sel_b", [T, NT, EXPERTS], BF16)
        wts, pos = sb("r_wts", [T, NT, EXPERTS]), sb("r_pos", [T, NT, EXPERTS])
        before, within = sb("r_before", [T, NT + 1, EXPERTS]), sb("r_within", [T, 2, W])
        over, tiles, base = sb("r_over", [T, EXPERTS, NT]), sb("r_tiles", [T, EXPERTS + 1]), sb("r_base", [T, EXPERTS])
        span = sb("r_span", [T, EXPERTS, EXPERTS])
        is_kth, picked = sb("r_is_kth", [T, NT, TOP * EXPERTS]), sb("r_picked", [T, NT, TOP * EXPERTS])
        row_of, row_i = sb("r_row", [T, NT, TOP]), sb("r_row_i", [T, NT * TOP], I32)
        token_i, entry = sb("r_token_i", [T, NT, TOP], I32), sb("r_entry", [T, NT, TOP, 2])
        blank = sb("r_blank", [P, SLOTS, 2])
        lists = sb("r_lists", [SLOTS, P, 2])
        consts, step, prob_in, exp_in, exp_done = sem("r_consts"), sem("r_step"), sem("r_bias_in"), sem("r_exp_in"), sem("r_exp_done")
        blank_set, blank_out, rows_ready, scattered = sem("r_blank_set"), sem("r_blank_out"), sem("r_rows_ready"), sem("r_scattered")
        sel_ready, counted, lists_in, lists_T, lists_done = sem("r_sel_ready"), sem("r_counted"), sem("r_lists_in"), sem("r_lists_T"), sem("r_lists_done")
        block = ctx.block()
        y_dram = out.rearrange("(t p) d -> t p d", p=T)

        @block.sync
        def _(sp):
            for k, name in enumerate(("s_gate", "s_up")):
                sp.dma_start(gu_raw[:, :, k * SHARED:(k + 1) * SHARED], io[name].rearrange("(c p) n -> p c n", p=P)).then_inc(gu_in[k], 16)

            def load_nT(t, b):
                load_tile(sp, nT_hi[:, b, :].bitcast(F32), scr["nT_hi"], t, nT_in[b])
                load_tile(sp, nT_lo[:, b, :].bitcast(F32), scr["nT_lo"], t, nT_in[b])

            def load_x1(t, b):
                load_tile(sp, y[:, b, :], scr["x1"], t, x1_in[b])

            load_nT(0, 0)
            sp.dma_start(d_raw[:, :, :], io["s_down"].rearrange("(c p) n -> p c n", p=P)).then_inc(d_in, 16)
            load_nT(1, 1)
            for b in range(2):
                load_x1(b, b)
            for k, (raw, src) in enumerate(scr["expert_pieces"](0)):
                sp.dma_start(raw, src).then_inc(scr["raw_in"][k], 16)

            def next_nT(t, b):
                sp.wait_ge(gu_mm, t + 1)
                load_nT(t + 2, b)

            def store_y(t, b, more):
                sp.wait_ge(y_done, 2 * t + 2)
                sp.dma_start(y_dram[bass.ds(t, 1), :, :].rearrange("o p d -> (o p) d"), y[:, b, :]).then_inc(stored[b], 16)
                if more:
                    sp.wait_ge(stored[b], 8 * (t - b) + 16)
                    load_x1(t + 2, b)

            next_nT(0, 0)
            next_nT(1, 1)
            store_y(0, 0, True)
            with sp.Fori(1, NT // 2 - 1) as i:
                for b in range(2):
                    next_nT(2 * i + b, b)
                    store_y(2 * i + b - 1, 1 - b, True)
            store_y(NT - 3, 1, True)
            for b in range(2):
                store_y(NT - 2 + b, b, False)
            for b in range(2):
                sp.wait_ge(stored[b], 8 * NT)

        @block.gpsimd
        def _(pool):
            pool.dma_start(bias[:, :], io["router_b"].to_broadcast([T, 1])).then_inc(prob_in, 16)
            nc.gpsimd.memset(blank[:, :, 0:1], float(FAR)).then_inc(blank_set, 1)
            nc.gpsimd.memset(blank[:, :, 1:2], 0.0).then_inc(blank_set, 1)
            pool.wait_ge(blank_set, 2)
            pool.dma_start(scr["lists"].rearrange("(p s) w -> p s w", p=P), blank[:, :, :]).then_inc(blank_out, 16)
            nc.gpsimd.iota(tri_i[:, :, :], pattern=[[1, EXPERTS], [-1, EXPERTS]], base=0, channel_multiplier=0).then_inc(consts, 1)
            nc.gpsimd.iota(full_i[:, :, :], pattern=[[0, EXPERTS], [P, NT]], base=0, channel_multiplier=0).then_inc(consts, 1)
            nc.gpsimd.iota(kth_i[:, :, :], pattern=[[1, TOP], [0, EXPERTS]], base=0, channel_multiplier=0).then_inc(consts, 1)
            nc.gpsimd.iota(below_i[:, :], pattern=[[1, T]], base=0, channel_multiplier=-1).then_inc(consts, 1)
            nc.gpsimd.iota(token_i[:, :, :], pattern=[[T, NT], [0, TOP]], base=0, channel_multiplier=1).then_inc(consts, 1)
            pool.wait_ge(rows_ready, 1)
            pool.wait_ge(blank_out, 16)
            for t in range(NT):
                for k in range(TOP):
                    n = t * TOP + k
                    pool.indirect_dma_start(out=scr["lists"], out_offset=bass.IndirectOffsetOnAxis(ap=row_i[:, n:n + 1].bitcast(U32), axis=0),
                                            in_=entry[:, t, k, :], in_offset=None).then_inc(scattered, 16)
            pool.wait_ge(scattered, 16 * NT * TOP)
            pool.dma_start(lists[:, :, :], scr["lists"].rearrange("(s r) w -> s r w", r=P)).then_inc(lists_in, 16)

        @block.scalar
        def _(act):
            carrier = Carrier(nc, scr, act, "scalar")
            act.wait_ge(exp_in, 1)
            nc.scalar.activation(ez[:, :, :], sc[:, :, :], ACT.Exp).then_inc(exp_done, 1)
            act.wait_ge(gu_in[0], 16)
            for c in range(C):
                split(nc, act, None, gu_raw[:, c, :], gu_hi[:, c, :], None, gu_in[1], 16, gu_hi_done, None, c)
            for c in range(2):
                split(nc, act, None, d_raw[:, c, :], d_hi[:, c, :], None, d_in, 16, d_hi_done, None, c)

            with act.Fori(0, NT) as t:
                hold(carrier, gu_mm, t + 1)
                nc.scalar.activation(sg[:, :], pgu[:, 0:SHARED], ACT.Silu).then_inc(sg_done, 1)
                act.wait_ge(aT_mm, t + 1)
                nc.scalar.copy(aT_hi[:, :], paT[:, :]).then_inc(aT_hi_done, 1)

        @block.vector
        def _(dve):
            n = [0]

            def link(ins):
                n[0] += 1
                ins.then_inc(step, 1)
                dve.wait_ge(step, n[0])

            inner = lambda t, shape: t.unsqueeze(len(t.shape)).to_broadcast(shape)
            every = lambda t, shape: t.unsqueeze(1).to_broadcast(shape)
            by_e = [T, NT, EXPERTS]
            logits = scr["logits"]
            link(nc.vector.tensor_reduce(row_max[:, :], logits[:, :, :], AX, ALU.max))
            nc.vector.tensor_tensor(sc[:, :, :], logits[:, :, :], inner(row_max[:, :], by_e), ALU.subtract).then_inc(exp_in, 1)
            dve.wait_ge(consts, 5)
            nc.vector.tensor_scalar(tri[:, :, :], tri_i[:, :, :], 0.0, None, ALU.is_gt)
            nc.vector.tensor_copy(full[:, :, :], full_i[:, :, :])
            nc.vector.tensor_copy(kth[:, :, :], kth_i[:, :, :])
            nc.vector.tensor_scalar(below[:, :], below_i[:, :], 0.0, None, ALU.is_gt)
            nc.vector.memset(all_ones[:, :], 1.0)
            nc.vector.tensor_copy(entry[:, :, :, 0], token_i[:, :, :])
            nc.vector.memset(before[:, 0, :], 0.0)
            dve.wait_ge(exp_done, 1)
            link(nc.vector.tensor_reduce(row_sum[:, :], ez[:, :, :], AX, ALU.add))
            link(nc.vector.reciprocal(row_max[:, :], row_sum[:, :]))
            link(nc.vector.tensor_tensor(ez[:, :, :], ez[:, :, :], inner(row_max[:, :], by_e), ALU.mult))
            dve.wait_ge(prob_in, 16)
            link(nc.vector.tensor_scalar(sc[:, :, :], ez[:, :, :], bias[:, 0:1], None, ALU.add))
            pair = [T, NT, EXPERTS, EXPERTS]
            view = lambda t: t[:, :, :].rearrange("p t (e f) -> p t e f", f=EXPERTS)
            own, other = sc[:, :, :].unsqueeze(3).to_broadcast(pair), sc[:, :, :].unsqueeze(2).to_broadcast(pair)
            nc.vector.tensor_tensor(view(gt), other, own, ALU.is_gt)
            link(nc.vector.tensor_tensor(view(eq), other, own, ALU.is_equal))
            flat_tri = tri[:, :, :].rearrange("p e f -> p (e f)")
            link(nc.vector.tensor_tensor(eq[:, :, :], eq[:, :, :], every(flat_tri, [T, NT, EXPERTS * EXPERTS]), ALU.mult))
            link(nc.vector.tensor_tensor(gt[:, :, :], gt[:, :, :], eq[:, :, :], ALU.add))
            link(nc.vector.tensor_reduce(rank[:, :, :], view(gt), AX, ALU.add))
            nc.vector.tensor_scalar(sel_b[:, :, :], rank[:, :, :], float(TOP), None, ALU.is_lt).then_inc(sel_ready, 1)
            link(nc.vector.tensor_scalar(sel[:, :, :], rank[:, :, :], float(TOP), None, ALU.is_lt))
            link(nc.vector.tensor_tensor(wts[:, :, :], ez[:, :, :], sel[:, :, :], ALU.mult))
            link(nc.vector.tensor_reduce(row_sum[:, :], wts[:, :, :], AX, ALU.add))
            link(nc.vector.tensor_scalar(row_sum[:, :], row_sum[:, :], 1e-20, None, ALU.add))
            link(nc.vector.reciprocal(row_max[:, :], row_sum[:, :]))
            link(nc.vector.tensor_tensor(wts[:, :, :], wts[:, :, :], inner(row_max[:, :], by_e), ALU.mult))
            dve.wait_ge(counted, 1)
            link(nc.vector.tensor_copy(within[:, :, :], pcount[:, :, :]))
            for t in range(NT):
                link(nc.vector.tensor_tensor(before[:, t + 1, :], before[:, t, :], within[:, 1, t * EXPERTS:(t + 1) * EXPERTS], ALU.add))
            link(nc.vector.tensor_tensor(over[:, :, :], inner(before[:, NT, :], [T, EXPERTS, NT]), full[:, :, :], ALU.is_gt))
            link(nc.vector.tensor_reduce(tiles[:, 0:EXPERTS], over[:, :, :], AX, ALU.add))
            link(nc.vector.tensor_scalar(tiles[:, 0:EXPERTS], tiles[:, 0:EXPERTS], 2.0, None, ALU.max))
            link(nc.vector.tensor_tensor(span[:, :, :], every(tiles[:, 0:EXPERTS], [T, EXPERTS, EXPERTS]), tri[:, :, :], ALU.mult))
            link(nc.vector.tensor_reduce(base[:, :], span[:, :, :], AX, ALU.add))
            link(nc.vector.tensor_tensor(tiles[:, EXPERTS:EXPERTS + 1], base[:, EXPERTS - 1:EXPERTS], tiles[:, EXPERTS - 1:EXPERTS], ALU.add))
            nc.vector.tensor_scalar(scr["tiles"][:, :], tiles[0:1, :], -1.0, None, ALU.add)
            link(nc.vector.tensor_scalar(base[:, :], base[:, :], float(P), None, ALU.mult))
            link(nc.vector.tensor_tensor(pos[:, :, :], before[:, 0:NT, :], within[:, 0, :].rearrange("p (t e) -> p t e", e=EXPERTS), ALU.add))
            link(nc.vector.tensor_tensor(pos[:, :, :], pos[:, :, :], every(base[:, :], by_e), ALU.add))
            four = [T, NT, TOP, EXPERTS]
            kview = lambda t: t[:, :, :].rearrange("p t (k e) -> p t k e", e=EXPERTS)
            over_k = lambda t: t[:, :, :].unsqueeze(2).to_broadcast(four)
            link(nc.vector.tensor_tensor(kview(is_kth), over_k(rank), kth[:, :, :].unsqueeze(1).to_broadcast(four), ALU.is_equal))
            link(nc.vector.tensor_tensor(kview(picked), kview(is_kth), over_k(pos), ALU.mult))
            link(nc.vector.tensor_reduce(row_of[:, :, :], kview(picked), AX, ALU.add))
            nc.vector.tensor_copy(row_i[:, :], row_of[:, :, :].rearrange("p t k -> p (t k)"))
            link(nc.vector.tensor_tensor(kview(picked), kview(is_kth), over_k(wts), ALU.mult))
            nc.vector.tensor_reduce(entry[:, :, :, 1], kview(picked), AX, ALU.add).then_inc(rows_ready, 1)

            for c in range(C):
                split(nc, None, dve, gu_raw[:, c, :], gu_hi[:, c, :], gu_lo[:, c, :], None, 0, gu_hi_done, gu_lo_done, c)
            for c in range(2):
                split(nc, None, dve, d_raw[:, c, :], d_hi[:, c, :], d_lo[:, c, :], None, 0, d_hi_done, d_lo_done, c)

            def activate(t):
                dve.wait_ge(sg_done, t + 1)
                nc.vector.tensor_tensor(a[:, :], sg[:, :], pgu[:, SHARED:G], ALU.mult).then_inc(a_done, 1)

            def add_down(t, b):
                dve.wait_ge(x1_in[b], 8 * (t - b) + 16)
                for h in range(2):
                    at = slice(h * HALF, (h + 1) * HALF)
                    dve.wait_ge(y_mm, 2 * t + h + 1)
                    nc.vector.tensor_tensor(y[:, b, at], y[:, b, at], py[h][:, :], ALU.add).then_inc(y_done, 1)

            def low(t):
                dve.wait_ge(aT_hi_done, t + 1)
                nc.vector.tensor_tensor(aT_lo[:, :], paT[:, :], aT_hi[:, :].bitcast(F32), ALU.subtract).then_inc(aT_lo_done, 1)

            activate(0)
            low(0)
            activate(1)
            add_down(0, 0)
            low(1)
            with dve.Fori(1, NT // 2) as i:
                for b in range(2):
                    activate(2 * i + b)
                    add_down(2 * i + b - 1, 1 - b)
                    low(2 * i + b)
            add_down(NT - 1, 1)
            dve.wait_ge(lists_T, 2)
            nc.vector.tensor_copy(scr["to_rows"][:, :], plist[:, 0, :])
            nc.vector.tensor_scalar(scr["from_rows"][:, :], plist[:, 0, :], float(N - 1), None, ALU.min)
            nc.vector.tensor_copy(scr["row_weights"][:, :], plist[:, 1, :]).then_inc(lists_done, 1)
            dve.wait_ge(lists_done, 1)

        @block.tensor
        def _(pe):
            pe.wait_ge(sel_ready, 1)
            flat = sel_b[:, :, :].rearrange("p t e -> p (t e)")
            pe.matmul(pcount[:, 0, :], below[:, :], flat, start=True, stop=True)
            pe.matmul(pcount[:, 1, :], all_ones[:, :], flat, start=True, stop=True).then_inc(counted, 1)

            def gate_up(t, b, first=False):
                pe.wait_ge(nT_in[b], 16 * (t - b) + 32)
                for c in range(C):
                    if first:
                        pe.wait_ge(gu_lo_done, c + 1)
                    at = slice(c * T, (c + 1) * T)
                    m = mm3(pe, pgu[:, :], nT_hi[:, b, at], nT_lo[:, b, at], gu_hi[:, c, :], gu_lo[:, c, :], c == 0, c == C - 1)
                m.then_inc(gu_mm, 1)

            def down(t, first=False):
                if first:
                    pe.wait_ge(d_lo_done, 2)
                pe.wait_ge(aT_lo_done, t + 1)
                for h in range(2):
                    col = slice(h * HALF, (h + 1) * HALF)
                    if not first:
                        pe.wait_ge(y_done, 2 * t - 1 + h)
                    for c in range(2):
                        at = slice(c * T, (c + 1) * T)
                        m = mm3(pe, py[h][:, :], aT_hi[:, at], aT_lo[:, at], d_hi[:, c, col], d_lo[:, c, col], c == 0, c == 1)
                    m.then_inc(y_mm, 1)

            def turn(t):
                pe.wait_ge(a_done, t + 1)
                for c in range(2):
                    m = pe.transpose(paT[:, c * T:(c + 1) * T], a[:, c * P:(c + 1) * P], scr["ident"][0:T, 0:T])
                m.then_inc(aT_mm, 1)

            gate_up(0, 0, first=True)
            turn(0)
            gate_up(1, 1)
            down(0, first=True)
            turn(1)
            with pe.Fori(1, NT // 2) as i:
                for b in range(2):
                    gate_up(2 * i + b, b)
                    down(2 * i + b - 1)
                    turn(2 * i + b)
            down(NT - 1)
            pe.wait_ge(lists_in, 16)
            for w in range(2):
                pe.transpose(plist[:, w, :], lists[:, :, w], scr["ident"][0:SLOTS, 0:SLOTS]).then_inc(lists_T, 1)


def experts(nc, io, scr, out):
    with Phase(nc) as ctx:
        sb = lambda n, s, d=F32: ctx.enter_context(nc.sbuf_tensor(n, s, d))
        ps = lambda n, s: ctx.enter_context(nc.psum_tensor(n, s, F32))
        sem = ctx.sem
        I4 = MOE // P
        gu_raw, d_raw, raw_in = scr["gu_raw"], scr["d_raw"], scr["raw_in"]
        gu_hi, gu_lo = sb("p7_gu_hi", [P, C, 2 * MOE], F32R), sb("p7_gu_lo", [P, C, 2 * MOE], F32R)
        d_hi, d_lo = sb("p7_d_hi", [P, I4, D], F32R), sb("p7_d_lo", [P, I4, D], F32R)
        x, y = sb("p7_x", [P, D]), sb("p7_y", [P, D])
        xT_hi, xT_lo = sb("p7_xT_hi", [P, D], F32R), sb("p7_xT_lo", [P, D], F32R)
        sg, a = sb("p7_sg", [P, MOE]), sb("p7_a", [P, MOE])
        aT_hi, aT_lo = sb("p7_aT_hi", [P, MOE], F32R), sb("p7_aT_lo", [P, MOE], F32R)
        from_cell, to_cell = sb("p7_from", [P, 1], I32), sb("p7_to", [P, 1], I32)
        pg, pu, paT = ps("p7_g", [P, MOE]), ps("p7_u", [P, MOE]), ps("p7_aT", [P, MOE])
        pxT, py = [ps(f"p7_xT{h}", [P, HALF]) for h in range(2)], [ps(f"p7_y{h}", [P, HALF]) for h in range(2)]
        gu_hi_done, gu_lo_done, d_hi_done, d_lo_done = sem("p7_gu_hi_done"), sem("p7_gu_lo_done"), sem("p7_d_hi_done"), sem("p7_d_lo_done")
        x_in, xT_mm, xT_hi_done, xT_lo_done = sem("p7_x_in"), sem("p7_xT_mm"), sem("p7_xT_hi_done"), sem("p7_xT_lo_done")
        gu_mm, sg_done, a_done = sem("p7_gu_mm"), sem("p7_sg_done"), sem("p7_a_done")
        aT_mm, aT_hi_done, aT_lo_done = sem("p7_aT_mm"), sem("p7_aT_hi_done"), sem("p7_aT_lo_done")
        y_mm, y_act, y_dve, y_out, y_free = sem("p7_y_mm"), sem("p7_y_act"), sem("p7_y_dve"), sem("p7_y_out"), sem("p7_y_free")
        from_set, to_set = sem("p7_from_set"), sem("p7_to_set")
        block = ctx.block()

        def by_expert(eng, first_tile, tile, last):
            with eng.register("p7_done") as done:
                eng.reg_mov(done, 0)

                def one(e, more):
                    others = eng.value_load(scr["tiles"][0:1, bass.ds(e, 1)], min_val=1, max_val=NT - 1)
                    start = eng.snap(done)
                    first_tile(e, start)
                    with eng.Fori(0, others) as t:
                        tile(e, eng.snap(start + t), eng.snap(start + t + 1))
                    last(e, eng.snap(start + others), more)
                    eng.reg_add(done, done, others)
                    eng.reg_add(done, done, 1)
                with eng.Fori(0, EXPERTS - 1) as e:
                    one(e, True)
                one(EXPERTS - 1, False)

        @block.sync
        def _(sp):
            with sp.Fori(0, EXPERTS - 1) as e:
                for k, (raw, src) in enumerate(scr["expert_pieces"](e + 1)):
                    if k < C:
                        sp.wait_ge(gu_lo_done, C * e + k + 1)
                    else:
                        sp.wait_ge(d_lo_done, I4 * e + k - C + 1)
                    sp.dma_start(raw, src).then_inc(raw_in[k], 16)

        @block.gpsimd
        def _(pool):
            others = pool.value_load(scr["tiles"][0:1, EXPERTS:EXPERTS + 1], min_val=2 * EXPERTS - 1, max_val=SLOTS - 4)
            for s in (y_act, y_dve, y_free):
                pool.sem_inc(s, 1)

            carrier = Carrier(nc, scr, pool, "gpsimd")

            def gather(g, first=False):
                if not first:
                    pool.wait_ge(x_in, 16 * g)
                    hold(carrier, xT_mm, 2 * g)
                nc.gpsimd.tensor_copy(from_cell[:, :], scr["from_rows"][:, bass.ds(g, 1)]).then_inc(from_set, 1)
                hold(carrier, from_set, g + 1)
                pool.indirect_dma_start(out=x[:, :], out_offset=None, in_=scr["xn2"],
                                        in_offset=bass.IndirectOffsetOnAxis(ap=from_cell[:, 0:1].bitcast(U32), axis=0)).then_inc(x_in, 16)

            def scatter(g):
                pool.wait_ge(y_act, g + 2)
                hold(carrier, y_dve, g + 2)
                nc.gpsimd.tensor_copy(to_cell[:, :], scr["to_rows"][:, bass.ds(g, 1)]).then_inc(to_set, 1)
                hold(carrier, to_set, g + 1)
                pool.indirect_dma_start(out=out, out_offset=bass.IndirectOffsetOnAxis(ap=to_cell[:, 0:1].bitcast(U32), axis=0),
                                        in_=y[:, :], in_offset=None, bounds_check=N - 1, oob_is_err=False, compute_op=ALU.add).then_inc(y_out, 16)
                hold(carrier, y_out, 16 * g + 16).then_inc(y_free, 1)

            gather(0, True)
            gather(1)
            gather(2)
            with pool.Fori(0, others) as g:
                gather(pool.snap(g + 3))
                scatter(g)
            scatter(others)

        @block.scalar
        def _(act):
            carrier = Carrier(nc, scr, act, "scalar")

            def split_gu(e):
                for c in range(C):
                    act.wait_ge(raw_in[c], 16 * e + 16)
                    nc.scalar.copy(gu_hi[:, c, :], gu_raw[:, c, :]).then_inc(gu_hi_done, 1)

            def split_d(e):
                for c in range(I4):
                    act.wait_ge(raw_in[C + c], 16 * e + 16)
                    nc.scalar.copy(d_hi[:, c, :], d_raw[:, c, :]).then_inc(d_hi_done, 1)

            def x_high(g):
                for h in range(2):
                    act.wait_ge(xT_mm, 2 * g + h + 1)
                    nc.scalar.copy(xT_hi[:, h * HALF:(h + 1) * HALF], pxT[h][:, :]).then_inc(xT_hi_done, 1)

            def silu(g):
                hold(carrier, gu_mm, 2 * g + 1)
                nc.scalar.activation(sg[:, :], pg[:, :], ACT.Silu).then_inc(sg_done, 1)

            def weigh(g):
                act.wait_ge(y_free, g + 1)
                hold(carrier, y_mm, 2 * g + 1)
                nc.scalar.activation(y[:, 0:HALF], py[0][:, :], ACT.Copy, scale=scr["row_weights"][:, bass.ds(g, 1)]).then_inc(y_act, 1)

            def a_high(g):
                act.wait_ge(aT_mm, g + 1)
                nc.scalar.copy(aT_hi[:, :], paT[:, :]).then_inc(aT_hi_done, 1)

            def first_tile(e, g):
                silu(g)
                x_high(g + 1)
                a_high(g)

            def tile(e, before, g):
                silu(g)
                x_high(g + 1)
                weigh(before)
                a_high(g)

            def last(e, g, more):
                if more:
                    split_gu(e + 1)
                weigh(g)
                if more:
                    act.wait_ge(y_mm, 2 * g + 2)
                    split_d(e + 1)

            x_high(0)
            split_gu(0)
            split_d(0)
            by_expert(act, first_tile, tile, last)

        @block.vector
        def _(dve):
            def split_gu(e):
                for c in range(C):
                    dve.wait_ge(gu_hi_done, C * e + c + 1)
                    nc.vector.tensor_tensor(gu_lo[:, c, :], gu_raw[:, c, :], gu_hi[:, c, :].bitcast(F32), ALU.subtract).then_inc(gu_lo_done, 1)

            def split_d(e):
                for c in range(I4):
                    dve.wait_ge(d_hi_done, I4 * e + c + 1)
                    nc.vector.tensor_tensor(d_lo[:, c, :], d_raw[:, c, :], d_hi[:, c, :].bitcast(F32), ALU.subtract).then_inc(d_lo_done, 1)

            def x_low(g):
                for h in range(2):
                    dve.wait_ge(xT_hi_done, 2 * g + h + 1)
                    at = slice(h * HALF, (h + 1) * HALF)
                    nc.vector.tensor_tensor(xT_lo[:, at], pxT[h][:, :], xT_hi[:, at].bitcast(F32), ALU.subtract).then_inc(xT_lo_done, 1)

            def multiply(g):
                dve.wait_ge(sg_done, g + 1)
                dve.wait_ge(gu_mm, 2 * g + 2)
                nc.vector.tensor_tensor(a[:, :], sg[:, :], pu[:, :], ALU.mult).then_inc(a_done, 1)

            def weigh(g):
                dve.wait_ge(y_free, g + 1)
                dve.wait_ge(y_mm, 2 * g + 2)
                nc.vector.tensor_scalar(y[:, HALF:D], py[1][:, :], scr["row_weights"][:, bass.ds(g, 1)], None, ALU.mult).then_inc(y_dve, 1)

            def a_low(g):
                dve.wait_ge(aT_hi_done, g + 1)
                nc.vector.tensor_tensor(aT_lo[:, :], paT[:, :], aT_hi[:, :].bitcast(F32), ALU.subtract).then_inc(aT_lo_done, 1)

            def first_tile(e, g):
                multiply(g)
                x_low(g + 1)
                a_low(g)

            def tile(e, before, g):
                multiply(g)
                x_low(g + 1)
                weigh(before)
                a_low(g)

            def last(e, g, more):
                if more:
                    split_gu(e + 1)
                weigh(g)
                if more:
                    split_d(e + 1)

            x_low(0)
            split_gu(0)
            split_d(0)
            by_expert(dve, first_tile, tile, last)

        @block.tensor
        def _(pe):
            def turn_x(g):
                pe.wait_ge(x_in, 16 * g + 16)
                for c in range(C):
                    m = pe.transpose(pxT[c // 4][:, (c % 4) * P:(c % 4 + 1) * P], x[:, c * P:(c + 1) * P], scr["ident"][:, :])
                    if c % 4 == 3:
                        m.then_inc(xT_mm, 1)

            def gate_up(e, g, first):
                pe.wait_ge(xT_lo_done, 2 * g + 2)
                for k, acc in enumerate((pg, pu)):
                    for c in range(C):
                        if first and k == 0:
                            pe.wait_ge(gu_lo_done, C * e + c + 1)
                        at, col = slice(c * P, (c + 1) * P), slice(k * MOE, (k + 1) * MOE)
                        m = mm3(pe, acc[:, :], xT_hi[:, at], xT_lo[:, at], gu_hi[:, c, col], gu_lo[:, c, col], c == 0, c == C - 1)
                    m.then_inc(gu_mm, 1)

            def down(e, g):
                pe.wait_ge(aT_lo_done, g + 1)
                pe.wait_ge(y_act, g + 1)
                pe.wait_ge(y_dve, g + 1)
                pe.wait_ge(d_lo_done, I4 * e + I4)
                for h in range(2):
                    col = slice(h * HALF, (h + 1) * HALF)
                    for c in range(I4):
                        at = slice(c * P, (c + 1) * P)
                        m = mm3(pe, py[h][:, :], aT_hi[:, at], aT_lo[:, at], d_hi[:, c, col], d_lo[:, c, col], c == 0, c == I4 - 1)
                    m.then_inc(y_mm, 1)

            def turn_a(g):
                pe.wait_ge(a_done, g + 1)
                for c in range(I4):
                    m = pe.transpose(paT[:, c * P:(c + 1) * P], a[:, c * P:(c + 1) * P], scr["ident"][:, :])
                m.then_inc(aT_mm, 1)

            def first_tile(e, g):
                gate_up(e, g, True)
                turn_x(g + 1)
                turn_a(g)

            def tile(e, before, g):
                gate_up(e, g, False)
                turn_x(g + 1)
                down(e, before)
                turn_a(g)

            def last(e, g, more):
                down(e, g)

            turn_x(0)
            by_expert(pe, first_tile, tile, last)


def program(nc, io, out):
    with ExitStack() as ctx:
        sem = lambda n: ctx.enter_context(nc.semaphore(n))
        scr = {}
        for name in ("xT_hi", "xT_lo"):
            scr[name] = nc.dram_tensor(name, (NT, P, C * T), F32).ap()
        for name in ("M_hi", "M_lo"):
            scr[name] = nc.dram_tensor(name, (C, P, D), F32).ap()
        for name in ("AT_hi", "AT_lo"):
            scr[name] = nc.dram_tensor(name, (NT, T, NT, T), F32).ap()
        scr["zero"] = ctx.enter_context(nc.sbuf_tensor("zero", [P, P], BF16))
        scr["ident"] = ctx.enter_context(nc.sbuf_tensor("ident", [P, P], F32))
        scr["spare"] = ctx.enter_context(nc.sbuf_tensor("spare", [1, 64], F32))
        scr["spare_used"] = 0
        scr["go"] = sem("go")
        ident_zero = sem("ident_zero")
        with nc.Block() as block:
            @block.gpsimd
            def _(pool):
                nc.gpsimd.memset(scr["spare"][:, :], 0.0)
                nc.gpsimd.memset(scr["zero"][:, :], 0.0)
                nc.gpsimd.memset(scr["ident"][:, :], 0.0).then_inc(ident_zero, 1)
                pool.wait_ge(ident_zero, 1)
                nc.gpsimd.affine_select(out=scr["ident"][:, :], in_=scr["ident"][:, :], compare_op=ALU.not_equal, fill=1.0,
                                        base=0, pattern=[[-1, P]], channel_multiplier=1).then_inc(scr["go"], 1)
        scr["x1"] = nc.dram_tensor("x1", (NT, T, D), F32).ap()
        scr["xn2"] = nc.dram_tensor("xn2", (N, D), F32).ap()
        for name in ("nT_hi", "nT_lo"):
            scr[name] = nc.dram_tensor(name, (NT, P, C * T), F32).ap()
        scr["dinv"] = ctx.enter_context(nc.sbuf_tensor("dinv", [T, NT], F32))
        scr["logits"] = ctx.enter_context(nc.sbuf_tensor("logits", [T, NT, EXPERTS], F32))
        with ExitStack() as kv_scope:
            scr["kvT"] = kv_scope.enter_context(nc.sbuf_tensor("kvT", [P, D], F32))
            project_kv(nc, io, scr)
            mixing_matrix(nc, io, scr)
        adjacency(nc, io, scr)
        with ExitStack() as hs_scope:
            scr["hs_hi"] = hs_scope.enter_context(nc.sbuf_tensor("hs_hi", [T, NT, D], F32R))
            scr["hs_lo"] = hs_scope.enter_context(nc.sbuf_tensor("hs_lo", [T, NT, D], F32R))
            node_features(nc, io, scr)
            aggregate_and_mix(nc, io, scr)
        scr["lists"] = nc.dram_tensor("lists", (SLOTS * P, 2), F32).ap()
        scr["tiles"] = ctx.enter_context(nc.sbuf_tensor("tiles", [1, EXPERTS + 1], I32))
        scr["to_rows"] = ctx.enter_context(nc.sbuf_tensor("to_rows", [P, SLOTS], I32))
        scr["from_rows"] = ctx.enter_context(nc.sbuf_tensor("from_rows", [P, SLOTS], I32))
        scr["row_weights"] = ctx.enter_context(nc.sbuf_tensor("row_weights", [P, SLOTS], F32))
        gu_raw = scr["gu_raw"] = ctx.enter_context(nc.sbuf_tensor("gu_raw", [P, C, 2 * MOE], F32))
        d_raw = scr["d_raw"] = ctx.enter_context(nc.sbuf_tensor("d_raw", [P, MOE // P, D], F32))
        scr["raw_in"] = [sem(f"raw_in{k}") for k in range(C + MOE // P)]
        downs = io["down"].rearrange("e (c p) n -> e c p n", p=P)

        def expert_pieces(e):
            pick = lambda t, c: t[bass.ds(e, 1), c, :, :].rearrange("o p n -> (o p) n")
            out_ = [(gu_raw[:, c, :], pick(io["gate_up"].rearrange("e (c p) n -> e c p n", p=P), c)) for c in range(C)]
            return out_ + [(d_raw[:, c, :], pick(downs, c)) for c in range(MOE // P)]
        scr["expert_pieces"] = expert_pieces
        shared_and_routing(nc, io, scr, out)
        experts(nc, io, scr, out)


def kernel(**a):
    import numpy as np
    import concourse.bacc as bacc
    from concourse.bass_utils import run_bass_kernel_spmd as run

    lay = {k: np.asarray(v) for k, v in a.items()}
    arrays = {
        "x": lay["x"], "src": lay["src"].reshape(160, 125).T, "dst": lay["dst"].reshape(160, 125).T,
        "wgT": lay["L0_gnn_W"].T, "gb": lay["L0_gnn_b"].reshape(1, D),
        "wkT": lay["L0_mix_W_k"].T, "wvT": lay["L0_mix_W_v"].T, "wq": lay["L0_mix_W_q"], "woT": lay["L0_mix_W_o"].T,
        "router": lay["L0_ffn_router_w"], "router_b": lay["L0_ffn_router_bias"].reshape(1, 1),
        "gate_up": np.concatenate([lay["L0_ffn_gate_w"], lay["L0_ffn_up_w"]], axis=2), "down": lay["L0_ffn_down_w"],
        "s_gate": lay["L0_ffn_s_gate_w"], "s_up": lay["L0_ffn_s_up_w"], "s_down": lay["L0_ffn_s_down_w"],
    }
    nc = bacc.Bacc("TRN2", target_bir_lowering=False, num_devices=1)
    arrays = {f"in_{k}": np.ascontiguousarray(v) for k, v in arrays.items()}
    io = {k[3:]: nc.dram_tensor(k, v.shape, mybir.dt.from_np(v.dtype), kind="ExternalInput").ap() for k, v in arrays.items()}
    out = nc.dram_tensor("out_x", (N, D), F32, kind="ExternalOutput").ap()
    program(nc, io, out)
    r = run(nc, [arrays], core_ids=[0])
    return r.results[0]["out_x"]
```

```python
import concourse.bass as bass
from concourse import mybir
from contextlib import ExitStack

F32 = mybir.dt.float32
F32R = mybir.dt.float32r
BF16 = mybir.dt.bfloat16
F16 = mybir.dt.float16
I32 = mybir.dt.int32
U32 = mybir.dt.uint32
ALU = mybir.AluOpType
ACT = mybir.ActivationFunctionType
AX = mybir.AxisListType.X

N = 1250
D = 1024
P = 128
T = 125
NT = N // T
C = D // P
HALF = 512
EPS = 1e-5


class Phase(ExitStack):
    def __init__(self, nc):
        super().__init__()
        self.nc, self.sems = nc, []

    def sem(self, name):
        self.sems.append(self.nc.alloc_semaphore(name))
        return self.sems[-1]

    def block(self):
        self.opened = self.nc.Block()
        return self.opened.__enter__()

    def __exit__(self, *error):
        self.opened.__exit__(*error)
        if error[0] is None:
            self.clear()
        return super().__exit__(*error)

    def clear(self):
        with self.nc.Block() as block:
            @block.gpsimd
            def _(pool):
                for s in self.sems:
                    pool.sem_clear(s)
        for s in self.sems:
            self.nc.release_semaphore(s)


def hold(carrier, sem, value):
    carrier.eng.wait_ge(sem, value)
    if not isinstance(value, int):
        return carrier.issue()


class Carrier:
    def __init__(self, nc, scr, eng, on):
        self.nc, self.scr, self.eng, self.on = nc, scr, eng, on

    def issue(self):
        self.scr["spare_used"] += 1
        at = self.scr["spare"][0:1, self.scr["spare_used"]:self.scr["spare_used"] + 1]
        zero = self.scr["spare"][0:1, 0:1]
        if self.on == "scalar":
            return self.nc.scalar.copy(at, zero)
        if self.on == "gpsimd":
            return self.nc.gpsimd.tensor_tensor(at, zero, zero, ALU.add)
        return self.nc.vector.memset(at, 0.0)


def layernorm(nc, carrier, src, dst, stats, mv, small, step, base, var_ready, std_ready, normed, t):
    dve = carrier.eng
    for h in range(2):
        i = nc.vector.bn_stats(stats[:, h, :], src[:, h * HALF:(h + 1) * HALF])
    i.then_inc(step, 1)
    hold(carrier, step, base + 1)
    nc.vector.bn_aggr(mv[:, :], stats[:, :, :]).then_inc(step, 1)
    dve.wait_ge(step, base + 2)
    nc.vector.tensor_scalar_add(small[:, 0:1], mv[:, 1:2], EPS).then_inc(var_ready, 1)
    dve.wait_ge(std_ready, t + 1)
    inverse_root(nc, dve, small, step, base + 2)
    dve.wait_ge(step, base + 6)
    nc.vector.tensor_scalar(dst, src, mv[:, 0:1], small[:, 6:7], ALU.subtract, ALU.mult).then_inc(normed, 1)
    dve.wait_ge(normed, t + 1)
    nc.vector.memset(small[:, 7:8], 0.0).then_inc(step, 1)


def inverse_root(nc, dve, small, step, base):
    nc.vector.reciprocal(small[:, 2:3], small[:, 1:2]).then_inc(step, 1)
    dve.wait_ge(step, base + 1)
    nc.vector.scalar_tensor_tensor(small[:, 3:4], small[:, 2:3], small[:, 2:3], small[:, 0:1], ALU.mult, ALU.mult).then_inc(step, 1)
    dve.wait_ge(step, base + 2)
    nc.vector.tensor_scalar(small[:, 5:6], small[:, 3:4], -0.5, 1.5, ALU.mult, ALU.add).then_inc(step, 1)
    dve.wait_ge(step, base + 3)
    nc.vector.tensor_tensor(small[:, 6:7], small[:, 5:6], small[:, 2:3], ALU.mult).then_inc(step, 1)


def mm3(pe, out, lhs_hi, lhs_lo, rhs_hi, rhs_lo, start, stop):
    pe.matmul(out, lhs_lo, rhs_hi, start=start, stop=False)
    pe.matmul(out, lhs_hi, rhs_lo, start=False, stop=False)
    return pe.matmul(out, lhs_hi, rhs_hi, start=False, stop=stop)


def before_split(nc, name, lo):
    return nc.alloc_sbuf_tensor_at(name, list(lo.shape), F32, offset=nc.lookup_mloc(lo).addr)


def split(nc, act, dve, raw, hi, lo, raw_in, raw_value, hi_done, lo_done, n):
    if act is not None:
        act.wait_ge(raw_in, raw_value)
        nc.scalar.copy(hi, raw).then_inc(hi_done, 1)
    if dve is not None:
        dve.wait_ge(hi_done, n + 1)
        nc.vector.tensor_tensor(lo, raw, hi.bitcast(F32), ALU.subtract).then_inc(lo_done, 1)


def project_kv(nc, io, scr):
    with Phase(nc) as ctx:
        sb = lambda n, s, d: ctx.enter_context(nc.sbuf_tensor(n, s, d))
        ps = lambda n, s: ctx.enter_context(nc.psum_tensor(n, s, F32))
        sem = ctx.sem
        w_hi = sb("p1_w_hi", [P, 2, C, D], F32R)
        w_lo = sb("p1_w_lo", [P, 2, C, D], F32R)
        w_raw = before_split(nc, "p1_w_raw", w_lo)
        x = sb("p1_x", [T, 2, D], F32)
        xT_hi = sb("p1_xT_hi", [P, 2, C * T], F32R)
        xT_lo = sb("p1_xT_lo", [P, 2, C * T], F32R)
        kv_hi = sb("p1_kv_hi", [T, 4 * HALF], F32R)
        kv_lo = sb("p1_kv_lo", [T, 4 * HALF], F32R)
        stats = sb("p1_stats", [T, 2, 6], F32)
        mv = sb("p1_mv", [T, 2], F32)
        small = sb("p1_small", [T, 8], F32)
        kvT = scr["kvT"]
        ident = scr["ident"]
        xp = [ps(f"p1_xp{i}", [P, 4 * T]) for i in range(2)]
        pkv = [ps(f"p1_kv{i}", [T, HALF]) for i in range(4)]
        pT = [ps(f"p1_kvT{i}", [P, HALF]) for i in range(2)]

        w_in = [sem(f"p1_w_in{n}") for n in range(2 * C)]
        w_hi_done, w_lo_done = sem("p1_w_hi_done"), sem("p1_w_lo_done")
        x_in = [sem(f"p1_x_in{i}") for i in range(2)]
        var_ready, std_ready, ln_step = sem("p1_var"), sem("p1_std"), sem("p1_ln_step")
        xn_ready, xT_mm, xT_hi_done, xT_lo_done = sem("p1_xn"), sem("p1_xT_mm"), sem("p1_xT_hi_done"), sem("p1_xT_lo_done")
        xT_out = [sem(f"p1_xT_out{i}") for i in range(2)]
        kv_mm, kv_hi_done, kv_lo_done = sem("p1_kv_mm"), sem("p1_kv_hi_done"), sem("p1_kv_lo_done")
        kvT_mm, kvT_added = sem("p1_kvT_mm"), sem("p1_kvT_added")

        x_dram = io["x"].rearrange("(t p) d -> t p d", p=T)
        w_dram = [io["wkT"].rearrange("(c p) n -> c p n", p=P), io["wvT"].rearrange("(c p) n -> c p n", p=P)]
        block = ctx.block()

        @block.sync
        def _(sp):
            def load_x(t, b, k):
                if k:
                    sp.wait_ge(xT_mm, 2 * (t - 1))
                sp.dma_start(x[:, b, :], x_dram[bass.ds(t, 1), :, :].rearrange("a p d -> (a p) d") if k else x_dram[t, :, :]).then_inc(x_in[b], 16)
            load_x(0, 0, False)
            for n in range(2 * C):
                sp.dma_start(w_raw[:, n // C, n % C, :], w_dram[n // C][n % C]).then_inc(w_in[n], 16)
                if n == C - 1:
                    load_x(1, 1, False)

            def store_xT(t, b):
                sp.wait_ge(xT_hi_done, 2 * t + 2)
                sp.wait_ge(xT_lo_done, 2 * t + 2)
                sp.dma_start(scr["xT_hi"][bass.ds(t, 1), :, :].rearrange("a p d -> (a p) d"), xT_hi[:, b, :].bitcast(F32)).then_inc(xT_out[b], 16)
                sp.dma_start(scr["xT_lo"][bass.ds(t, 1), :, :].rearrange("a p d -> (a p) d"), xT_lo[:, b, :].bitcast(F32)).then_inc(xT_out[b], 16)
            with sp.Fori(0, NT // 2 - 1) as i:
                for b in range(2):
                    load_x(2 * i + 2 + b, b, True)
                    store_xT(2 * i + b, b)
            for b in range(2):
                store_xT(NT - 2 + b, b)
            for b in range(2):
                sp.wait_ge(xT_out[b], 32 * (NT // 2))

        def xT_halves(act, t, b, guard):
            if guard:
                act.wait_ge(kv_mm, 4 * t - 4)
                act.wait_ge(xT_out[b], 16 * (t - b))
            for h in range(2):
                act.wait_ge(xT_mm, 2 * t + h + 1)
                nc.scalar.copy(xT_hi[:, b, h * 4 * T:(h + 1) * 4 * T], xp[h][:, :]).then_inc(xT_hi_done, 1)

        def kv_half(act, t, q):
            if q == 0:
                act.wait_ge(kvT_mm, t)
            act.wait_ge(kv_mm, 4 * t + q + 1)
            nc.scalar.copy(kv_hi[:, q * HALF:(q + 1) * HALF], pkv[q][:, :]).then_inc(kv_hi_done, 1)

        @block.scalar
        def _(act):
            act_carrier = Carrier(nc, scr, act, "scalar")
            nc.scalar.activation(scr["spare"][0:1, 63:64], scr["spare"][0:1, 0:1], ACT.Sqrt)

            def root(t):
                hold(act_carrier, var_ready, t + 1)
                nc.scalar.activation(small[:, 1:2], small[:, 0:1], ACT.Sqrt).then_inc(std_ready, 1)

            for n in range(2 * C):
                split(nc, act, None, w_raw[:, n // C, n % C, :], w_hi[:, n // C, n % C, :], None, w_in[n], 16, w_hi_done, None, n)
                if n == 0:
                    root(0)
                if n == 2:
                    xT_halves(act, 0, 0, False)
                if n == C + 1:
                    root(1)

            def tile(t, b, first=False, last=False):
                kv_half(act, t, 0)
                if not first and not last:
                    root(t + 1)
                kv_half(act, t, 1)
                kv_half(act, t, 2)
                if not last:
                    xT_halves(act, t + 1, 1 - b, True)
                kv_half(act, t, 3)

            tile(0, 0, first=True)
            tile(1, 1)
            with act.Fori(1, NT // 2 - 1) as i:
                for b in range(2):
                    tile(2 * i + b, b)
            for b in range(2):
                tile(NT - 2 + b, b, last=b == 1)

        @block.vector
        def _(dve):
            dve_carrier = Carrier(nc, scr, dve, "vector")

            def norm(t, b):
                dve.wait_ge(x_in[b], 8 * (t - b) + 16)
                layernorm(nc, dve_carrier, x[:, b, :], x[:, b, :], stats, mv, small, ln_step, 7 * t, var_ready, std_ready, xn_ready, t)

            def xT_low(t, b):
                for h in range(2):
                    dve.wait_ge(xT_hi_done, 2 * t + h + 1)
                    at = slice(h * 4 * T, (h + 1) * 4 * T)
                    nc.vector.tensor_tensor(xT_lo[:, b, at], xp[h][:, :], xT_hi[:, b, at].bitcast(F32), ALU.subtract).then_inc(xT_lo_done, 1)

            def kv_low(t, q):
                dve.wait_ge(kv_hi_done, 4 * t + q + 1)
                at = slice(q * HALF, (q + 1) * HALF)
                nc.vector.tensor_tensor(kv_lo[:, at], pkv[q][:, :], kv_hi[:, at].bitcast(F32), ALU.subtract).then_inc(kv_lo_done, 1)

            def add_kvT(t):
                for h in range(2):
                    dve.wait_ge(kvT_mm, t + 1)
                    dve.wait_ge(kvT_added, 2 * t + h + 1)
                    at = slice(h * HALF, (h + 1) * HALF)
                    nc.vector.tensor_tensor(kvT[:, at], kvT[:, at], pT[h][:, :], ALU.add).then_inc(kvT_added, 1)

            def tile(t, b, first=False, last=False):
                if not first:
                    add_kvT(t - 1)
                kv_low(t, 0)
                if not first and not last:
                    norm(t + 1, 1 - b)
                kv_low(t, 1)
                kv_low(t, 2)
                if not last:
                    xT_low(t + 1, 1 - b)
                kv_low(t, 3)

            for h in range(2):
                nc.vector.memset(kvT[:, h * HALF:(h + 1) * HALF], 0.0).then_inc(kvT_added, 1)
            norm(0, 0)
            for n in range(2 * C):
                split(nc, None, dve, w_raw[:, n // C, n % C, :], w_hi[:, n // C, n % C, :], w_lo[:, n // C, n % C, :], None, 0, w_hi_done, w_lo_done, n)
                if n == 2:
                    xT_low(0, 0)
                if n == C + 1:
                    norm(1, 1)
            tile(0, 0, first=True)
            tile(1, 1)
            with dve.Fori(1, NT // 2 - 1) as i:
                for b in range(2):
                    tile(2 * i + b, b)
            for b in range(2):
                tile(NT - 2 + b, b, last=b == 1)
            add_kvT(NT - 1)

        @block.tensor
        def _(pe):
            def transposes(t, b):
                pe.wait_ge(xn_ready, t + 1)
                pe.wait_ge(xT_lo_done, 2 * t)
                for c in range(C):
                    i = pe.transpose(xp[c // 4][:, (c % 4) * T:(c % 4 + 1) * T], x[:, b, c * P:(c + 1) * P], ident[0:T, 0:T])
                    if c % 4 == 3:
                        i.then_inc(xT_mm, 1)

            def project(t, b, q, first):
                pe.wait_ge(xT_lo_done, 2 * t + 2)
                if not first:
                    pe.wait_ge(kv_lo_done, 4 * t - 3 + q)
                for c in range(C):
                    if first and t == 0:
                        pe.wait_ge(w_lo_done, (q // 2) * C + c + 1)
                    at = slice(c * T, (c + 1) * T)
                    col = slice((q % 2) * HALF, (q % 2 + 1) * HALF)
                    i = mm3(pe, pkv[q][:, :], xT_hi[:, b, at], xT_lo[:, b, at],
                            w_hi[:, q // 2, c, col], w_lo[:, q // 2, c, col], c == 0, c == C - 1)
                i.then_inc(kv_mm, 1)

            def products(t):
                pe.wait_ge(kv_lo_done, 4 * t + 4)
                pe.wait_ge(kvT_added, 2 * t + 2)
                for j in range(C):
                    k, v = slice(j * P, (j + 1) * P), slice(D + j * P, D + (j + 1) * P)
                    i = mm3(pe, pT[j // 4][:, (j % 4) * P:(j % 4 + 1) * P], kv_hi[:, v], kv_lo[:, v], kv_hi[:, k], kv_lo[:, k], True, True)
                i.then_inc(kvT_mm, 1)

            def tile(t, b, first=False, last=False):
                project(t, b, 0, first)
                if not first:
                    products(t - 1)
                project(t, b, 1, first)
                project(t, b, 2, first)
                if not last:
                    transposes(t + 1, 1 - b)
                project(t, b, 3, first)

            pe.wait_ge(scr["go"], 1)
            transposes(0, 0)
            tile(0, 0, first=True)
            tile(1, 1)
            with pe.Fori(1, NT // 2 - 1) as i:
                for b in range(2):
                    tile(2 * i + b, b)
            for b in range(2):
                tile(NT - 2 + b, b, last=b == 1)
            products(NT - 1)


E = 20000
EC = 125
NCH = E // EC
NPAIR = NCH // 2
PIECES = ((0, 418), (418, 834), (834, 1250))


def mixing_and_adjacency(nc, io, scr):
    with Phase(nc) as ctx:
        sb = lambda n, s, d: ctx.enter_context(nc.sbuf_tensor(n, s, d))
        ps = lambda n, s: ctx.enter_context(nc.psum_tensor(n, s, F32))
        sem = ctx.sem
        kv_hi, kv_lo = sb("p2_kv_hi", [P, D], F32R), sb("p2_kv_lo", [P, D], F32R)
        WB = 3
        w_hi, w_lo = sb("p2_w_hi", [P, WB, D], F32R), sb("p2_w_lo", [P, WB, D], F32R)
        w_raw = before_split(nc, "p2_w_raw", w_lo)
        by_block = lambda t, b: t[:, b, :].rearrange("p (j c) -> p j c", c=P)
        kvo_hi, kvo_lo = sb("p2_kvo_hi", [P, C, D], F32R), sb("p2_kvo_lo", [P, C, D], F32R)
        m_full, m_hi, m_lo = sb("p2_m_full", [P, D], F32), sb("p2_m_hi", [P, 2, D], F32R), sb("p2_m_lo", [P, 2, D], F32R)
        pm = [ps(f"p2_m{h}", [P, HALF]) for h in range(2)]
        o_in, q_in = [sem(f"p2_o_in{b}") for b in range(WB)], [sem(f"p2_q_in{b}") for b in range(2)]
        kv_zero, kv_hi_done, kv_lo_done = sem("p2_kv_zero"), sem("p2_kv_hi_done"), sem("p2_kv_lo_done")
        o_hi_done, o_lo_done, q_hi_done, q_lo_done = sem("p2_o_hi_done"), sem("p2_o_lo_done"), sem("p2_q_hi_done"), sem("p2_q_lo_done")
        kvo_mm, kvo_hi_done, kvo_lo_done = sem("p2_kvo_mm"), sem("p2_kvo_hi_done"), sem("p2_kvo_lo_done")
        m_mm, m_hi_done, m_full_done, m_lo_done = sem("p2_m_mm"), sem("p2_m_hi_done"), sem("p2_m_full_done"), sem("p2_m_lo_done")
        m_out = [sem(f"p2_m_out{b}") for b in range(2)]
        HOT = 16
        src_i, dst_i = sb("p2_src_i", [EC, NCH], I32), sb("p2_dst_i", [EC, NCH], I32)
        src, dst = sb("p2_src", [EC, NCH], F32), sb("p2_dst", [EC, NCH], F32)
        nodes = sb("p2_nodes", [T, N], F16)
        own_i, own = sb("p2_own_i", [T, NT], I32), sb("p2_own", [T, NT], F32)
        at_least = sb("p2_at_least", [EC, NT + 1, NCH], BF16)
        inside = sb("p2_inside", [EC, NT, NCH], BF16)
        ones, eye = sb("p2_ones", [EC, 1], BF16), sb("p2_eye", [T, T], BF16)
        up_i, up = sb("p2_up_i", [1, NPAIR, 2], I32), sb("p2_up", [1, NPAIR, 2], BF16)
        down = sb("p2_down", [1, NPAIR, 2], BF16)
        held, work = sb("p2_held", [1, NT, NCH], BF16), sb("p2_work", [1, NT, NCH], BF16)
        last, first = sb("p2_last", [1, NT], F32), sb("p2_first", [1, NT], F32)
        before, total = sb("p2_before", [1, NT], F32), sb("p2_total", [1, NT], F32)
        bounds = sb("p2_bounds", [1, 2, NT], I32)
        row, col = sb("p2_row", [EC, HOT, N], BF16), sb("p2_col", [EC, HOT, T], BF16)
        self_row = sb("p2_self_row", [T, N], BF16)
        full, hi, lo = sb("p2_full", [T, N], F32), sb("p2_hi", [T, 2, N], F32R), sb("p2_lo", [T, N], F32R)
        nodes_i = full[:, :].bitcast(I32)
        acc = [[ps(f"p2_acc{a}{b}", [T, HALF]) for b in range(3)] for a in range(2)]
        edges_in, step, counted, bounds_ready = sem("p2_edges_in"), sem("p2_step"), sem("p2_counted"), sem("p2_bounds_ready")
        iotas, inside_ready = sem("p2_iotas"), sem("p2_inside_ready")
        hot_ready, hot_used, self_ready, self_used = sem("p2_hot_ready"), sem("p2_hot_used"), sem("p2_self_ready"), sem("p2_self_used")
        acc_done, hi_done, full_done, lo_done = sem("p2_acc_done"), sem("p2_hi_done"), sem("p2_full_done"), sem("p2_lo_done")
        stored, stored_lo = [sem(f"p2_stored{b}") for b in range(2)], sem("p2_stored_lo")
        wo = io["woT"].rearrange("(c p) n -> c p n", p=P)
        wq = io["wq"].rearrange("(j p) c -> p j c", p=P)
        block = ctx.block()

        def pairs(eng, b):
            lo_ = eng.value_load(bounds[0:1, 0, bass.ds(b, 1)], min_val=0, max_val=NPAIR - 1)
            hi_ = eng.value_load(bounds[0:1, 1, bass.ds(b, 1)], min_val=1, max_val=NPAIR)
            return lo_, hi_

        def know_width(eng):
            eng.wait_ge(bounds_ready, 1)
            return wide_counts(eng, scr)

        @block.sync
        def _(sp):
            sp.dma_start(src_i[:, :], io["src"]).then_inc(edges_in, 16)
            sp.dma_start(dst_i[:, :], io["dst"]).then_inc(edges_in, 16)
            for j in range(C):
                if j >= WB:
                    sp.wait_ge(kvo_mm, 2 * (j - WB + 1))
                sp.dma_start(w_raw[:, j % WB, :], wo[j]).then_inc(o_in[j % WB], 16)

            def load_q(c, b):
                sp.dma_start(by_block(w_raw, b), wq[:, :, bass.ds(c * P, P)]).then_inc(q_in[b], 16)

            for b in range(2):
                sp.wait_ge(kvo_mm, 2 * max(j + 1 for j in range(C) if j % WB == b))
                load_q(b, b)
            wide = know_width(sp)

            def next_q(n, b):
                sp.wait_ge(m_mm, 2 * n + 2)
                load_q(n + 2, b)

            def store_adjacency(n, b):
                def store(name, t, signal):
                    sp.dma_start(scr[name][:, :, bass.ds(n, 1), :].rearrange("t p b i -> p t (b i)"),
                                 t.bitcast(F32).rearrange("p (t i) -> p t i", i=T)).then_inc(signal, 16)
                sp.wait_ge(hi_done, n + 1)
                store("AT_hi", hi[:, b, :], stored[b])
                with sp.If(wide > 0):
                    sp.wait_ge(lo_done, n + 1)
                    store("AT_lo", lo[:, :], stored_lo)

            def store_m(c, b):
                for name, t, done in (("M_hi", m_hi, m_hi_done), ("M_lo", m_lo, m_lo_done)):
                    sp.wait_ge(done, 2 * c + 2)
                    sp.dma_start(scr[name][bass.ds(c, 1), :, :].rearrange("a p n -> (a p) n"), t[:, b, :].bitcast(F32)).then_inc(m_out[b], 16)

            with sp.Fori(0, C // 2 - 1) as i:
                for b in range(2):
                    store_adjacency(2 * i + b, b)
                    next_q(2 * i + b, b)
                    store_m(2 * i + b, b)
            for n in range(C - 2, NT):
                store_adjacency(n, n % 2)
                if n < C:
                    store_m(n, n % 2)
            for b in range(2):
                sp.wait_ge(stored[b], 16 * (NT // 2) + 1)
                sp.wait_ge(m_out[b], 16 * C + 1)
            with sp.If(wide > 0):
                sp.wait_ge(stored_lo, 16 * NT)

        @block.gpsimd
        def _(pool):
            carrier = Carrier(nc, scr, pool, "gpsimd")
            for s in (*stored, *m_out, self_used):
                pool.sem_inc(s, 1)
            nc.gpsimd.iota(nodes_i, pattern=[[1, N]], base=0, channel_multiplier=0).then_inc(iotas, 1)
            nc.gpsimd.iota(own_i[:, :], pattern=[[T, NT]], base=0, channel_multiplier=1).then_inc(iotas, 1)
            nc.gpsimd.iota(up_i[:, :, :], pattern=[[1, NPAIR], [0, 2]], base=1, channel_multiplier=0).then_inc(iotas, 1)

            def low(b, done, value, signal):
                pool.wait_ge(done, value)
                nc.gpsimd.tensor_tensor(w_lo[:, b, :], w_raw[:, b, :], w_hi[:, b, :].bitcast(F32), ALU.subtract).then_inc(signal, 1)

            def q_low(c, b):
                low(b, q_hi_done, c + 1, q_lo_done)

            for j in range(C):
                low(j % WB, o_hi_done, j + 1, o_lo_done)
            wide = know_width(pool)

            def adjacency_low(n, b):
                with pool.If(wide > 0):
                    if not (isinstance(n, int) and n == 0):
                        pool.wait_ge(stored_lo, 16 * n)
                    pool.wait_ge(full_done, n + 1)
                    nc.gpsimd.tensor_tensor(lo[:, :], full[:, :], hi[:, b, :].bitcast(F32), ALU.subtract).then_inc(lo_done, 1)

            def m_low(c, b):
                for h in range(2):
                    at = slice(h * HALF, (h + 1) * HALF)
                    pool.wait_ge(m_full_done, 2 * c + h + 1)
                    nc.gpsimd.tensor_tensor(m_lo[:, b, at], m_full[:, at], m_hi[:, b, at].bitcast(F32), ALU.subtract).then_inc(m_lo_done, 1)

            for b in range(2):
                q_low(b, b)
            for b in range(2):
                adjacency_low(b, b)
                m_low(b, b)
                q_low(2 + b, b)
            with pool.Fori(1, C // 2 - 1) as i:
                for b in range(2):
                    adjacency_low(2 * i + b, b)
                    m_low(2 * i + b, b)
                    q_low(2 * i + 2 + b, b)
            for n in range(C - 2, NT):
                adjacency_low(n, n % 2)
                if n < C:
                    m_low(n, n % 2)

        @block.scalar
        def _(act):
            carrier = Carrier(nc, scr, act, "scalar")
            act.wait_ge(kv_zero, 2)
            for h in range(2):
                rows = slice(64 * h, 64 * h + 64)
                d = lambda t: t[rows, :].rearrange("p (j x) -> p j x", x=P)[:, :, 64 * h:64 * h + 64]
                i = nc.scalar.mul(d(kv_hi), d(scr["kvT"]), 0.125)
            i.then_inc(kv_hi_done, 1)

            def product_high(j):
                for h in range(2):
                    act.wait_ge(kvo_mm, 2 * j + h + 1)
                    nc.scalar.copy(kvo_hi[:, j, h * HALF:(h + 1) * HALF], pm[h][:, :]).then_inc(kvo_hi_done, 1)

            for j in range(C):
                split(nc, act, None, w_raw[:, j % WB, :], w_hi[:, j % WB, :], None, o_in[j % WB], 16 * (j // WB + 1), o_hi_done, None, j)
                if j:
                    product_high(j - 1)
            product_high(C - 1)

            def q_high(c, b):
                act.wait_ge(q_in[b], 8 * (c - b) + 16)
                nc.scalar.copy(w_hi[:, b, :], w_raw[:, b, :]).then_inc(q_hi_done, 1)

            for b in range(2):
                q_high(b, b)

            wide = know_width(act)

            def adjacency_high(n, b, first=False):
                act.wait_ge(stored[b], 8 * (n - b) + 1)
                hold(carrier, acc_done, n + 1)
                if not first:
                    with act.If(wide > 0):
                        hold(carrier, lo_done, n)
                for k, (a, z) in enumerate(PIECES):
                    s = nc.scalar.copy(hi[:, b, a:z], acc[b][k][:, 0:z - a])
                s.then_inc(hi_done, 1)
                with act.If(wide > 0):
                    for k, (a, z) in enumerate(PIECES):
                        s = nc.scalar.copy(full[:, a:z], acc[b][k][:, 0:z - a])
                    s.then_inc(full_done, 1)

            def m_high(c, b, first=False):
                act.wait_ge(m_out[b], 16 * (c - b) + 1)
                for h in range(2):
                    at = slice(h * HALF, (h + 1) * HALF)
                    act.wait_ge(m_mm, 2 * c + h + 1)
                    nc.scalar.copy(m_hi[:, b, at], pm[h][:, :]).then_inc(m_hi_done, 1)
                    if not first:
                        act.wait_ge(m_lo_done, 2 * c + h - 1)
                    nc.scalar.copy(m_full[:, at], pm[h][:, :]).then_inc(m_full_done, 1)

            adjacency_high(0, 0, first=True)
            m_high(0, 0, first=True)
            q_high(2, 0)
            adjacency_high(1, 1)
            m_high(1, 1)
            q_high(3, 1)
            with act.Fori(1, C // 2 - 1) as i:
                for b in range(2):
                    adjacency_high(2 * i + b, b)
                    m_high(2 * i + b, b)
                    q_high(2 * i + 2 + b, b)
            for n in range(C - 2, NT):
                adjacency_high(n, n % 2)
                if n < C:
                    m_high(n, n % 2)

        @block.vector
        def _(dve):
            n = [0]

            def link(ins):
                n[0] += 1
                ins.then_inc(step, 1)
                dve.wait_ge(step, n[0])

            nc.vector.memset(kv_hi[:, :].bitcast(F32), 0.0).then_inc(kv_zero, 1)
            nc.vector.memset(kv_lo[:, :].bitcast(F32), 0.0).then_inc(kv_zero, 1)
            nc.vector.memset(ones[:, :], 1.0)
            nc.vector.tensor_copy(eye[:, :], scr["ident"][0:T, 0:T])
            dve.wait_ge(edges_in, 32)
            nc.vector.tensor_copy(src[:, :], src_i[:, :])
            link(nc.vector.tensor_copy(dst[:, :], dst_i[:, :]))
            for b in range(NT + 1):
                i = nc.vector.tensor_scalar(at_least[:, b, :], dst[:, :], float(b * T), None, ALU.is_ge)
            link(i)
            nc.vector.tensor_tensor(inside[:, :, :], at_least[:, 0:NT, :], at_least[:, 1:NT + 1, :], ALU.subtract).then_inc(inside_ready, 1)

            dve.wait_ge(kv_zero, 2)
            dve.wait_ge(kv_hi_done, 1)
            for h in range(2):
                rows = slice(64 * h, 64 * h + 64)
                d = lambda t: t[rows, :].rearrange("p (j x) -> p j x", x=P)[:, :, 64 * h:64 * h + 64]
                i = nc.vector.scalar_tensor_tensor(d(kv_lo), d(scr["kvT"]), 0.125, d(kv_hi.bitcast(F32)), ALU.mult, ALU.subtract)
            i.then_inc(kv_lo_done, 1)

            def product_low(j):
                for h in range(2):
                    dve.wait_ge(kvo_hi_done, 2 * j + h + 1)
                    at = slice(h * HALF, (h + 1) * HALF)
                    nc.vector.tensor_tensor(kvo_lo[:, j, at], pm[h][:, :], kvo_hi[:, j, at].bitcast(F32), ALU.subtract).then_inc(kvo_lo_done, 1)

            dve.wait_ge(iotas, 3)
            nc.vector.tensor_copy(nodes[:, :], nodes_i)
            nc.vector.tensor_copy(own[:, :], own_i[:, :])
            link(nc.vector.tensor_copy(up[:, :, :], up_i[:, :, :]))
            nc.vector.tensor_scalar(down[:, :, :], up[:, :, :], -1.0, NPAIR + 1.0, ALU.mult, ALU.add)
            dve.wait_ge(counted, 1)
            for k in range(NT // 2):
                i = nc.vector.tensor_scalar(held[:, 2 * k:2 * k + 2, :], acc[k // 3][k % 3][0:1, 0:2 * NCH].rearrange("p (b c) -> p b c", c=NCH), 1.0, None, ALU.min)
            link(i)
            for k in range(NT // 2):
                i = nc.vector.tensor_reduce(total[:, 2 * k:2 * k + 2], acc[k // 3][k % 3][0:1, 0:2 * NCH].rearrange("p (b c) -> p b c", c=NCH), AX, ALU.add)
            link(i)
            link(nc.vector.tensor_reduce(before[:, 0:1], total[:, :], AX, ALU.max))
            link(nc.vector.tensor_scalar(scr["wide"][:, :], before[:, 0:1], 4095.0, None, ALU.is_gt))
            flat = lambda t: t[:, :, :].rearrange("p k j -> p (k j)").unsqueeze(1).to_broadcast([1, NT, NCH])
            link(nc.vector.tensor_tensor(work[:, :, :], held[:, :, :], flat(up), ALU.mult))
            link(nc.vector.tensor_reduce(last[:, :], work[:, :, :], AX, ALU.max))
            product_low(0)
            link(nc.vector.tensor_tensor(work[:, :, :], held[:, :, :], flat(down), ALU.mult))
            link(nc.vector.tensor_reduce(first[:, :], work[:, :, :], AX, ALU.max))
            product_low(1)
            link(nc.vector.tensor_scalar(last[:, :], last[:, :], 1.0, None, ALU.max))
            link(nc.vector.tensor_scalar(first[:, :], first[:, :], -1.0, float(NPAIR), ALU.mult, ALU.add))
            link(nc.vector.tensor_scalar(before[:, :], last[:, :], -1.0, None, ALU.add))
            link(nc.vector.tensor_tensor(first[:, :], first[:, :], before[:, :], ALU.min))
            link(nc.vector.tensor_copy(bounds[:, 0, :], first[:, :]))
            nc.vector.tensor_copy(bounds[:, 1, :], last[:, :]).then_inc(bounds_ready, 1)
            for j in range(2, C):
                product_low(j)

            dve.wait_ge(bounds_ready, 1)
            with dve.register("p2_dve_taken") as taken:
                dve.reg_mov(taken, 0)
                with dve.Fori(0, NT) as blk:
                    lo_, hi_ = pairs(dve, blk)
                    dve.wait_ge(self_used, blk + 1)
                    nc.vector.tensor_scalar(self_row[:, :], nodes[:, :], own[:, bass.ds(blk, 1)], None, ALU.is_equal).then_inc(self_ready, 1)
                    with dve.Fori(lo_, hi_) as p:
                        done = dve.snap(taken)
                        at = dve.snap((done % (HOT // 2)) * 2)
                        for j in range(2):
                            dve.wait_ge(hot_used, 2 * done + (j + 1))
                            nc.vector.tensor_scalar(col[:, bass.ds(at + j, 1), :].rearrange("p o i -> p (o i)"), nodes[:, bass.ds(blk * T, T)], dst[:, bass.ds(2 * p + j, 1)], None, ALU.is_equal)
                            nc.vector.tensor_scalar(row[:, bass.ds(at + j, 1), :].rearrange("p o i -> p (o i)"), nodes[:, :], src[:, bass.ds(2 * p + j, 1)], None, ALU.is_equal).then_inc(hot_ready, 1)
                        dve.reg_add(taken, taken, 1)

        @block.tensor
        def _(pe):
            pe.sem_inc(hot_used, HOT)
            pe.wait_ge(inside_ready, 1)
            for k in range(NT // 2):
                i = pe.matmul(acc[k // 3][k % 3][0:1, 0:2 * NCH], ones[:, :], inside[:, 2 * k:2 * k + 2, :].rearrange("p b c -> p (b c)"), start=True, stop=True)
            i.then_inc(counted, 1)
            pe.wait_ge(kv_lo_done, 1)
            for j in range(C):
                pe.wait_ge(o_lo_done, j + 1)
                for h in range(2):
                    if j:
                        pe.wait_ge(kvo_lo_done, 2 * j - 1 + h)
                    at, k = slice(h * HALF, (h + 1) * HALF), slice(j * P, (j + 1) * P)
                    mm3(pe, pm[h][:, :], kv_hi[:, k], kv_lo[:, k], w_hi[:, j % WB, at], w_lo[:, j % WB, at], True, True).then_inc(kvo_mm, 1)
            pe.wait_ge(kvo_lo_done, 2 * C)
            wide = know_width(pe)

            with pe.register("p2_pe_taken") as taken:
                pe.reg_mov(taken, 0)

                def adjacency_block(blk, b, first=False):
                    lo_, hi_ = pairs(pe, blk)
                    if not first:
                        pe.wait_ge(hi_done, blk - b)
                        with pe.If(wide > 0):
                            pe.wait_ge(full_done, blk - b)
                    pe.wait_ge(self_ready, blk + 1)
                    for k, (a, z) in enumerate(PIECES):
                        m = pe.matmul(acc[b][k][:, 0:z - a], eye[:, :], self_row[:, a:z], start=True, stop=False)
                    m.then_inc(self_used, 1)
                    with pe.Fori(lo_, hi_) as p:
                        done = pe.snap(taken)
                        at = pe.snap((done % (HOT // 2)) * 2)
                        for j in range(2):
                            pe.wait_ge(hot_ready, 2 * done + (j + 1))
                            for k, (a, z) in enumerate(PIECES):
                                m = pe.matmul(acc[b][k][:, 0:z - a], col[:, bass.ds(at + j, 1), :].rearrange("p o i -> p (o i)"),
                                              row[:, bass.ds(at + j, 1), a:z].rearrange("p o i -> p (o i)"), start=False, stop=False)
                            m.then_inc(hot_used, 1)
                        pe.reg_add(taken, taken, 1)
                    for k in range(3):
                        m = pe.matmul(acc[b][k][0:T, 0:2], scr["zero"][0:T, 0:T], scr["zero"][0:T, 0:2], start=False, stop=True)
                    m.then_inc(acc_done, 1)

                def m_rows(c, b, first=False):
                    pe.wait_ge(q_lo_done, c + 1)
                    for h in range(2):
                        if not first:
                            pe.wait_ge(m_full_done, 2 * c - 1 + h)
                        at = slice(h * HALF, (h + 1) * HALF)
                        for j in range(C):
                            m = mm3(pe, pm[h][:, :], by_block(w_hi, b)[:, j, :], by_block(w_lo, b)[:, j, :], kvo_hi[:, j, at], kvo_lo[:, j, at], j == 0, j == C - 1)
                        m.then_inc(m_mm, 1)

                for b in range(2):
                    adjacency_block(b, b, first=True)
                    m_rows(b, b, first=b == 0)
                with pe.Fori(1, C // 2) as i:
                    for b in range(2):
                        adjacency_block(2 * i + b, b)
                        m_rows(2 * i + b, b)
                for b in range(2):
                    adjacency_block(C + b, b)


def wide_counts(eng, scr):
    return eng.value_load(scr["wide"][0:1, 0:1], min_val=0, max_val=1)


def load_tile(sp, dst, dram, t, done):
    src = dram[bass.ds(t, 1)] if not isinstance(t, int) else dram[t:t + 1]
    names = "abc"[:len(dram.shape) - 2]
    sp.dma_start(dst, src.rearrange(f"o p {' '.join(names)} -> (o p) ({' '.join(names)})")).then_inc(done, 16)


def node_features(nc, io, scr):
    with Phase(nc) as ctx:
        sb = lambda n, s, d: ctx.enter_context(nc.sbuf_tensor(n, s, d))
        sem = ctx.sem
        w_hi, w_lo = sb("p4_w_hi", [P, C, D], F32R), sb("p4_w_lo", [P, C, D], F32R)
        w_raw = before_split(nc, "p4_w_raw", w_lo)
        xT_hi, xT_lo = sb("p4_xT_hi", [P, 2, C * T], F32R), sb("p4_xT_lo", [P, 2, C * T], F32R)
        at_hi, at_lo = sb("p4_at_hi", [T, NT * T], F32R), sb("p4_at_lo", [T, NT * T], F32R)
        bias, h_b = sb("p4_bias", [T, D], F32), sb("p4_h_b", [T, D], F32)
        ones = sb("p4_ones", [T, 2], F32R)
        small = sb("p4_small", [T, 8], F32)
        hs_hi, hs_lo, dinv = scr["hs_hi"], scr["hs_lo"], scr["dinv"]
        ph = [ctx.enter_context(nc.psum_tensor(f"p4_h{b}", [T, HALF], F32)) for b in range(4)]
        pdeg = ctx.enter_context(nc.psum_tensor("p4_deg", [T, 2], F32))
        w_in, x_in = [sem(f"p4_w_in{c}") for c in range(C)], [sem(f"p4_x_in{b}") for b in range(2)]
        at_in, at_lo_in, bias_in, ones_ready = sem("p4_at_in"), sem("p4_at_lo_in"), sem("p4_bias_in"), sem("p4_ones")
        w_hi_done, w_lo_done = sem("p4_w_hi_done"), sem("p4_w_lo_done")
        deg_mm, deg_ready, root_ready, step, dinv_ready = sem("p4_deg_mm"), sem("p4_deg"), sem("p4_root"), sem("p4_step"), sem("p4_dinv")
        h_mm, hb_done, hi_done, lo_done = sem("p4_h_mm"), sem("p4_hb_done"), sem("p4_hi_done"), sem("p4_lo_done")
        block = ctx.block()
        wg = io["wgT"].rearrange("(c p) n -> c p n", p=P)

        @block.sync
        def _(sp):
            wide = wide_counts(sp, scr)

            def loads(t, b):
                load_tile(sp, xT_hi[:, b, :].bitcast(F32), scr["xT_hi"], t, x_in[b])
                load_tile(sp, xT_lo[:, b, :].bitcast(F32), scr["xT_lo"], t, x_in[b])

            def load_at(t):
                load_tile(sp, at_hi[:, :].bitcast(F32), scr["AT_hi"], t, at_in)
                with sp.If(wide > 0):
                    load_tile(sp, at_lo[:, :].bitcast(F32), scr["AT_lo"], t, at_lo_in)

            for c in range(C):
                sp.dma_start(w_raw[:, c, :], wg[c]).then_inc(w_in[c], 16)
                if c == 0:
                    loads(0, 0)
            load_at(0)
            loads(1, 1)
            sp.dma_start(bias[:, :], io["gb"].to_broadcast([T, D])).then_inc(bias_in, 16)
            sp.wait_ge(deg_mm, 1)
            load_at(1)
            with sp.Fori(1, NT // 2) as i:
                for b in range(2):
                    t = 2 * i + b
                    sp.wait_ge(h_mm, 2 * (t - 1))
                    loads(t, b)
                    sp.wait_ge(deg_mm, t)
                    load_at(t)

        @block.scalar
        def _(act):
            carrier = Carrier(nc, scr, act, "scalar")
            for c in range(C):
                split(nc, act, None, w_raw[:, c, :], w_hi[:, c, :], None, w_in[c], 16, w_hi_done, None, c)

            def root(t):
                hold(carrier, deg_ready, t + 2)
                nc.scalar.activation(small[:, 1:2], small[:, 0:1], ACT.Sqrt).then_inc(root_ready, 1)

            def tile(t):
                for h in range(2):
                    hold(carrier, hb_done, 2 * t + h + 5)
                    nc.scalar.activation(hs_hi[:, bass.ds(t, 1), h * HALF:(h + 1) * HALF].rearrange("p o n -> p (o n)"),
                                         h_b[:, h * HALF:(h + 1) * HALF], ACT.Copy, scale=dinv[:, bass.ds(t, 1)]).then_inc(hi_done, 1)

            with act.Fori(0, NT) as t:
                root(t)
                tile(t)

        @block.vector
        def _(dve):
            nc.vector.memset(ones[:, :].bitcast(F32), 1.0).then_inc(ones_ready, 1)
            for c in range(C):
                split(nc, None, dve, w_raw[:, c, :], w_hi[:, c, :], w_lo[:, c, :], None, 0, w_hi_done, w_lo_done, c)
            dve.wait_ge(bias_in, 16)

            def tile(t, b):
                dve.wait_ge(deg_mm, t + 1)
                nc.vector.tensor_copy(small[:, 0:1], pdeg[:, 0:1]).then_inc(deg_ready, 1)
                dve.wait_ge(root_ready, t + 1)
                inverse_root(nc, dve, small, step, 4 * t)
                dve.wait_ge(step, 4 * t + 4)
                nc.vector.tensor_copy(dinv[:, bass.ds(t, 1)], small[:, 6:7]).then_inc(dinv_ready, 1)
                dve.wait_ge(dinv_ready, t + 1)
                for h in range(2):
                    at = slice(h * HALF, (h + 1) * HALF)
                    dve.wait_ge(h_mm, 2 * t + h + 1)
                    nc.vector.tensor_tensor(h_b[:, at], ph[2 * b + h][:, :], bias[:, at], ALU.add).then_inc(hb_done, 1)
                for h in range(2):
                    at = slice(h * HALF, (h + 1) * HALF)
                    dve.wait_ge(hi_done, 2 * t + h + 1)
                    flat = lambda x: x[:, bass.ds(t, 1), at].rearrange("p o n -> p (o n)")
                    nc.vector.scalar_tensor_tensor(flat(hs_lo), h_b[:, at], dinv[:, bass.ds(t, 1)], flat(hs_hi).bitcast(F32), ALU.mult, ALU.subtract).then_inc(lo_done, 1)

            with dve.Fori(0, NT // 2) as i:
                for b in range(2):
                    tile(2 * i + b, b)

        @block.tensor
        def _(pe):
            pe.sem_inc(hb_done, 4)
            pe.sem_inc(deg_ready, 1)
            pe.wait_ge(ones_ready, 1)
            wide = wide_counts(pe, scr)

            def degree(t):
                pe.wait_ge(deg_ready, t + 1)
                pe.wait_ge(at_in, 16 * t + 16)
                pe.matmul(pdeg[:, :], at_hi[:, 0:T], ones[:, :], start=True, stop=False)
                with pe.If(wide > 0):
                    pe.wait_ge(at_lo_in, 16 * t + 16)
                    for j in range(NT):
                        pe.matmul(pdeg[:, :], at_lo[:, j * T:(j + 1) * T], ones[:, :], start=False, stop=False)
                for j in range(1, NT):
                    m = pe.matmul(pdeg[:, :], at_hi[:, j * T:(j + 1) * T], ones[:, :], start=False, stop=j == NT - 1)
                m.then_inc(deg_mm, 1)

            def features(t, b, first=False):
                pe.wait_ge(x_in[b], 16 * (t - b) + 32)
                for h in range(2):
                    pe.wait_ge(hb_done, 2 * t + h + 1)
                    col = slice(h * HALF, (h + 1) * HALF)
                    for c in range(C):
                        if first and h == 0:
                            pe.wait_ge(w_lo_done, c + 1)
                        at = slice(c * T, (c + 1) * T)
                        m = mm3(pe, ph[2 * b + h][:, :], xT_hi[:, b, at], xT_lo[:, b, at], w_hi[:, c, col], w_lo[:, c, col], c == 0, c == C - 1)
                    m.then_inc(h_mm, 1)

            features(0, 0, first=True)
            degree(0)
            features(1, 1)
            degree(1)
            with pe.Fori(1, NT // 2) as i:
                for b in range(2):
                    features(2 * i + b, b)
                    degree(2 * i + b)


EXPERTS = 8


def aggregate_and_mix(nc, io, scr):
    with Phase(nc) as ctx:
        sb = lambda n, s, d: ctx.enter_context(nc.sbuf_tensor(n, s, d))
        ps = lambda n, s: ctx.enter_context(nc.psum_tensor(n, s, F32))
        sem = ctx.sem
        m_hi, m_lo = sb("p5_m_hi", [P, C, D], F32R), sb("p5_m_lo", [P, C, D], F32R)
        at_hi, at_lo = sb("p5_at_hi", [T, 2, NT * T], F32R), sb("p5_at_lo", [T, NT * T], F32R)
        xT_hi, xT_lo = sb("p5_xT_hi", [P, 2, C * T], F32R), sb("p5_xT_lo", [P, C * T], F32R)
        x1, xn = sb("p5_x1", [T, 2, D], F32), sb("p5_xn", [T, D], F32)
        nT_hi, nT_lo = sb("p5_nT_hi", [P, C * T], F32R), sb("p5_nT_lo", [P, C * T], F32R)
        r_raw = sb("p5_r_raw", [P, C, EXPERTS], F32)
        r_parts = sb("p5_r_parts", [P, C, 2, EXPERTS], F32R)
        r_hi, r_lo = r_parts[:, :, 0, :], r_parts[:, :, 1, :]
        log_low = sb("p5_log_low", [T, EXPERTS], F32)
        stats, mv, small = sb("p5_stats", [T, 2, 6], F32), sb("p5_mv", [T, 2], F32), sb("p5_small", [T, 8], F32)
        hs_hi, hs_lo, dinv, logits = scr["hs_hi"], scr["hs_lo"], scr["dinv"], scr["logits"]
        pagg, pmix = [ps(f"p5_agg{h}", [T, HALF]) for h in range(2)], [ps(f"p5_mix{h}", [T, HALF]) for h in range(2)]
        pT = [ps(f"p5_T{h}", [P, 4 * T]) for h in range(2)]
        plog = ps("p5_log", [T, 2, EXPERTS])
        m_in, r_in = [sem(f"p5_m_in{h}") for h in range(2)], sem("p5_r_in")
        at_in, at_lo_in = [sem(f"p5_at_in{b}") for b in range(2)], sem("p5_at_lo_in")
        xT_in, xT_lo_in, x_in = [sem(f"p5_xT_in{b}") for b in range(2)], sem("p5_xT_lo_in"), [sem(f"p5_x_in{b}") for b in range(2)]
        agg_mm, mix_mm = sem("p5_agg_mm"), sem("p5_mix_mm")
        agg_added, mix_added, x1_stored = sem("p5_agg_added"), sem("p5_mix_added"), [sem(f"p5_x1_stored{b}") for b in range(2)]
        step, var_ready, std_ready, xn_ready, xn_stored = sem("p5_step"), sem("p5_var"), sem("p5_std"), sem("p5_xn"), sem("p5_xn_stored")
        nT_mm, nT_hi_done, nT_lo_done, nT_stored = sem("p5_nT_mm"), sem("p5_nT_hi_done"), sem("p5_nT_lo_done"), sem("p5_nT_stored")
        r_hi_done, r_lo_done, log_mm, log_done = sem("p5_r_hi_done"), sem("p5_r_lo_done"), sem("p5_log_mm"), sem("p5_log_done")
        low_taken = sem("p5_low_taken")
        block = ctx.block()
        x_dram = io["x"].rearrange("(t p) d -> t p d", p=T)

        @block.sync
        def _(sp):
            wide = wide_counts(sp, scr)

            def load_at_lo(t):
                with sp.If(wide > 0):
                    if not (isinstance(t, int) and t == 0):
                        sp.wait_ge(agg_mm, 2 * t)
                    load_tile(sp, at_lo[:, :].bitcast(F32), scr["AT_lo"], t, at_lo_in)

            def load_at_hi(t, b):
                load_tile(sp, at_hi[:, b, :].bitcast(F32), scr["AT_hi"], t, at_in[b])

            def load_xT_hi(t, b):
                load_tile(sp, xT_hi[:, b, :].bitcast(F32), scr["xT_hi"], t, xT_in[b])

            def load_x(t, b):
                load_tile(sp, x1[:, b, :], x_dram, t, x_in[b])

            load_at_hi(0, 0)
            load_at_lo(0)
            load_x(0, 0)
            load_at_hi(1, 1)
            load_xT_hi(0, 0)
            load_tile(sp, xT_lo[:, :].bitcast(F32), scr["xT_lo"], 0, xT_lo_in)
            for h in range(2):
                at = slice(h * HALF, (h + 1) * HALF)
                for t_, name in ((m_hi, "M_hi"), (m_lo, "M_lo")):
                    sp.dma_start(t_[:, :, at].bitcast(F32), scr[name][:, :, at].rearrange("c p n -> p c n")).then_inc(m_in[h], 16)
            load_xT_hi(1, 1)
            load_x(1, 1)

            def rest(t, b, more):
                if more >= 1:
                    load_at_lo(t + 1)
                sp.wait_ge(mix_mm, 2 * t + 2)
                if more >= 1:
                    load_tile(sp, xT_lo[:, :].bitcast(F32), scr["xT_lo"], t + 1, xT_lo_in)
                if more >= 2:
                    load_at_hi(t + 2, b)
                    load_xT_hi(t + 2, b)
                sp.wait_ge(mix_added, 2 * t + 2)
                load_store = scr["x1"][bass.ds(t, 1), :, :].rearrange("o p d -> (o p) d")
                sp.dma_start(load_store, x1[:, b, :]).then_inc(x1_stored[b], 16)
                sp.wait_ge(xn_ready, t + 1)
                sp.dma_start(scr["xn2"][bass.ds(t * T, T), :], xn[:, :]).then_inc(xn_stored, 16)
                if more >= 2:
                    sp.wait_ge(x1_stored[b], 8 * (t - b) + 16)
                    load_x(t + 2, b)
                sp.wait_ge(nT_lo_done, 2 * t + 2)
                for name, t_ in (("nT_hi", nT_hi), ("nT_lo", nT_lo)):
                    sp.dma_start(scr[name][bass.ds(t, 1), :, :].rearrange("o p d -> (o p) d"), t_[:, :].bitcast(F32)).then_inc(nT_stored, 16)

            with sp.Fori(0, NT // 2 - 1) as i:
                for b in range(2):
                    rest(2 * i + b, b, 2)
            for b in range(2):
                rest(NT - 2 + b, b, 1 - b)
            for b in range(2):
                sp.wait_ge(x1_stored[b], 8 * NT)
            sp.wait_ge(xn_stored, 16 * NT)
            sp.wait_ge(nT_stored, 32 * NT)

        @block.gpsimd
        def _(pool):
            pool.dma_start(r_raw[:, :, :], io["router"].rearrange("(c p) e -> p c e", p=P)).then_inc(r_in, 16)

        @block.scalar
        def _(act):
            carrier = Carrier(nc, scr, act, "scalar")
            split(nc, act, None, r_raw[:, :, :], r_hi, None, r_in, 16, r_hi_done, None, 0)

            def tile(t, first=False):
                hold(carrier, var_ready, t + 1)
                nc.scalar.activation(small[:, 1:2], small[:, 0:1], ACT.Sqrt).then_inc(std_ready, 1)
                if not first:
                    act.wait_ge(nT_stored, 32 * t)
                    act.wait_ge(log_mm, t)
                for h in range(2):
                    act.wait_ge(nT_mm, 2 * t + h + 1)
                    nc.scalar.copy(nT_hi[:, h * 4 * T:(h + 1) * 4 * T], pT[h][:, :]).then_inc(nT_hi_done, 1)

            tile(0, True)
            with act.Fori(1, NT) as t:
                tile(t)

        @block.vector
        def _(dve):
            carrier = Carrier(nc, scr, dve, "vector")
            split(nc, None, dve, r_raw[:, :, :], r_hi, r_lo, None, 0, r_hi_done, r_lo_done, 0)

            def tile(t, b, first):
                dve.wait_ge(x_in[b], 8 * (t - b) + 16)
                for h in range(2):
                    at = slice(h * HALF, (h + 1) * HALF)
                    dve.wait_ge(agg_mm, 2 * t + h + 1)
                    nc.vector.scalar_tensor_tensor(x1[:, b, at], pagg[h][:, :], dinv[:, bass.ds(t, 1)], x1[:, b, at], ALU.mult, ALU.add).then_inc(agg_added, 1)
                for h in range(2):
                    at = slice(h * HALF, (h + 1) * HALF)
                    dve.wait_ge(agg_added, 2 * t + h + 1)
                    dve.wait_ge(mix_mm, 2 * t + h + 1)
                    nc.vector.tensor_tensor(x1[:, b, at], x1[:, b, at], pmix[h][:, :], ALU.add).then_inc(mix_added, 1)
                dve.wait_ge(mix_added, 2 * t + 2)
                if not first:
                    dve.wait_ge(xn_stored, 16 * t)
                    dve.wait_ge(nT_mm, 2 * t)
                layernorm(nc, carrier, x1[:, b, :], xn[:, :], stats, mv, small, step, 7 * t, var_ready, std_ready, xn_ready, t)
                for h in range(2):
                    dve.wait_ge(nT_hi_done, 2 * t + h + 1)
                    at = slice(h * 4 * T, (h + 1) * 4 * T)
                    nc.vector.tensor_tensor(nT_lo[:, at], pT[h][:, :], nT_hi[:, at].bitcast(F32), ALU.subtract).then_inc(nT_lo_done, 1)
                dve.wait_ge(log_mm, t + 1)
                nc.vector.tensor_copy(log_low[:, :], plog[:, 1, :]).then_inc(low_taken, 1)
                dve.wait_ge(low_taken, t + 1)
                nc.vector.tensor_tensor(logits[:, bass.ds(t, 1), :].rearrange("p o e -> p (o e)"), plog[:, 0, :], log_low[:, :], ALU.add).then_inc(log_done, 1)

            for b in range(2):
                tile(b, b, b == 0)
            with dve.Fori(1, NT // 2) as i:
                for b in range(2):
                    tile(2 * i + b, b, False)

        @block.tensor
        def _(pe):
            wide = wide_counts(pe, scr)

            def aggregate(t, b, h):
                if h == 0:
                    pe.wait_ge(at_in[b], 8 * (t - b) + 16)
                col = slice(h * HALF, (h + 1) * HALF)
                if not (isinstance(t, int) and t == 0):
                    pe.wait_ge(agg_added, 2 * t - 1 + h)
                counts = lambda x, j: x[:, j * T:(j + 1) * T]
                for j in range(NT):
                    pe.matmul(pagg[h][:, :], counts(at_hi[:, b, :], j), hs_lo[:, j, col], start=j == 0, stop=False)
                with pe.If(wide > 0):
                    pe.wait_ge(at_lo_in, 16 * t + 16)
                    for j in range(NT):
                        pe.matmul(pagg[h][:, :], counts(at_lo, j), hs_hi[:, j, col], start=False, stop=False)
                for j in range(NT):
                    m = pe.matmul(pagg[h][:, :], counts(at_hi[:, b, :], j), hs_hi[:, j, col], start=False, stop=j == NT - 1)
                m.then_inc(agg_mm, 1)

            def mix(t, b, first=False):
                pe.wait_ge(xT_in[b], 8 * (t - b) + 16)
                pe.wait_ge(xT_lo_in, 16 * t + 16)
                for h in range(2):
                    col = slice(h * HALF, (h + 1) * HALF)
                    if first:
                        pe.wait_ge(m_in[h], 32)
                    else:
                        pe.wait_ge(mix_added, 2 * t - 1 + h)
                    for c in range(C):
                        at = slice(c * T, (c + 1) * T)
                        m = mm3(pe, pmix[h][:, :], xT_hi[:, b, at], xT_lo[:, at], m_hi[:, c, col], m_lo[:, c, col], c == 0, c == C - 1)
                    m.then_inc(mix_mm, 1)

            def turn(t, first=False):
                pe.wait_ge(xn_ready, t + 1)
                if not first:
                    pe.wait_ge(nT_lo_done, 2 * t)
                for c in range(C):
                    m = pe.transpose(pT[c // 4][:, (c % 4) * T:(c % 4 + 1) * T], xn[:, c * P:(c + 1) * P], scr["ident"][0:T, 0:T])
                    if c % 4 == 3:
                        m.then_inc(nT_mm, 1)

            def route(t, first=False):
                if not first:
                    pe.wait_ge(log_done, t)
                pe.wait_ge(nT_lo_done, 2 * t + 2)
                for c in range(C):
                    at = slice(c * T, (c + 1) * T)
                    both = r_parts[:, c, :, :].rearrange("p k e -> p (k e)")
                    pe.matmul(plog[:, :, :].rearrange("p k e -> p (k e)"), nT_lo[:, at], both, start=c == 0, stop=False)
                    m = pe.matmul(plog[:, :, :].rearrange("p k e -> p (k e)"), nT_hi[:, at], both, start=False, stop=c == C - 1)
                m.then_inc(log_mm, 1)

            pe.wait_ge(r_lo_done, 1)
            for t in range(2):
                for h in range(2):
                    aggregate(t, t, h)
            mix(0, 0, first=True)
            mix(1, 1)
            turn(0, first=True)
            route(0, first=True)
            with pe.Fori(1, NT // 2) as i:
                for b in range(2):
                    t = 2 * i + b
                    aggregate(t, b, 0)
                    turn(t - 1)
                    aggregate(t, b, 1)
                    route(t - 1)
                    mix(t, b)
            turn(NT - 1)
            route(NT - 1)


TOP = 4
MOE = 512
SHARED = 256
SLOTS = 64
FAR = 1 << 20


def shared_and_routing(nc, io, scr, out):
    with Phase(nc) as ctx:
        sb = lambda n, s, d=F32: ctx.enter_context(nc.sbuf_tensor(n, s, d))
        ps = lambda n, s: ctx.enter_context(nc.psum_tensor(n, s, F32))
        sem = ctx.sem
        G = 2 * SHARED
        gu_raw, gu_hi, gu_lo = sb("p6_gu_raw", [P, C, G]), sb("p6_gu_hi", [P, C, G], F32R), sb("p6_gu_lo", [P, C, G], F32R)
        d_raw, d_hi, d_lo = sb("p6_d_raw", [P, 2, D]), sb("p6_d_hi", [P, 2, D], F32R), sb("p6_d_lo", [P, 2, D], F32R)
        nT_hi, nT_lo = sb("p6_nT_hi", [P, 2, C * T], F32R), sb("p6_nT_lo", [P, 2, C * T], F32R)
        y = sb("p6_y", [T, 2, D])
        sg, a = sb("p6_sg", [T, SHARED]), sb("p6_a", [T, SHARED])
        aT_hi, aT_lo = sb("p6_aT_hi", [P, 2 * T], F32R), sb("p6_aT_lo", [P, 2 * T], F32R)
        pgu, py = ps("p6_gu", [T, G]), [ps(f"p6_y{h}", [T, HALF]) for h in range(2)]
        paT = ps("p6_aT", [P, 2 * T])
        pcount = ps("p6_count", [T, 2, NT * EXPERTS])
        plist = ps("p6_list", [P, 2, SLOTS])
        gu_in, d_in = [sem(f"p6_gu_in{k}") for k in range(2)], sem("p6_d_in")
        nT_in, x1_in, stored = [sem(f"p6_nT_in{b}") for b in range(2)], [sem(f"p6_x1_in{b}") for b in range(2)], [sem(f"p6_stored{b}") for b in range(2)]
        gu_hi_done, gu_lo_done, d_hi_done, d_lo_done = sem("p6_gu_hi_done"), sem("p6_gu_lo_done"), sem("p6_d_hi_done"), sem("p6_d_lo_done")
        gu_mm, sg_done, a_done, aT_mm, aT_hi_done, aT_lo_done = sem("p6_gu_mm"), sem("p6_sg"), sem("p6_a"), sem("p6_aT_mm"), sem("p6_aT_hi_done"), sem("p6_aT_lo_done")
        y_mm, y_done = sem("p6_y_mm"), sem("p6_y_done")
        W = NT * EXPERTS
        sc, ez = sb("r_scores", [T, NT, EXPERTS]), sb("r_exp", [T, NT, EXPERTS])
        row_max, row_sum = sb("r_max", [T, NT]), sb("r_sum", [T, NT])
        bias = sb("r_bias", [T, 1])
        tri_i, tri = sb("r_tri_i", [T, EXPERTS, EXPERTS], I32), sb("r_tri", [T, EXPERTS, EXPERTS])
        full_i, full = sb("r_full_i", [T, EXPERTS, NT], I32), sb("r_full", [T, EXPERTS, NT])
        kth_i, kth = sb("r_kth_i", [T, TOP, EXPERTS], I32), sb("r_kth", [T, TOP, EXPERTS])
        below_i, below = sb("r_below_i", [T, T], I32), sb("r_below", [T, T], BF16)
        all_ones = sb("r_ones", [T, T], BF16)
        gt, eq = sb("r_gt", [T, NT, EXPERTS * EXPERTS]), sb("r_eq", [T, NT, EXPERTS * EXPERTS])
        rank, sel, sel_b = sb("r_rank", [T, NT, EXPERTS]), sb("r_sel", [T, NT, EXPERTS]), sb("r_sel_b", [T, NT, EXPERTS], BF16)
        wts, pos = sb("r_wts", [T, NT, EXPERTS]), sb("r_pos", [T, NT, EXPERTS])
        before, within = sb("r_before", [T, NT + 1, EXPERTS]), sb("r_within", [T, 2, W])
        over, tiles, base = sb("r_over", [T, EXPERTS, NT]), sb("r_tiles", [T, EXPERTS + 1]), sb("r_base", [T, EXPERTS])
        span = sb("r_span", [T, EXPERTS, EXPERTS])
        is_kth, picked = sb("r_is_kth", [T, NT, TOP * EXPERTS]), sb("r_picked", [T, NT, TOP * EXPERTS])
        row_of, row_i = sb("r_row", [T, NT, TOP]), sb("r_row_i", [T, NT * TOP], I32)
        token_i, entry = sb("r_token_i", [T, NT, TOP], I32), sb("r_entry", [T, NT, TOP, 2])
        blank = sb("r_blank", [P, SLOTS, 2])
        lists = sb("r_lists", [SLOTS, P, 2])
        consts, step, prob_in, exp_in, exp_done = sem("r_consts"), sem("r_step"), sem("r_bias_in"), sem("r_exp_in"), sem("r_exp_done")
        blank_set, blank_out, rows_ready, scattered = sem("r_blank_set"), sem("r_blank_out"), sem("r_rows_ready"), sem("r_scattered")
        sel_ready, counted, lists_in, lists_T, lists_done = sem("r_sel_ready"), sem("r_counted"), sem("r_lists_in"), sem("r_lists_T"), sem("r_lists_done")
        block = ctx.block()
        y_dram = out.rearrange("(t p) d -> t p d", p=T)

        @block.sync
        def _(sp):
            for k, name in enumerate(("s_gate", "s_up")):
                sp.dma_start(gu_raw[:, :, k * SHARED:(k + 1) * SHARED], io[name].rearrange("(c p) n -> p c n", p=P)).then_inc(gu_in[k], 16)

            def load_nT(t, b):
                load_tile(sp, nT_hi[:, b, :].bitcast(F32), scr["nT_hi"], t, nT_in[b])
                load_tile(sp, nT_lo[:, b, :].bitcast(F32), scr["nT_lo"], t, nT_in[b])

            def load_x1(t, b):
                load_tile(sp, y[:, b, :], scr["x1"], t, x1_in[b])

            load_nT(0, 0)
            sp.dma_start(d_raw[:, :, :], io["s_down"].rearrange("(c p) n -> p c n", p=P)).then_inc(d_in, 16)
            load_nT(1, 1)
            for b in range(2):
                load_x1(b, b)
            for k, (raw, src) in enumerate(scr["expert_pieces"](0)):
                sp.dma_start(raw, src).then_inc(scr["raw_in"][k], 16)

            def next_nT(t, b):
                sp.wait_ge(gu_mm, t + 1)
                load_nT(t + 2, b)

            def store_y(t, b, more):
                sp.wait_ge(y_done, 2 * t + 2)
                sp.dma_start(y_dram[bass.ds(t, 1), :, :].rearrange("o p d -> (o p) d"), y[:, b, :]).then_inc(stored[b], 16)
                if more:
                    sp.wait_ge(stored[b], 8 * (t - b) + 16)
                    load_x1(t + 2, b)

            next_nT(0, 0)
            next_nT(1, 1)
            store_y(0, 0, True)
            with sp.Fori(1, NT // 2 - 1) as i:
                for b in range(2):
                    next_nT(2 * i + b, b)
                    store_y(2 * i + b - 1, 1 - b, True)
            store_y(NT - 3, 1, True)
            for b in range(2):
                store_y(NT - 2 + b, b, False)
            for b in range(2):
                sp.wait_ge(stored[b], 8 * NT)

        @block.gpsimd
        def _(pool):
            pool.dma_start(bias[:, :], io["router_b"].to_broadcast([T, 1])).then_inc(prob_in, 16)
            nc.gpsimd.memset(blank[:, :, 0:1], float(FAR)).then_inc(blank_set, 1)
            nc.gpsimd.memset(blank[:, :, 1:2], 0.0).then_inc(blank_set, 1)
            pool.wait_ge(blank_set, 2)
            pool.dma_start(scr["lists"].rearrange("(p s) w -> p s w", p=P), blank[:, :, :]).then_inc(blank_out, 16)
            nc.gpsimd.iota(tri_i[:, :, :], pattern=[[1, EXPERTS], [-1, EXPERTS]], base=0, channel_multiplier=0).then_inc(consts, 1)
            nc.gpsimd.iota(full_i[:, :, :], pattern=[[0, EXPERTS], [P, NT]], base=0, channel_multiplier=0).then_inc(consts, 1)
            nc.gpsimd.iota(kth_i[:, :, :], pattern=[[1, TOP], [0, EXPERTS]], base=0, channel_multiplier=0).then_inc(consts, 1)
            nc.gpsimd.iota(below_i[:, :], pattern=[[1, T]], base=0, channel_multiplier=-1).then_inc(consts, 1)
            nc.gpsimd.iota(token_i[:, :, :], pattern=[[T, NT], [0, TOP]], base=0, channel_multiplier=1).then_inc(consts, 1)
            pool.wait_ge(rows_ready, 1)
            pool.wait_ge(blank_out, 16)
            for t in range(NT):
                for k in range(TOP):
                    n = t * TOP + k
                    pool.indirect_dma_start(out=scr["lists"], out_offset=bass.IndirectOffsetOnAxis(ap=row_i[:, n:n + 1].bitcast(U32), axis=0),
                                            in_=entry[:, t, k, :], in_offset=None).then_inc(scattered, 16)
            pool.wait_ge(scattered, 16 * NT * TOP)
            pool.dma_start(lists[:, :, :], scr["lists"].rearrange("(s r) w -> s r w", r=P)).then_inc(lists_in, 16)

        @block.scalar
        def _(act):
            carrier = Carrier(nc, scr, act, "scalar")
            act.wait_ge(exp_in, 1)
            nc.scalar.activation(ez[:, :, :], sc[:, :, :], ACT.Exp).then_inc(exp_done, 1)
            act.wait_ge(gu_in[0], 16)
            for c in range(C):
                split(nc, act, None, gu_raw[:, c, :], gu_hi[:, c, :], None, gu_in[1], 16, gu_hi_done, None, c)
            for c in range(2):
                split(nc, act, None, d_raw[:, c, :], d_hi[:, c, :], None, d_in, 16, d_hi_done, None, c)

            with act.Fori(0, NT) as t:
                hold(carrier, gu_mm, t + 1)
                nc.scalar.activation(sg[:, :], pgu[:, 0:SHARED], ACT.Silu).then_inc(sg_done, 1)
                act.wait_ge(aT_mm, t + 1)
                nc.scalar.copy(aT_hi[:, :], paT[:, :]).then_inc(aT_hi_done, 1)

        @block.vector
        def _(dve):
            n = [0]

            def link(ins):
                n[0] += 1
                ins.then_inc(step, 1)
                dve.wait_ge(step, n[0])

            inner = lambda t, shape: t.unsqueeze(len(t.shape)).to_broadcast(shape)
            every = lambda t, shape: t.unsqueeze(1).to_broadcast(shape)
            by_e = [T, NT, EXPERTS]
            logits = scr["logits"]
            link(nc.vector.tensor_reduce(row_max[:, :], logits[:, :, :], AX, ALU.max))
            nc.vector.tensor_tensor(sc[:, :, :], logits[:, :, :], inner(row_max[:, :], by_e), ALU.subtract).then_inc(exp_in, 1)
            dve.wait_ge(consts, 5)
            nc.vector.tensor_scalar(tri[:, :, :], tri_i[:, :, :], 0.0, None, ALU.is_gt)
            nc.vector.tensor_copy(full[:, :, :], full_i[:, :, :])
            nc.vector.tensor_copy(kth[:, :, :], kth_i[:, :, :])
            nc.vector.tensor_scalar(below[:, :], below_i[:, :], 0.0, None, ALU.is_gt)
            nc.vector.memset(all_ones[:, :], 1.0)
            nc.vector.tensor_copy(entry[:, :, :, 0], token_i[:, :, :])
            nc.vector.memset(before[:, 0, :], 0.0)
            dve.wait_ge(exp_done, 1)
            link(nc.vector.tensor_reduce(row_sum[:, :], ez[:, :, :], AX, ALU.add))
            link(nc.vector.reciprocal(row_max[:, :], row_sum[:, :]))
            link(nc.vector.tensor_tensor(ez[:, :, :], ez[:, :, :], inner(row_max[:, :], by_e), ALU.mult))
            dve.wait_ge(prob_in, 16)
            link(nc.vector.tensor_scalar(sc[:, :, :], ez[:, :, :], bias[:, 0:1], None, ALU.add))
            pair = [T, NT, EXPERTS, EXPERTS]
            view = lambda t: t[:, :, :].rearrange("p t (e f) -> p t e f", f=EXPERTS)
            own, other = sc[:, :, :].unsqueeze(3).to_broadcast(pair), sc[:, :, :].unsqueeze(2).to_broadcast(pair)
            nc.vector.tensor_tensor(view(gt), other, own, ALU.is_gt)
            link(nc.vector.tensor_tensor(view(eq), other, own, ALU.is_equal))
            flat_tri = tri[:, :, :].rearrange("p e f -> p (e f)")
            link(nc.vector.tensor_tensor(eq[:, :, :], eq[:, :, :], every(flat_tri, [T, NT, EXPERTS * EXPERTS]), ALU.mult))
            link(nc.vector.tensor_tensor(gt[:, :, :], gt[:, :, :], eq[:, :, :], ALU.add))
            link(nc.vector.tensor_reduce(rank[:, :, :], view(gt), AX, ALU.add))
            nc.vector.tensor_scalar(sel_b[:, :, :], rank[:, :, :], float(TOP), None, ALU.is_lt).then_inc(sel_ready, 1)
            link(nc.vector.tensor_scalar(sel[:, :, :], rank[:, :, :], float(TOP), None, ALU.is_lt))
            link(nc.vector.tensor_tensor(wts[:, :, :], ez[:, :, :], sel[:, :, :], ALU.mult))
            link(nc.vector.tensor_reduce(row_sum[:, :], wts[:, :, :], AX, ALU.add))
            link(nc.vector.tensor_scalar(row_sum[:, :], row_sum[:, :], 1e-20, None, ALU.add))
            link(nc.vector.reciprocal(row_max[:, :], row_sum[:, :]))
            link(nc.vector.tensor_tensor(wts[:, :, :], wts[:, :, :], inner(row_max[:, :], by_e), ALU.mult))
            dve.wait_ge(counted, 1)
            link(nc.vector.tensor_copy(within[:, :, :], pcount[:, :, :]))
            for t in range(NT):
                link(nc.vector.tensor_tensor(before[:, t + 1, :], before[:, t, :], within[:, 1, t * EXPERTS:(t + 1) * EXPERTS], ALU.add))
            link(nc.vector.tensor_tensor(over[:, :, :], inner(before[:, NT, :], [T, EXPERTS, NT]), full[:, :, :], ALU.is_gt))
            link(nc.vector.tensor_reduce(tiles[:, 0:EXPERTS], over[:, :, :], AX, ALU.add))
            link(nc.vector.tensor_scalar(tiles[:, 0:EXPERTS], tiles[:, 0:EXPERTS], 2.0, None, ALU.max))
            link(nc.vector.tensor_tensor(span[:, :, :], every(tiles[:, 0:EXPERTS], [T, EXPERTS, EXPERTS]), tri[:, :, :], ALU.mult))
            link(nc.vector.tensor_reduce(base[:, :], span[:, :, :], AX, ALU.add))
            link(nc.vector.tensor_tensor(tiles[:, EXPERTS:EXPERTS + 1], base[:, EXPERTS - 1:EXPERTS], tiles[:, EXPERTS - 1:EXPERTS], ALU.add))
            nc.vector.tensor_scalar(scr["tiles"][:, :], tiles[0:1, :], -1.0, None, ALU.add)
            link(nc.vector.tensor_scalar(base[:, :], base[:, :], float(P), None, ALU.mult))
            link(nc.vector.tensor_tensor(pos[:, :, :], before[:, 0:NT, :], within[:, 0, :].rearrange("p (t e) -> p t e", e=EXPERTS), ALU.add))
            link(nc.vector.tensor_tensor(pos[:, :, :], pos[:, :, :], every(base[:, :], by_e), ALU.add))
            four = [T, NT, TOP, EXPERTS]
            kview = lambda t: t[:, :, :].rearrange("p t (k e) -> p t k e", e=EXPERTS)
            over_k = lambda t: t[:, :, :].unsqueeze(2).to_broadcast(four)
            link(nc.vector.tensor_tensor(kview(is_kth), over_k(rank), kth[:, :, :].unsqueeze(1).to_broadcast(four), ALU.is_equal))
            link(nc.vector.tensor_tensor(kview(picked), kview(is_kth), over_k(pos), ALU.mult))
            link(nc.vector.tensor_reduce(row_of[:, :, :], kview(picked), AX, ALU.add))
            nc.vector.tensor_copy(row_i[:, :], row_of[:, :, :].rearrange("p t k -> p (t k)"))
            link(nc.vector.tensor_tensor(kview(picked), kview(is_kth), over_k(wts), ALU.mult))
            nc.vector.tensor_reduce(entry[:, :, :, 1], kview(picked), AX, ALU.add).then_inc(rows_ready, 1)

            for c in range(C):
                split(nc, None, dve, gu_raw[:, c, :], gu_hi[:, c, :], gu_lo[:, c, :], None, 0, gu_hi_done, gu_lo_done, c)
            for c in range(2):
                split(nc, None, dve, d_raw[:, c, :], d_hi[:, c, :], d_lo[:, c, :], None, 0, d_hi_done, d_lo_done, c)

            def activate(t):
                dve.wait_ge(sg_done, t + 1)
                nc.vector.tensor_tensor(a[:, :], sg[:, :], pgu[:, SHARED:G], ALU.mult).then_inc(a_done, 1)

            def add_down(t, b):
                dve.wait_ge(x1_in[b], 8 * (t - b) + 16)
                for h in range(2):
                    at = slice(h * HALF, (h + 1) * HALF)
                    dve.wait_ge(y_mm, 2 * t + h + 1)
                    nc.vector.tensor_tensor(y[:, b, at], y[:, b, at], py[h][:, :], ALU.add).then_inc(y_done, 1)

            def low(t):
                dve.wait_ge(aT_hi_done, t + 1)
                nc.vector.tensor_tensor(aT_lo[:, :], paT[:, :], aT_hi[:, :].bitcast(F32), ALU.subtract).then_inc(aT_lo_done, 1)

            activate(0)
            low(0)
            activate(1)
            add_down(0, 0)
            low(1)
            with dve.Fori(1, NT // 2) as i:
                for b in range(2):
                    activate(2 * i + b)
                    add_down(2 * i + b - 1, 1 - b)
                    low(2 * i + b)
            add_down(NT - 1, 1)
            dve.wait_ge(lists_T, 2)
            nc.vector.tensor_copy(scr["to_rows"][:, :], plist[:, 0, :])
            nc.vector.tensor_scalar(scr["from_rows"][:, :], plist[:, 0, :], float(N - 1), None, ALU.min)
            nc.vector.tensor_copy(scr["row_weights"][:, :], plist[:, 1, :]).then_inc(lists_done, 1)
            dve.wait_ge(lists_done, 1)

        @block.tensor
        def _(pe):
            pe.wait_ge(sel_ready, 1)
            flat = sel_b[:, :, :].rearrange("p t e -> p (t e)")
            pe.matmul(pcount[:, 0, :], below[:, :], flat, start=True, stop=True)
            pe.matmul(pcount[:, 1, :], all_ones[:, :], flat, start=True, stop=True).then_inc(counted, 1)

            def gate_up(t, b, first=False):
                pe.wait_ge(nT_in[b], 16 * (t - b) + 32)
                for c in range(C):
                    if first:
                        pe.wait_ge(gu_lo_done, c + 1)
                    at = slice(c * T, (c + 1) * T)
                    m = mm3(pe, pgu[:, :], nT_hi[:, b, at], nT_lo[:, b, at], gu_hi[:, c, :], gu_lo[:, c, :], c == 0, c == C - 1)
                m.then_inc(gu_mm, 1)

            def down(t, first=False):
                if first:
                    pe.wait_ge(d_lo_done, 2)
                pe.wait_ge(aT_lo_done, t + 1)
                for h in range(2):
                    col = slice(h * HALF, (h + 1) * HALF)
                    if not first:
                        pe.wait_ge(y_done, 2 * t - 1 + h)
                    for c in range(2):
                        at = slice(c * T, (c + 1) * T)
                        m = mm3(pe, py[h][:, :], aT_hi[:, at], aT_lo[:, at], d_hi[:, c, col], d_lo[:, c, col], c == 0, c == 1)
                    m.then_inc(y_mm, 1)

            def turn(t):
                pe.wait_ge(a_done, t + 1)
                for c in range(2):
                    m = pe.transpose(paT[:, c * T:(c + 1) * T], a[:, c * P:(c + 1) * P], scr["ident"][0:T, 0:T])
                m.then_inc(aT_mm, 1)

            gate_up(0, 0, first=True)
            turn(0)
            gate_up(1, 1)
            down(0, first=True)
            turn(1)
            with pe.Fori(1, NT // 2) as i:
                for b in range(2):
                    gate_up(2 * i + b, b)
                    down(2 * i + b - 1)
                    turn(2 * i + b)
            down(NT - 1)
            pe.wait_ge(lists_in, 16)
            for w in range(2):
                pe.transpose(plist[:, w, :], lists[:, :, w], scr["ident"][0:SLOTS, 0:SLOTS]).then_inc(lists_T, 1)


def experts(nc, io, scr, out):
    with Phase(nc) as ctx:
        sb = lambda n, s, d=F32: ctx.enter_context(nc.sbuf_tensor(n, s, d))
        ps = lambda n, s: ctx.enter_context(nc.psum_tensor(n, s, F32))
        sem = ctx.sem
        I4 = MOE // P
        gu_raw, d_raw, raw_in = scr["gu_raw"], scr["d_raw"], scr["raw_in"]
        gu_hi, gu_lo = sb("p7_gu_hi", [P, C, 2 * MOE], F32R), sb("p7_gu_lo", [P, C, 2 * MOE], F32R)
        d_hi, d_lo = sb("p7_d_hi", [P, I4, D], F32R), sb("p7_d_lo", [P, I4, D], F32R)
        x, y = sb("p7_x", [P, D]), sb("p7_y", [P, D])
        xT_hi, xT_lo = sb("p7_xT_hi", [P, D], F32R), sb("p7_xT_lo", [P, D], F32R)
        sg, a = sb("p7_sg", [P, MOE]), sb("p7_a", [P, MOE])
        aT_hi, aT_lo = sb("p7_aT_hi", [P, MOE], F32R), sb("p7_aT_lo", [P, MOE], F32R)
        from_cell, to_cell = sb("p7_from", [P, 1], I32), sb("p7_to", [P, 1], I32)
        pg, pu, paT = ps("p7_g", [P, MOE]), ps("p7_u", [P, MOE]), ps("p7_aT", [P, MOE])
        pxT, py = [ps(f"p7_xT{h}", [P, HALF]) for h in range(2)], [ps(f"p7_y{h}", [P, HALF]) for h in range(2)]
        gu_hi_done, gu_lo_done, d_hi_done, d_lo_done = sem("p7_gu_hi_done"), sem("p7_gu_lo_done"), sem("p7_d_hi_done"), sem("p7_d_lo_done")
        x_in, xT_mm, xT_hi_done, xT_lo_done = sem("p7_x_in"), sem("p7_xT_mm"), sem("p7_xT_hi_done"), sem("p7_xT_lo_done")
        gu_mm, sg_done, a_done = sem("p7_gu_mm"), sem("p7_sg_done"), sem("p7_a_done")
        aT_mm, aT_hi_done, aT_lo_done = sem("p7_aT_mm"), sem("p7_aT_hi_done"), sem("p7_aT_lo_done")
        y_mm, y_act, y_dve, y_out, y_free = sem("p7_y_mm"), sem("p7_y_act"), sem("p7_y_dve"), sem("p7_y_out"), sem("p7_y_free")
        from_set, to_set = sem("p7_from_set"), sem("p7_to_set")
        block = ctx.block()

        def by_expert(eng, first_tile, tile, last):
            with eng.register("p7_done") as done:
                eng.reg_mov(done, 0)

                def one(e, more):
                    others = eng.value_load(scr["tiles"][0:1, bass.ds(e, 1)], min_val=1, max_val=NT - 1)
                    start = eng.snap(done)
                    first_tile(e, start)
                    with eng.Fori(0, others) as t:
                        tile(e, eng.snap(start + t), eng.snap(start + t + 1))
                    last(e, eng.snap(start + others), more)
                    eng.reg_add(done, done, others)
                    eng.reg_add(done, done, 1)
                with eng.Fori(0, EXPERTS - 1) as e:
                    one(e, True)
                one(EXPERTS - 1, False)

        @block.sync
        def _(sp):
            with sp.Fori(0, EXPERTS - 1) as e:
                for k, (raw, src) in enumerate(scr["expert_pieces"](e + 1)):
                    if k < C:
                        sp.wait_ge(gu_lo_done, C * e + k + 1)
                    else:
                        sp.wait_ge(d_lo_done, I4 * e + k - C + 1)
                    sp.dma_start(raw, src).then_inc(raw_in[k], 16)

        @block.gpsimd
        def _(pool):
            others = pool.value_load(scr["tiles"][0:1, EXPERTS:EXPERTS + 1], min_val=2 * EXPERTS - 1, max_val=SLOTS - 4)
            for s in (y_act, y_dve, y_free):
                pool.sem_inc(s, 1)

            carrier = Carrier(nc, scr, pool, "gpsimd")

            def gather(g, first=False):
                if not first:
                    pool.wait_ge(x_in, 16 * g)
                    hold(carrier, xT_mm, 2 * g)
                nc.gpsimd.tensor_copy(from_cell[:, :], scr["from_rows"][:, bass.ds(g, 1)]).then_inc(from_set, 1)
                hold(carrier, from_set, g + 1)
                pool.indirect_dma_start(out=x[:, :], out_offset=None, in_=scr["xn2"],
                                        in_offset=bass.IndirectOffsetOnAxis(ap=from_cell[:, 0:1].bitcast(U32), axis=0)).then_inc(x_in, 16)

            def scatter(g):
                pool.wait_ge(y_act, g + 2)
                hold(carrier, y_dve, g + 2)
                nc.gpsimd.tensor_copy(to_cell[:, :], scr["to_rows"][:, bass.ds(g, 1)]).then_inc(to_set, 1)
                hold(carrier, to_set, g + 1)
                pool.indirect_dma_start(out=out, out_offset=bass.IndirectOffsetOnAxis(ap=to_cell[:, 0:1].bitcast(U32), axis=0),
                                        in_=y[:, :], in_offset=None, bounds_check=N - 1, oob_is_err=False, compute_op=ALU.add).then_inc(y_out, 16)
                hold(carrier, y_out, 16 * g + 16).then_inc(y_free, 1)

            gather(0, True)
            gather(1)
            gather(2)
            with pool.Fori(0, others) as g:
                gather(pool.snap(g + 3))
                scatter(g)
            scatter(others)

        @block.scalar
        def _(act):
            carrier = Carrier(nc, scr, act, "scalar")

            def split_gu(e):
                for c in range(C):
                    act.wait_ge(raw_in[c], 16 * e + 16)
                    nc.scalar.copy(gu_hi[:, c, :], gu_raw[:, c, :]).then_inc(gu_hi_done, 1)

            def split_d(e):
                for c in range(I4):
                    act.wait_ge(raw_in[C + c], 16 * e + 16)
                    nc.scalar.copy(d_hi[:, c, :], d_raw[:, c, :]).then_inc(d_hi_done, 1)

            def x_high(g):
                for h in range(2):
                    act.wait_ge(xT_mm, 2 * g + h + 1)
                    nc.scalar.copy(xT_hi[:, h * HALF:(h + 1) * HALF], pxT[h][:, :]).then_inc(xT_hi_done, 1)

            def silu(g):
                hold(carrier, gu_mm, 2 * g + 1)
                nc.scalar.activation(sg[:, :], pg[:, :], ACT.Silu).then_inc(sg_done, 1)

            def weigh(g):
                act.wait_ge(y_free, g + 1)
                hold(carrier, y_mm, 2 * g + 1)
                nc.scalar.activation(y[:, 0:HALF], py[0][:, :], ACT.Copy, scale=scr["row_weights"][:, bass.ds(g, 1)]).then_inc(y_act, 1)

            def a_high(g):
                act.wait_ge(aT_mm, g + 1)
                nc.scalar.copy(aT_hi[:, :], paT[:, :]).then_inc(aT_hi_done, 1)

            def first_tile(e, g):
                silu(g)
                x_high(g + 1)
                a_high(g)

            def tile(e, before, g):
                silu(g)
                x_high(g + 1)
                weigh(before)
                a_high(g)

            def last(e, g, more):
                if more:
                    split_gu(e + 1)
                weigh(g)
                if more:
                    act.wait_ge(y_mm, 2 * g + 2)
                    split_d(e + 1)

            x_high(0)
            split_gu(0)
            split_d(0)
            by_expert(act, first_tile, tile, last)

        @block.vector
        def _(dve):
            def split_gu(e):
                for c in range(C):
                    dve.wait_ge(gu_hi_done, C * e + c + 1)
                    nc.vector.tensor_tensor(gu_lo[:, c, :], gu_raw[:, c, :], gu_hi[:, c, :].bitcast(F32), ALU.subtract).then_inc(gu_lo_done, 1)

            def split_d(e):
                for c in range(I4):
                    dve.wait_ge(d_hi_done, I4 * e + c + 1)
                    nc.vector.tensor_tensor(d_lo[:, c, :], d_raw[:, c, :], d_hi[:, c, :].bitcast(F32), ALU.subtract).then_inc(d_lo_done, 1)

            def x_low(g):
                for h in range(2):
                    dve.wait_ge(xT_hi_done, 2 * g + h + 1)
                    at = slice(h * HALF, (h + 1) * HALF)
                    nc.vector.tensor_tensor(xT_lo[:, at], pxT[h][:, :], xT_hi[:, at].bitcast(F32), ALU.subtract).then_inc(xT_lo_done, 1)

            def multiply(g):
                dve.wait_ge(sg_done, g + 1)
                dve.wait_ge(gu_mm, 2 * g + 2)
                nc.vector.tensor_tensor(a[:, :], sg[:, :], pu[:, :], ALU.mult).then_inc(a_done, 1)

            def weigh(g):
                dve.wait_ge(y_free, g + 1)
                dve.wait_ge(y_mm, 2 * g + 2)
                nc.vector.tensor_scalar(y[:, HALF:D], py[1][:, :], scr["row_weights"][:, bass.ds(g, 1)], None, ALU.mult).then_inc(y_dve, 1)

            def a_low(g):
                dve.wait_ge(aT_hi_done, g + 1)
                nc.vector.tensor_tensor(aT_lo[:, :], paT[:, :], aT_hi[:, :].bitcast(F32), ALU.subtract).then_inc(aT_lo_done, 1)

            def first_tile(e, g):
                multiply(g)
                x_low(g + 1)
                a_low(g)

            def tile(e, before, g):
                multiply(g)
                x_low(g + 1)
                weigh(before)
                a_low(g)

            def last(e, g, more):
                if more:
                    split_gu(e + 1)
                weigh(g)
                if more:
                    split_d(e + 1)

            x_low(0)
            split_gu(0)
            split_d(0)
            by_expert(dve, first_tile, tile, last)

        @block.tensor
        def _(pe):
            def turn_x(g):
                pe.wait_ge(x_in, 16 * g + 16)
                for c in range(C):
                    m = pe.transpose(pxT[c // 4][:, (c % 4) * P:(c % 4 + 1) * P], x[:, c * P:(c + 1) * P], scr["ident"][:, :])
                    if c % 4 == 3:
                        m.then_inc(xT_mm, 1)

            def gate_up(e, g, first):
                pe.wait_ge(xT_lo_done, 2 * g + 2)
                for k, acc in enumerate((pg, pu)):
                    for c in range(C):
                        if first and k == 0:
                            pe.wait_ge(gu_lo_done, C * e + c + 1)
                        at, col = slice(c * P, (c + 1) * P), slice(k * MOE, (k + 1) * MOE)
                        m = mm3(pe, acc[:, :], xT_hi[:, at], xT_lo[:, at], gu_hi[:, c, col], gu_lo[:, c, col], c == 0, c == C - 1)
                    m.then_inc(gu_mm, 1)

            def down(e, g):
                pe.wait_ge(aT_lo_done, g + 1)
                pe.wait_ge(y_act, g + 1)
                pe.wait_ge(y_dve, g + 1)
                pe.wait_ge(d_lo_done, I4 * e + I4)
                for h in range(2):
                    col = slice(h * HALF, (h + 1) * HALF)
                    for c in range(I4):
                        at = slice(c * P, (c + 1) * P)
                        m = mm3(pe, py[h][:, :], aT_hi[:, at], aT_lo[:, at], d_hi[:, c, col], d_lo[:, c, col], c == 0, c == I4 - 1)
                    m.then_inc(y_mm, 1)

            def turn_a(g):
                pe.wait_ge(a_done, g + 1)
                for c in range(I4):
                    m = pe.transpose(paT[:, c * P:(c + 1) * P], a[:, c * P:(c + 1) * P], scr["ident"][:, :])
                m.then_inc(aT_mm, 1)

            def first_tile(e, g):
                gate_up(e, g, True)
                turn_x(g + 1)
                turn_a(g)

            def tile(e, before, g):
                gate_up(e, g, False)
                turn_x(g + 1)
                down(e, before)
                turn_a(g)

            def last(e, g, more):
                down(e, g)

            turn_x(0)
            by_expert(pe, first_tile, tile, last)


def program(nc, io, out):
    with ExitStack() as ctx:
        sem = lambda n: ctx.enter_context(nc.semaphore(n))
        scr = {}
        for name in ("xT_hi", "xT_lo"):
            scr[name] = nc.dram_tensor(name, (NT, P, C * T), F32).ap()
        for name in ("M_hi", "M_lo"):
            scr[name] = nc.dram_tensor(name, (C, P, D), F32).ap()
        for name in ("AT_hi", "AT_lo"):
            scr[name] = nc.dram_tensor(name, (NT, T, NT, T), F32).ap()
        scr["zero"] = ctx.enter_context(nc.sbuf_tensor("zero", [P, P], BF16))
        scr["ident"] = ctx.enter_context(nc.sbuf_tensor("ident", [P, P], F32))
        scr["spare"] = ctx.enter_context(nc.sbuf_tensor("spare", [1, 64], F32))
        scr["spare_used"] = 0
        scr["go"] = sem("go")
        ident_zero = sem("ident_zero")
        with nc.Block() as block:
            @block.gpsimd
            def _(pool):
                nc.gpsimd.memset(scr["spare"][:, :], 0.0)
                nc.gpsimd.memset(scr["zero"][:, :], 0.0)
                nc.gpsimd.memset(scr["ident"][:, :], 0.0).then_inc(ident_zero, 1)
                pool.wait_ge(ident_zero, 1)
                nc.gpsimd.affine_select(out=scr["ident"][:, :], in_=scr["ident"][:, :], compare_op=ALU.not_equal, fill=1.0,
                                        base=0, pattern=[[-1, P]], channel_multiplier=1).then_inc(scr["go"], 1)
        scr["x1"] = nc.dram_tensor("x1", (NT, T, D), F32).ap()
        scr["xn2"] = nc.dram_tensor("xn2", (N, D), F32).ap()
        for name in ("nT_hi", "nT_lo"):
            scr[name] = nc.dram_tensor(name, (NT, P, C * T), F32).ap()
        scr["wide"] = ctx.enter_context(nc.sbuf_tensor("wide", [1, 1], I32))
        scr["dinv"] = ctx.enter_context(nc.sbuf_tensor("dinv", [T, NT], F32))
        scr["logits"] = ctx.enter_context(nc.sbuf_tensor("logits", [T, NT, EXPERTS], F32))
        with ExitStack() as kv_scope:
            scr["kvT"] = kv_scope.enter_context(nc.sbuf_tensor("kvT", [P, D], F32))
            project_kv(nc, io, scr)
            mixing_and_adjacency(nc, io, scr)
        with ExitStack() as hs_scope:
            scr["hs_hi"] = hs_scope.enter_context(nc.sbuf_tensor("hs_hi", [T, NT, D], F32R))
            scr["hs_lo"] = hs_scope.enter_context(nc.sbuf_tensor("hs_lo", [T, NT, D], F32R))
            node_features(nc, io, scr)
            aggregate_and_mix(nc, io, scr)
        scr["lists"] = nc.dram_tensor("lists", (SLOTS * P, 2), F32).ap()
        scr["tiles"] = ctx.enter_context(nc.sbuf_tensor("tiles", [1, EXPERTS + 1], I32))
        scr["to_rows"] = ctx.enter_context(nc.sbuf_tensor("to_rows", [P, SLOTS], I32))
        scr["from_rows"] = ctx.enter_context(nc.sbuf_tensor("from_rows", [P, SLOTS], I32))
        scr["row_weights"] = ctx.enter_context(nc.sbuf_tensor("row_weights", [P, SLOTS], F32))
        gu_raw = scr["gu_raw"] = ctx.enter_context(nc.sbuf_tensor("gu_raw", [P, C, 2 * MOE], F32))
        d_raw = scr["d_raw"] = ctx.enter_context(nc.sbuf_tensor("d_raw", [P, MOE // P, D], F32))
        scr["raw_in"] = [sem(f"raw_in{k}") for k in range(C + MOE // P)]
        downs = io["down"].rearrange("e (c p) n -> e c p n", p=P)

        def expert_pieces(e):
            pick = lambda t, c: t[bass.ds(e, 1), c, :, :].rearrange("o p n -> (o p) n")
            out_ = [(gu_raw[:, c, :], pick(io["gate_up"].rearrange("e (c p) n -> e c p n", p=P), c)) for c in range(C)]
            return out_ + [(d_raw[:, c, :], pick(downs, c)) for c in range(MOE // P)]
        scr["expert_pieces"] = expert_pieces
        shared_and_routing(nc, io, scr, out)
        experts(nc, io, scr, out)


def kernel(**a):
    import numpy as np
    import concourse.bacc as bacc
    from concourse.bass_utils import run_bass_kernel_spmd as run

    lay = {k: np.asarray(v) for k, v in a.items()}
    arrays = {
        "x": lay["x"], "src": lay["src"].reshape(160, 125).T, "dst": lay["dst"].reshape(160, 125).T,
        "wgT": lay["L0_gnn_W"].T, "gb": lay["L0_gnn_b"].reshape(1, D),
        "wkT": lay["L0_mix_W_k"].T, "wvT": lay["L0_mix_W_v"].T, "wq": lay["L0_mix_W_q"], "woT": lay["L0_mix_W_o"].T,
        "router": lay["L0_ffn_router_w"], "router_b": lay["L0_ffn_router_bias"].reshape(1, 1),
        "gate_up": np.concatenate([lay["L0_ffn_gate_w"], lay["L0_ffn_up_w"]], axis=2), "down": lay["L0_ffn_down_w"],
        "s_gate": lay["L0_ffn_s_gate_w"], "s_up": lay["L0_ffn_s_up_w"], "s_down": lay["L0_ffn_s_down_w"],
    }
    nc = bacc.Bacc("TRN2", target_bir_lowering=False, num_devices=1)
    arrays = {f"in_{k}": np.ascontiguousarray(v) for k, v in arrays.items()}
    io = {k[3:]: nc.dram_tensor(k, v.shape, mybir.dt.from_np(v.dtype), kind="ExternalInput").ap() for k, v in arrays.items()}
    out = nc.dram_tensor("out_x", (N, D), F32, kind="ExternalOutput").ap()
    program(nc, io, out)
    r = run(nc, [arrays], core_ids=[0])
    return r.results[0]["out_x"]
```

```python
import concourse.bass as bass
from concourse import mybir
from contextlib import ExitStack

F32 = mybir.dt.float32
F32R = mybir.dt.float32r
BF16 = mybir.dt.bfloat16
F16 = mybir.dt.float16
I32 = mybir.dt.int32
U32 = mybir.dt.uint32
ALU = mybir.AluOpType
ACT = mybir.ActivationFunctionType
AX = mybir.AxisListType.X

N = 1250
D = 1024
P = 128
T = 125
NT = N // T
C = D // P
HALF = 512
EPS = 1e-5


class Phase(ExitStack):
    def __init__(self, nc):
        super().__init__()
        self.nc, self.sems = nc, []

    def sem(self, name):
        self.sems.append(self.nc.alloc_semaphore(name))
        return self.sems[-1]

    def block(self):
        self.opened = self.nc.Block()
        return self.opened.__enter__()

    def __exit__(self, *error):
        self.opened.__exit__(*error)
        if error[0] is None:
            self.clear()
        return super().__exit__(*error)

    def clear(self):
        with self.nc.Block() as block:
            @block.gpsimd
            def _(pool):
                for s in self.sems:
                    pool.sem_clear(s)
        for s in self.sems:
            self.nc.release_semaphore(s)


def hold(carrier, sem, value):
    carrier.eng.wait_ge(sem, value)
    if not isinstance(value, int):
        return carrier.issue()


class Carrier:
    def __init__(self, nc, scr, eng, on):
        self.nc, self.scr, self.eng, self.on = nc, scr, eng, on

    def issue(self):
        self.scr["spare_used"] += 1
        assert self.scr["spare_used"] < self.scr["spare"].shape[1]
        at = self.scr["spare"][0:1, self.scr["spare_used"]:self.scr["spare_used"] + 1]
        zero = self.scr["spare"][0:1, 0:1]
        if self.on == "scalar":
            return self.nc.scalar.copy(at, zero)
        if self.on == "gpsimd":
            return self.nc.gpsimd.tensor_tensor(at, zero, zero, ALU.add)
        return self.nc.vector.memset(at, 0.0)


def layernorm(nc, carrier, src, dst, stats, mv, small, step, base, var_ready, std_ready, normed, t):
    dve = carrier.eng
    for h in range(2):
        i = nc.vector.bn_stats(stats[:, h, :], src[:, h * HALF:(h + 1) * HALF])
    i.then_inc(step, 1)
    hold(carrier, step, base + 1)
    nc.vector.bn_aggr(mv[:, :], stats[:, :, :]).then_inc(step, 1)
    dve.wait_ge(step, base + 2)
    nc.vector.tensor_scalar_add(small[:, 0:1], mv[:, 1:2], EPS).then_inc(var_ready, 1)
    dve.wait_ge(std_ready, t + 1)
    inverse_root(nc, dve, small, step, base + 2)
    dve.wait_ge(step, base + 6)
    nc.vector.tensor_scalar(dst, src, mv[:, 0:1], small[:, 6:7], ALU.subtract, ALU.mult).then_inc(normed, 1)
    dve.wait_ge(normed, t + 1)
    nc.vector.memset(small[:, 7:8], 0.0).then_inc(step, 1)


def inverse_root(nc, dve, small, step, base):
    nc.vector.reciprocal(small[:, 2:3], small[:, 1:2]).then_inc(step, 1)
    dve.wait_ge(step, base + 1)
    nc.vector.scalar_tensor_tensor(small[:, 3:4], small[:, 2:3], small[:, 2:3], small[:, 0:1], ALU.mult, ALU.mult).then_inc(step, 1)
    dve.wait_ge(step, base + 2)
    nc.vector.tensor_scalar(small[:, 5:6], small[:, 3:4], -0.5, 1.5, ALU.mult, ALU.add).then_inc(step, 1)
    dve.wait_ge(step, base + 3)
    nc.vector.tensor_tensor(small[:, 6:7], small[:, 5:6], small[:, 2:3], ALU.mult).then_inc(step, 1)


def mm3(pe, out, lhs_hi, lhs_lo, rhs_hi, rhs_lo, start, stop):
    pe.matmul(out, lhs_lo, rhs_hi, start=start, stop=False)
    pe.matmul(out, lhs_hi, rhs_lo, start=False, stop=False)
    return pe.matmul(out, lhs_hi, rhs_hi, start=False, stop=stop)


def before_split(nc, name, lo):
    return nc.alloc_sbuf_tensor_at(name, list(lo.shape), F32, offset=nc.lookup_mloc(lo).addr)


def split(nc, act, dve, raw, hi, lo, raw_in, raw_value, hi_done, lo_done, n):
    if act is not None:
        act.wait_ge(raw_in, raw_value)
        nc.scalar.copy(hi, raw).then_inc(hi_done, 1)
    if dve is not None:
        dve.wait_ge(hi_done, n + 1)
        nc.vector.tensor_tensor(lo, raw, hi.bitcast(F32), ALU.subtract).then_inc(lo_done, 1)


def project_kv(nc, io, scr):
    with Phase(nc) as ctx:
        sb = lambda n, s, d: ctx.enter_context(nc.sbuf_tensor(n, s, d))
        ps = lambda n, s: ctx.enter_context(nc.psum_tensor(n, s, F32))
        sem = ctx.sem
        w_hi = sb("p1_w_hi", [P, 2, C, D], F32R)
        w_lo = sb("p1_w_lo", [P, 2, C, D], F32R)
        w_raw = before_split(nc, "p1_w_raw", w_lo)
        x = sb("p1_x", [T, 2, D], F32)
        xT_hi = sb("p1_xT_hi", [P, 2, C * T], F32R)
        xT_lo = sb("p1_xT_lo", [P, 2, C * T], F32R)
        kv_hi = sb("p1_kv_hi", [T, 4 * HALF], F32R)
        kv_lo = sb("p1_kv_lo", [T, 4 * HALF], F32R)
        stats = sb("p1_stats", [T, 2, 6], F32)
        mv = sb("p1_mv", [T, 2], F32)
        small = sb("p1_small", [T, 8], F32)
        kvT = scr["kvT"]
        ident = scr["ident"]
        xp = [ps(f"p1_xp{i}", [P, 4 * T]) for i in range(2)]
        pkv = [ps(f"p1_kv{i}", [T, HALF]) for i in range(4)]
        pT = [ps(f"p1_kvT{i}", [P, HALF]) for i in range(2)]

        w_in = [sem(f"p1_w_in{n}") for n in range(2 * C)]
        w_hi_done, w_lo_done = sem("p1_w_hi_done"), sem("p1_w_lo_done")
        x_in = [sem(f"p1_x_in{i}") for i in range(2)]
        var_ready, std_ready, ln_step = sem("p1_var"), sem("p1_std"), sem("p1_ln_step")
        xn_ready, xT_mm, xT_hi_done, xT_lo_done = sem("p1_xn"), sem("p1_xT_mm"), sem("p1_xT_hi_done"), sem("p1_xT_lo_done")
        xT_out = [sem(f"p1_xT_out{i}") for i in range(2)]
        kv_mm, kv_hi_done, kv_lo_done = sem("p1_kv_mm"), sem("p1_kv_hi_done"), sem("p1_kv_lo_done")
        kvT_mm, kvT_added = sem("p1_kvT_mm"), sem("p1_kvT_added")

        x_dram = io["x"].rearrange("(t p) d -> t p d", p=T)
        w_dram = [io["wkT"].rearrange("(c p) n -> c p n", p=P), io["wvT"].rearrange("(c p) n -> c p n", p=P)]
        block = ctx.block()

        @block.sync
        def _(sp):
            def load_x(t, b, k):
                if k:
                    sp.wait_ge(xT_mm, 2 * (t - 1))
                sp.dma_start(x[:, b, :], x_dram[bass.ds(t, 1), :, :].rearrange("a p d -> (a p) d") if k else x_dram[t, :, :]).then_inc(x_in[b], 16)
            load_x(0, 0, False)
            for n in range(2 * C):
                sp.dma_start(w_raw[:, n // C, n % C, :], w_dram[n // C][n % C]).then_inc(w_in[n], 16)
                if n == C - 1:
                    load_x(1, 1, False)

            def store_xT(t, b):
                sp.wait_ge(xT_hi_done, 2 * t + 2)
                sp.wait_ge(xT_lo_done, 2 * t + 2)
                sp.dma_start(scr["xT_hi"][bass.ds(t, 1), :, :].rearrange("a p d -> (a p) d"), xT_hi[:, b, :].bitcast(F32)).then_inc(xT_out[b], 16)
                sp.dma_start(scr["xT_lo"][bass.ds(t, 1), :, :].rearrange("a p d -> (a p) d"), xT_lo[:, b, :].bitcast(F32)).then_inc(xT_out[b], 16)
            with sp.Fori(0, NT // 2 - 1) as i:
                for b in range(2):
                    load_x(2 * i + 2 + b, b, True)
                    store_xT(2 * i + b, b)
            for b in range(2):
                store_xT(NT - 2 + b, b)
            for b in range(2):
                sp.wait_ge(xT_out[b], 32 * (NT // 2))

        def xT_halves(act, t, b, guard):
            if guard:
                act.wait_ge(kv_mm, 4 * t - 4)
                act.wait_ge(xT_out[b], 16 * (t - b))
            for h in range(2):
                act.wait_ge(xT_mm, 2 * t + h + 1)
                nc.scalar.copy(xT_hi[:, b, h * 4 * T:(h + 1) * 4 * T], xp[h][:, :]).then_inc(xT_hi_done, 1)

        def kv_half(act, t, q):
            if q == 0:
                act.wait_ge(kvT_mm, t)
            act.wait_ge(kv_mm, 4 * t + q + 1)
            nc.scalar.copy(kv_hi[:, q * HALF:(q + 1) * HALF], pkv[q][:, :]).then_inc(kv_hi_done, 1)

        @block.scalar
        def _(act):
            act_carrier = Carrier(nc, scr, act, "scalar")
            nc.scalar.activation(scr["spare"][0:1, 1:2], scr["spare"][0:1, 0:1], ACT.Sqrt)

            def root(t):
                hold(act_carrier, var_ready, t + 1)
                nc.scalar.activation(small[:, 1:2], small[:, 0:1], ACT.Sqrt).then_inc(std_ready, 1)

            for n in range(2 * C):
                split(nc, act, None, w_raw[:, n // C, n % C, :], w_hi[:, n // C, n % C, :], None, w_in[n], 16, w_hi_done, None, n)
                if n == 0:
                    root(0)
                if n == 2:
                    xT_halves(act, 0, 0, False)
                if n == C + 1:
                    root(1)

            def tile(t, b, first=False, last=False):
                kv_half(act, t, 0)
                if not first and not last:
                    root(t + 1)
                kv_half(act, t, 1)
                kv_half(act, t, 2)
                if not last:
                    xT_halves(act, t + 1, 1 - b, True)
                kv_half(act, t, 3)

            tile(0, 0, first=True)
            tile(1, 1)
            with act.Fori(1, NT // 2 - 1) as i:
                for b in range(2):
                    tile(2 * i + b, b)
            for b in range(2):
                tile(NT - 2 + b, b, last=b == 1)

        @block.vector
        def _(dve):
            dve_carrier = Carrier(nc, scr, dve, "vector")

            def norm(t, b):
                dve.wait_ge(x_in[b], 8 * (t - b) + 16)
                layernorm(nc, dve_carrier, x[:, b, :], x[:, b, :], stats, mv, small, ln_step, 7 * t, var_ready, std_ready, xn_ready, t)

            def xT_low(t, b):
                for h in range(2):
                    dve.wait_ge(xT_hi_done, 2 * t + h + 1)
                    at = slice(h * 4 * T, (h + 1) * 4 * T)
                    nc.vector.tensor_tensor(xT_lo[:, b, at], xp[h][:, :], xT_hi[:, b, at].bitcast(F32), ALU.subtract).then_inc(xT_lo_done, 1)

            def kv_low(t, q):
                dve.wait_ge(kv_hi_done, 4 * t + q + 1)
                at = slice(q * HALF, (q + 1) * HALF)
                nc.vector.tensor_tensor(kv_lo[:, at], pkv[q][:, :], kv_hi[:, at].bitcast(F32), ALU.subtract).then_inc(kv_lo_done, 1)

            def add_kvT(t):
                for h in range(2):
                    dve.wait_ge(kvT_mm, t + 1)
                    dve.wait_ge(kvT_added, 2 * t + h + 1)
                    at = slice(h * HALF, (h + 1) * HALF)
                    nc.vector.tensor_tensor(kvT[:, at], kvT[:, at], pT[h][:, :], ALU.add).then_inc(kvT_added, 1)

            def tile(t, b, first=False, last=False):
                if not first:
                    add_kvT(t - 1)
                kv_low(t, 0)
                if not first and not last:
                    norm(t + 1, 1 - b)
                kv_low(t, 1)
                kv_low(t, 2)
                if not last:
                    xT_low(t + 1, 1 - b)
                kv_low(t, 3)

            for h in range(2):
                nc.vector.memset(kvT[:, h * HALF:(h + 1) * HALF], 0.0).then_inc(kvT_added, 1)
            norm(0, 0)
            for n in range(2 * C):
                split(nc, None, dve, w_raw[:, n // C, n % C, :], w_hi[:, n // C, n % C, :], w_lo[:, n // C, n % C, :], None, 0, w_hi_done, w_lo_done, n)
                if n == 2:
                    xT_low(0, 0)
                if n == C + 1:
                    norm(1, 1)
            tile(0, 0, first=True)
            tile(1, 1)
            with dve.Fori(1, NT // 2 - 1) as i:
                for b in range(2):
                    tile(2 * i + b, b)
            for b in range(2):
                tile(NT - 2 + b, b, last=b == 1)
            add_kvT(NT - 1)

        @block.tensor
        def _(pe):
            def transposes(t, b):
                pe.wait_ge(xn_ready, t + 1)
                pe.wait_ge(xT_lo_done, 2 * t)
                for c in range(C):
                    i = pe.transpose(xp[c // 4][:, (c % 4) * T:(c % 4 + 1) * T], x[:, b, c * P:(c + 1) * P], ident[0:T, 0:T])
                    if c % 4 == 3:
                        i.then_inc(xT_mm, 1)

            def project(t, b, q, first):
                pe.wait_ge(xT_lo_done, 2 * t + 2)
                if not first:
                    pe.wait_ge(kv_lo_done, 4 * t - 3 + q)
                for c in range(C):
                    if first and t == 0:
                        pe.wait_ge(w_lo_done, (q // 2) * C + c + 1)
                    at = slice(c * T, (c + 1) * T)
                    col = slice((q % 2) * HALF, (q % 2 + 1) * HALF)
                    i = mm3(pe, pkv[q][:, :], xT_hi[:, b, at], xT_lo[:, b, at],
                            w_hi[:, q // 2, c, col], w_lo[:, q // 2, c, col], c == 0, c == C - 1)
                i.then_inc(kv_mm, 1)

            def products(t):
                pe.wait_ge(kv_lo_done, 4 * t + 4)
                pe.wait_ge(kvT_added, 2 * t + 2)
                for j in range(C):
                    k, v = slice(j * P, (j + 1) * P), slice(D + j * P, D + (j + 1) * P)
                    i = mm3(pe, pT[j // 4][:, (j % 4) * P:(j % 4 + 1) * P], kv_hi[:, v], kv_lo[:, v], kv_hi[:, k], kv_lo[:, k], True, True)
                i.then_inc(kvT_mm, 1)

            def tile(t, b, first=False, last=False):
                project(t, b, 0, first)
                if not first:
                    products(t - 1)
                project(t, b, 1, first)
                project(t, b, 2, first)
                if not last:
                    transposes(t + 1, 1 - b)
                project(t, b, 3, first)

            pe.wait_ge(scr["go"], 1)
            transposes(0, 0)
            tile(0, 0, first=True)
            tile(1, 1)
            with pe.Fori(1, NT // 2 - 1) as i:
                for b in range(2):
                    tile(2 * i + b, b)
            for b in range(2):
                tile(NT - 2 + b, b, last=b == 1)
            products(NT - 1)


E = 20000
EC = 125
NCH = E // EC
NPAIR = NCH // 2
PIECES = ((0, 418), (418, 834), (834, 1250))


def mixing_and_adjacency(nc, io, scr):
    with Phase(nc) as ctx:
        sb = lambda n, s, d: ctx.enter_context(nc.sbuf_tensor(n, s, d))
        ps = lambda n, s: ctx.enter_context(nc.psum_tensor(n, s, F32))
        sem = ctx.sem
        kv_hi, kv_lo = sb("p2_kv_hi", [P, D], F32R), sb("p2_kv_lo", [P, D], F32R)
        WB = 3
        w_hi, w_lo = sb("p2_w_hi", [P, WB, D], F32R), sb("p2_w_lo", [P, WB, D], F32R)
        w_raw = before_split(nc, "p2_w_raw", w_lo)
        by_block = lambda t, b: t[:, b, :].rearrange("p (j c) -> p j c", c=P)
        kvo_hi, kvo_lo = scr["matrix_hi"], scr["matrix_lo"]
        wo_raw = scr["matrix_raw"]
        m_buf = sb("p2_m", [P, 2, D], F32)
        pm = [ps(f"p2_m{h}", [P, HALF]) for h in range(2)]
        o_in, q_in = [sem(f"p2_o_in{j}") for j in range(C)], [sem(f"p2_q_in{b}") for b in range(2)]
        kv_zero, kv_hi_done, kv_lo_done = sem("p2_kv_zero"), sem("p2_kv_hi_done"), sem("p2_kv_lo_done")
        o_hi_done, o_lo_done, q_hi_done, q_lo_done = sem("p2_o_hi_done"), [sem(f"p2_o_lo_done{k}") for k in range(2)], sem("p2_q_hi_done"), sem("p2_q_lo_done")
        kvo_mm, kvo_hi_done, kvo_lo_done = sem("p2_kvo_mm"), sem("p2_kvo_hi_done"), sem("p2_kvo_lo_done")
        m_mm, m_done = sem("p2_m_mm"), sem("p2_m_done")
        m_out = [sem(f"p2_m_out{b}") for b in range(2)]
        HOT = 8
        src_i, dst_i = sb("p2_src_i", [EC, NCH], I32), sb("p2_dst_i", [EC, NCH], I32)
        src, dst = sb("p2_src", [EC, NCH], F32), sb("p2_dst", [EC, NCH], F32)
        nodes = sb("p2_nodes", [T, N], F16)
        own_i, own = sb("p2_own_i", [T, NT], I32), sb("p2_own", [T, NT], F32)
        at_least = sb("p2_at_least", [EC, NT + 1, NCH], BF16)
        inside = sb("p2_inside", [EC, NT, NCH], BF16)
        ones, eye = sb("p2_ones", [EC, 1], BF16), sb("p2_eye", [T, T], BF16)
        up_i, up = sb("p2_up_i", [1, NPAIR, 2], I32), sb("p2_up", [1, NPAIR, 2], BF16)
        down = sb("p2_down", [1, NPAIR, 2], BF16)
        held, work = sb("p2_held", [1, NT, NCH], BF16), sb("p2_work", [1, NT, NCH], BF16)
        last, first = sb("p2_last", [1, NT], F32), sb("p2_first", [1, NT], F32)
        before, total = sb("p2_before", [1, NT], F32), sb("p2_total", [1, NT], F32)
        bounds = sb("p2_bounds", [1, 2, NT], I32)
        row, col = sb("p2_row", [EC, HOT, 2, N], BF16), sb("p2_col", [EC, HOT, 2, T], BF16)
        one = lambda t, at, j: t[:, bass.ds(at, 1), j, :].rearrange("p o i -> p (o i)")
        self_row = sb("p2_self_row", [T, N], BF16)
        full, hi, lo = sb("p2_full", [T, N], F32), sb("p2_hi", [T, 2, N], F32R), sb("p2_lo", [T, N], F32R)
        nodes_i = full[:, :].bitcast(I32)
        acc = [[ps(f"p2_acc{a}{b}", [P, HALF]) for b in range(3)] for a in range(2)]
        pk = [pm, acc[0][0:2]]
        edges_in, step, counted, bounds_ready = sem("p2_edges_in"), sem("p2_step"), sem("p2_counted"), sem("p2_bounds_ready")
        iotas, inside_ready = sem("p2_iotas"), sem("p2_inside_ready")
        hot_ready, hot_used, self_ready, self_used = sem("p2_hot_ready"), sem("p2_hot_used"), sem("p2_self_ready"), sem("p2_self_used")
        acc_done, hi_done, full_done, lo_done = sem("p2_acc_done"), sem("p2_hi_done"), sem("p2_full_done"), sem("p2_lo_done")
        stored, stored_lo = [sem(f"p2_stored{b}") for b in range(2)], sem("p2_stored_lo")
        wo = io["woT"].rearrange("(c p) n -> c p n", p=P)
        wq = io["wq"].rearrange("(j p) c -> p j c", p=P)
        wg = io["wgT"].rearrange("(c p) n -> c p n", p=P)
        block = ctx.block()

        def pairs(eng, b):
            lo_ = eng.value_load(bounds[0:1, 0, bass.ds(b, 1)], min_val=0, max_val=NPAIR - 1)
            hi_ = eng.value_load(bounds[0:1, 1, bass.ds(b, 1)], min_val=1, max_val=NPAIR)
            return lo_, hi_

        product = lambda j, h: pk[j % 2][h][:, :]

        def know_width(eng):
            eng.wait_ge(bounds_ready, 1)
            return wide_counts(eng, scr)

        @block.sync
        def _(sp):
            sp.dma_start(src_i[:, :], io["src"]).then_inc(edges_in, 16)
            sp.dma_start(dst_i[:, :], io["dst"]).then_inc(edges_in, 16)
            for j in range(C):
                sp.dma_start(wo_raw[:, j, :], wo[j]).then_inc(o_in[j], 16)

            def load_q(c, b):
                sp.dma_start(by_block(w_raw, b), wq[:, :, bass.ds(c * P, P)]).then_inc(q_in[b], 16)

            for b in range(2):
                sp.dma_start(by_block(m_buf, b), wq[:, :, b * P:(b + 1) * P]).then_inc(q_in[b], 16)
            wide = know_width(sp)

            def next_q(n, b):
                sp.wait_ge(m_mm, 2 * n + 2)
                load_q(n + 2, b)

            def store_adjacency(n, b):
                def store(name, t, signal):
                    sp.dma_start(scr[name][:, :, bass.ds(n, 1), :].rearrange("t p b i -> p t (b i)"),
                                 t.bitcast(F32).rearrange("p (t i) -> p t i", i=T)).then_inc(signal, 16)
                sp.wait_ge(hi_done, n + 1)
                store("AT_hi", hi[:, b, :], stored[b])
                with sp.If(wide > 0):
                    sp.wait_ge(lo_done, n + 1)
                    store("AT_lo", lo[:, :], stored_lo)

            def store_m(c, b):
                sp.wait_ge(m_done, 2 * c + 2)
                sp.dma_start(scr["M"][bass.ds(c, 1), :, :].rearrange("a p n -> (a p) n"), m_buf[:, b, :]).then_inc(m_out[b], 16)

            with sp.Fori(0, C // 2 - 1) as i:
                for b in range(2):
                    next_q(2 * i + b, b)
                    store_m(2 * i + b, b)
                    store_adjacency(2 * i + b, b)
            for n in range(C - 2, NT):
                if n < C:
                    store_m(n, n % 2)
                if n == C:
                    for c in range(C):
                        sp.dma_start(scr["matrix_raw"][:, c, :], wg[c]).then_inc(scr["wg_in"][c], 16)
                store_adjacency(n, n % 2)
            for b in range(2):
                sp.wait_ge(stored[b], 16 * (NT // 2) + 1)
                sp.wait_ge(m_out[b], 8 * C + 1)
            with sp.If(wide > 0):
                sp.wait_ge(stored_lo, 16 * NT)

        @block.gpsimd
        def _(pool):
            carrier = Carrier(nc, scr, pool, "gpsimd")
            for s in (*stored, *m_out, self_used):
                pool.sem_inc(s, 1)
            nc.gpsimd.iota(nodes_i, pattern=[[1, N]], base=0, channel_multiplier=0).then_inc(iotas, 1)
            nc.gpsimd.iota(own_i[:, :], pattern=[[T, NT]], base=0, channel_multiplier=1).then_inc(iotas, 1)
            nc.gpsimd.iota(up_i[:, :, :], pattern=[[1, NPAIR], [0, 2]], base=1, channel_multiplier=0).then_inc(iotas, 1)

            def low(raw, b, done, value, signal):
                pool.wait_ge(done, value)
                nc.gpsimd.tensor_tensor(w_lo[:, b, :], raw, w_hi[:, b, :].bitcast(F32), ALU.subtract).then_inc(signal, 1)

            def q_low(c, b):
                low(w_raw[:, b, :], b, q_hi_done, c + 1, q_lo_done)

            for j in range(1, C, 2):
                low(wo_raw[:, j, :], j % WB, o_hi_done, j + 1, o_lo_done[1])
            wide = know_width(pool)

            def adjacency_low(n, b):
                with pool.If(wide > 0):
                    if not (isinstance(n, int) and n == 0):
                        pool.wait_ge(stored_lo, 16 * n)
                    pool.wait_ge(full_done, n + 1)
                    nc.gpsimd.tensor_tensor(lo[:, :], full[:, :], hi[:, b, :].bitcast(F32), ALU.subtract).then_inc(lo_done, 1)

            for b in range(2):
                q_low(2 + b, b)
                adjacency_low(b, b)
            with pool.Fori(1, C // 2 - 1) as i:
                for b in range(2):
                    q_low(2 * i + 2 + b, b)
                    adjacency_low(2 * i + b, b)
            for n in range(C - 2, NT):
                adjacency_low(n, n % 2)

        @block.scalar
        def _(act):
            carrier = Carrier(nc, scr, act, "scalar")
            act.wait_ge(kv_zero, 2)
            for h in range(2):
                rows = slice(64 * h, 64 * h + 64)
                d = lambda t: t[rows, :].rearrange("p (j x) -> p j x", x=P)[:, :, 64 * h:64 * h + 64]
                i = nc.scalar.mul(d(kv_hi), d(scr["kvT"]), 0.125)
            i.then_inc(kv_hi_done, 1)

            def product_high(j):
                for h in range(2):
                    act.wait_ge(kvo_mm, 2 * j + h + 1)
                    nc.scalar.copy(kvo_hi[:, j, h * HALF:(h + 1) * HALF], product(j, h)).then_inc(kvo_hi_done, 1)

            def wo_high(j):
                if j >= WB:
                    act.wait_ge(kvo_mm, 2 * (j - WB + 1))
                split(nc, act, None, wo_raw[:, j, :], w_hi[:, j % WB, :], None, o_in[j], 16, o_hi_done, None, j)

            for j in range(WB):
                wo_high(j)
            for j in range(C):
                product_high(j)
                if j + WB < C:
                    wo_high(j + WB)

            def q_high(c, b, raw=w_raw):
                act.wait_ge(q_in[b], 8 * (c - b) + 16)
                nc.scalar.copy(w_hi[:, b, :], raw[:, b, :]).then_inc(q_hi_done, 1)

            for b in range(2):
                q_high(b, b, m_buf)

            def adjacency_high(n, b, first=False):
                act.wait_ge(stored[b], 8 * (n - b) + 1)
                hold(carrier, acc_done, n + 1)
                if not first:
                    with act.If(wide > 0):
                        hold(carrier, lo_done, n)
                for k, (a, z) in enumerate(PIECES):
                    s = nc.scalar.copy(hi[:, b, a:z], acc[b][k][0:T, 0:z - a])
                s.then_inc(hi_done, 1)
                with act.If(wide > 0):
                    for k, (a, z) in enumerate(PIECES):
                        s = nc.scalar.copy(full[:, a:z], acc[b][k][0:T, 0:z - a])
                    s.then_inc(full_done, 1)

            def m_copy(c, b):
                act.wait_ge(m_out[b], 8 * (c - b) + 1)
                for h in range(2):
                    act.wait_ge(m_mm, 2 * c + h + 1)
                    nc.scalar.copy(m_buf[:, b, h * HALF:(h + 1) * HALF], pm[h][:, :]).then_inc(m_done, 1)

            m_copy(0, 0)
            q_high(2, 0)
            wide = know_width(act)
            adjacency_high(0, 0, first=True)
            m_copy(1, 1)
            q_high(3, 1)
            adjacency_high(1, 1)
            with act.Fori(1, C // 2 - 1) as i:
                for b in range(2):
                    m_copy(2 * i + b, b)
                    q_high(2 * i + 2 + b, b)
                    adjacency_high(2 * i + b, b)
            for n in range(C - 2, NT):
                if n < C:
                    m_copy(n, n % 2)
                adjacency_high(n, n % 2)

        @block.vector
        def _(dve):
            n = [0]

            def link(ins):
                n[0] += 1
                ins.then_inc(step, 1)
                dve.wait_ge(step, n[0])

            nc.vector.memset(kv_hi[:, :].bitcast(F32), 0.0).then_inc(kv_zero, 1)
            nc.vector.memset(kv_lo[:, :].bitcast(F32), 0.0).then_inc(kv_zero, 1)
            nc.vector.memset(ones[:, :], 1.0)
            nc.vector.tensor_copy(eye[:, :], scr["ident"][0:T, 0:T])
            dve.wait_ge(kv_zero, 2)
            dve.wait_ge(kv_hi_done, 1)
            for h in range(2):
                rows = slice(64 * h, 64 * h + 64)
                d = lambda t: t[rows, :].rearrange("p (j x) -> p j x", x=P)[:, :, 64 * h:64 * h + 64]
                i = nc.vector.scalar_tensor_tensor(d(kv_lo), d(scr["kvT"]), 0.125, d(kv_hi.bitcast(F32)), ALU.mult, ALU.subtract)
            i.then_inc(kv_lo_done, 1)

            def product_low(j):
                for h in range(2):
                    dve.wait_ge(kvo_hi_done, 2 * j + h + 1)
                    at = slice(h * HALF, (h + 1) * HALF)
                    nc.vector.tensor_tensor(kvo_lo[:, j, at], product(j, h), kvo_hi[:, j, at].bitcast(F32), ALU.subtract).then_inc(kvo_lo_done, 1)

            def low(raw, b, done, value, signal):
                dve.wait_ge(done, value)
                nc.vector.tensor_tensor(w_lo[:, b, :], raw, w_hi[:, b, :].bitcast(F32), ALU.subtract).then_inc(signal, 1)

            def wo_low(j):
                if j % 2 == 0 and j < C:
                    low(wo_raw[:, j, :], j % WB, o_hi_done, j + 1, o_lo_done[0])

            for j in range(WB):
                wo_low(j)
            dve.wait_ge(edges_in, 32)
            nc.vector.tensor_copy(src[:, :], src_i[:, :])
            link(nc.vector.tensor_copy(dst[:, :], dst_i[:, :]))
            for b in range(NT + 1):
                i = nc.vector.tensor_scalar(at_least[:, b, :], dst[:, :], float(b * T), None, ALU.is_ge)
            link(i)
            nc.vector.tensor_tensor(inside[:, :, :], at_least[:, 0:NT, :], at_least[:, 1:NT + 1, :], ALU.subtract).then_inc(inside_ready, 1)
            for j in range(C):
                product_low(j)
                wo_low(j + WB)
            for b in range(2):
                low(m_buf[:, b, :], b, q_hi_done, b + 1, q_lo_done)

            dve.wait_ge(iotas, 3)
            nc.vector.tensor_copy(nodes[:, :], nodes_i)
            nc.vector.tensor_copy(own[:, :], own_i[:, :])
            link(nc.vector.tensor_copy(up[:, :, :], up_i[:, :, :]))
            nc.vector.tensor_scalar(down[:, :, :], up[:, :, :], -1.0, NPAIR + 1.0, ALU.mult, ALU.add)
            dve.wait_ge(counted, 1)
            for k in range(NT // 2):
                i = nc.vector.tensor_scalar(held[:, 2 * k:2 * k + 2, :], acc[k // 3][k % 3][0:1, 0:2 * NCH].rearrange("p (b c) -> p b c", c=NCH), 1.0, None, ALU.min)
            link(i)
            for k in range(NT // 2):
                i = nc.vector.tensor_reduce(total[:, 2 * k:2 * k + 2], acc[k // 3][k % 3][0:1, 0:2 * NCH].rearrange("p (b c) -> p b c", c=NCH), AX, ALU.add)
            link(i)
            link(nc.vector.tensor_reduce(before[:, 0:1], total[:, :], AX, ALU.max))
            link(nc.vector.tensor_scalar(scr["wide"][:, :], before[:, 0:1], 4095.0, None, ALU.is_gt))
            flat = lambda t: t[:, :, :].rearrange("p k j -> p (k j)").unsqueeze(1).to_broadcast([1, NT, NCH])
            link(nc.vector.tensor_tensor(work[:, :, :], held[:, :, :], flat(up), ALU.mult))
            link(nc.vector.tensor_reduce(last[:, :], work[:, :, :], AX, ALU.max))
            link(nc.vector.tensor_tensor(work[:, :, :], held[:, :, :], flat(down), ALU.mult))
            link(nc.vector.tensor_reduce(first[:, :], work[:, :, :], AX, ALU.max))
            link(nc.vector.tensor_scalar(last[:, :], last[:, :], 1.0, None, ALU.max))
            link(nc.vector.tensor_scalar(first[:, :], first[:, :], -1.0, float(NPAIR), ALU.mult, ALU.add))
            link(nc.vector.tensor_scalar(before[:, :], last[:, :], -1.0, None, ALU.add))
            link(nc.vector.tensor_tensor(first[:, :], first[:, :], before[:, :], ALU.min))
            link(nc.vector.tensor_copy(bounds[:, 0, :], first[:, :]))
            nc.vector.tensor_copy(bounds[:, 1, :], last[:, :]).then_inc(bounds_ready, 1)
            dve.wait_ge(bounds_ready, 1)
            with dve.register("p2_dve_taken") as taken:
                dve.reg_mov(taken, 0)
                src2, dst2 = (t[:, :].rearrange("p (k j) -> p k j", j=2) for t in (src, dst))
                with dve.Fori(0, NT) as blk:
                    lo_, hi_ = pairs(dve, blk)
                    first_node = dve.snap(blk * T)
                    dve.wait_ge(self_used, blk + 1)
                    nc.vector.tensor_scalar(self_row[:, :], nodes[:, :], own[:, bass.ds(blk, 1)], None, ALU.is_equal).then_inc(self_ready, 1)
                    with dve.Fori(lo_, hi_) as p:
                        done = dve.snap(taken)
                        at = dve.snap(done % HOT)
                        dve.wait_ge(hot_used, done + 1)
                        for j in range(2):
                            nc.vector.tensor_scalar(one(col, at, j), nodes[:, bass.ds(first_node, T)], dst2[:, bass.ds(p, 1), j], None, ALU.is_equal)
                            i = nc.vector.tensor_scalar(one(row, at, j), nodes[:, :], src2[:, bass.ds(p, 1), j], None, ALU.is_equal)
                        i.then_inc(hot_ready, 1)
                        dve.reg_add(taken, taken, 1)

        @block.tensor
        def _(pe):
            pe.sem_inc(hot_used, HOT)
            pe.wait_ge(kv_lo_done, 1)
            for j in range(C):
                pe.wait_ge(o_lo_done[j % 2], j // 2 + 1)
                for h in range(2):
                    if j >= 2:
                        pe.wait_ge(kvo_lo_done, 2 * j - 3 + h)
                    at, k = slice(h * HALF, (h + 1) * HALF), slice(j * P, (j + 1) * P)
                    mm3(pe, product(j, h), kv_hi[:, k], kv_lo[:, k], w_hi[:, j % WB, at], w_lo[:, j % WB, at], True, True).then_inc(kvo_mm, 1)
            pe.wait_ge(kvo_lo_done, 2 * C)
            pe.wait_ge(inside_ready, 1)
            for k in range(NT // 2):
                i = pe.matmul(acc[k // 3][k % 3][0:1, 0:2 * NCH], ones[:, :], inside[:, 2 * k:2 * k + 2, :].rearrange("p b c -> p (b c)"), start=True, stop=True)
            i.then_inc(counted, 1)
            with pe.register("p2_pe_taken") as taken:
                pe.reg_mov(taken, 0)

                def m_rows(c, b, first=False):
                    pe.wait_ge(q_lo_done, c + 1)
                    for h in range(2):
                        if not first:
                            pe.wait_ge(m_done, 2 * c - 1 + h)
                        at = slice(h * HALF, (h + 1) * HALF)
                        for j in range(C):
                            m = mm3(pe, pm[h][:, :], by_block(w_hi, b)[:, j, :], by_block(w_lo, b)[:, j, :], kvo_hi[:, j, at], kvo_lo[:, j, at], j == 0, j == C - 1)
                        m.then_inc(m_mm, 1)

                m_rows(0, 0, first=True)
                wide = know_width(pe)

                def adjacency_block(blk, b, first=False):
                    lo_, hi_ = pairs(pe, blk)
                    if not first:
                        pe.wait_ge(hi_done, blk - b)
                        with pe.If(wide > 0):
                            pe.wait_ge(full_done, blk - b)
                    pe.wait_ge(self_ready, blk + 1)
                    for k, (a, z) in enumerate(PIECES):
                        m = pe.matmul(acc[b][k][0:T, 0:z - a], eye[:, :], self_row[:, a:z], start=True, stop=False)
                    m.then_inc(self_used, 1)
                    with pe.Fori(lo_, hi_) as p:
                        done = pe.snap(taken)
                        at = pe.snap(done % HOT)
                        pe.wait_ge(hot_ready, done + 1)
                        for j in range(2):
                            for k, (a, z) in enumerate(PIECES):
                                m = pe.matmul(acc[b][k][0:T, 0:z - a], one(col, at, j), one(row, at, j)[:, a:z], start=False, stop=False)
                        m.then_inc(hot_used, 1)
                        pe.reg_add(taken, taken, 1)
                    for k in range(3):
                        m = pe.matmul(acc[b][k][0:T, 0:2], scr["zero"][0:T, 0:T], scr["zero"][0:T, 0:2], start=False, stop=True)
                    m.then_inc(acc_done, 1)

                adjacency_block(0, 0, first=True)
                m_rows(1, 1)
                adjacency_block(1, 1, first=True)
                with pe.Fori(1, C // 2) as i:
                    for b in range(2):
                        m_rows(2 * i + b, b)
                        adjacency_block(2 * i + b, b)
                for b in range(2):
                    adjacency_block(C + b, b)


def wide_counts(eng, scr):
    return eng.value_load(scr["wide"][0:1, 0:1], min_val=0, max_val=1)


def load_tile(sp, dst, dram, t, done):
    src = dram[bass.ds(t, 1)] if not isinstance(t, int) else dram[t:t + 1]
    names = "abc"[:len(dram.shape) - 2]
    sp.dma_start(dst, src.rearrange(f"o p {' '.join(names)} -> (o p) ({' '.join(names)})")).then_inc(done, 16)


def node_features(nc, io, scr):
    with Phase(nc) as ctx:
        sb = lambda n, s, d: ctx.enter_context(nc.sbuf_tensor(n, s, d))
        sem = ctx.sem
        w_hi, w_lo, w_raw, w_in = scr["matrix_hi"], scr["matrix_lo"], scr["matrix_raw"], scr["wg_in"]
        xT_hi, xT_lo = sb("p4_xT_hi", [P, 2, C * T], F32R), sb("p4_xT_lo", [P, 2, C * T], F32R)
        at_hi, at_lo = sb("p4_at_hi", [T, NT * T], F32R), sb("p4_at_lo", [T, NT * T], F32R)
        bias, h_b = sb("p4_bias", [T, D], F32), sb("p4_h_b", [T, D], F32)
        ones = sb("p4_ones", [T, 2], F32R)
        small = sb("p4_small", [T, 8], F32)
        hs_hi, hs_lo, dinv = scr["hs_hi"], scr["hs_lo"], scr["dinv"]
        ph = [ctx.enter_context(nc.psum_tensor(f"p4_h{b}", [T, HALF], F32)) for b in range(4)]
        pdeg = ctx.enter_context(nc.psum_tensor("p4_deg", [T, 2], F32))
        x_in = [sem(f"p4_x_in{b}") for b in range(2)]
        at_in, at_lo_in, bias_in, ones_ready = sem("p4_at_in"), sem("p4_at_lo_in"), sem("p4_bias_in"), sem("p4_ones")
        w_hi_done, w_lo_done = sem("p4_w_hi_done"), sem("p4_w_lo_done")
        deg_mm, deg_ready, root_ready, step, dinv_ready = sem("p4_deg_mm"), sem("p4_deg"), sem("p4_root"), sem("p4_step"), sem("p4_dinv")
        h_mm, hb_done, hi_done, lo_done = sem("p4_h_mm"), sem("p4_hb_done"), sem("p4_hi_done"), sem("p4_lo_done")
        block = ctx.block()

        @block.sync
        def _(sp):
            wide = wide_counts(sp, scr)

            def loads(t, b):
                load_tile(sp, xT_hi[:, b, :].bitcast(F32), scr["xT_hi"], t, x_in[b])
                load_tile(sp, xT_lo[:, b, :].bitcast(F32), scr["xT_lo"], t, x_in[b])

            def load_at(t):
                load_tile(sp, at_hi[:, :].bitcast(F32), scr["AT_hi"], t, at_in)
                with sp.If(wide > 0):
                    load_tile(sp, at_lo[:, :].bitcast(F32), scr["AT_lo"], t, at_lo_in)

            loads(0, 0)
            load_at(0)
            loads(1, 1)
            sp.dma_start(bias[:, :], io["gb"].to_broadcast([T, D])).then_inc(bias_in, 16)
            sp.wait_ge(deg_mm, 1)
            load_at(1)
            with sp.Fori(1, NT // 2) as i:
                for b in range(2):
                    t = 2 * i + b
                    sp.wait_ge(h_mm, 2 * (t - 1))
                    loads(t, b)
                    sp.wait_ge(deg_mm, t)
                    load_at(t)
            for b in range(2):
                load_tile(sp, scr["at_hi"][:, b, :].bitcast(F32), scr["AT_hi"], b, scr["at_in"][b])

        @block.scalar
        def _(act):
            carrier = Carrier(nc, scr, act, "scalar")
            for c in range(C):
                split(nc, act, None, w_raw[:, c, :], w_hi[:, c, :], None, w_in[c], 16, w_hi_done, None, c)

            def root(t):
                hold(carrier, deg_ready, t + 2)
                nc.scalar.activation(small[:, 1:2], small[:, 0:1], ACT.Sqrt).then_inc(root_ready, 1)

            def tile(t):
                for h in range(2):
                    hold(carrier, hb_done, 2 * t + h + 5)
                    nc.scalar.activation(hs_hi[:, bass.ds(t, 1), h * HALF:(h + 1) * HALF].rearrange("p o n -> p (o n)"),
                                         h_b[:, h * HALF:(h + 1) * HALF], ACT.Copy, scale=dinv[:, bass.ds(t, 1)]).then_inc(hi_done, 1)

            with act.Fori(0, NT) as t:
                root(t)
                tile(t)

        @block.vector
        def _(dve):
            nc.vector.memset(ones[:, :].bitcast(F32), 1.0).then_inc(ones_ready, 1)
            for c in range(C):
                split(nc, None, dve, w_raw[:, c, :], w_hi[:, c, :], w_lo[:, c, :], None, 0, w_hi_done, w_lo_done, c)
            dve.wait_ge(bias_in, 16)

            def tile(t, b):
                dve.wait_ge(deg_mm, t + 1)
                nc.vector.tensor_copy(small[:, 0:1], pdeg[:, 0:1]).then_inc(deg_ready, 1)
                dve.wait_ge(root_ready, t + 1)
                inverse_root(nc, dve, small, step, 4 * t)
                dve.wait_ge(step, 4 * t + 4)
                nc.vector.tensor_copy(dinv[:, bass.ds(t, 1)], small[:, 6:7]).then_inc(dinv_ready, 1)
                dve.wait_ge(dinv_ready, t + 1)
                for h in range(2):
                    at = slice(h * HALF, (h + 1) * HALF)
                    dve.wait_ge(h_mm, 2 * t + h + 1)
                    nc.vector.tensor_tensor(h_b[:, at], ph[2 * b + h][:, :], bias[:, at], ALU.add).then_inc(hb_done, 1)
                for h in range(2):
                    at = slice(h * HALF, (h + 1) * HALF)
                    dve.wait_ge(hi_done, 2 * t + h + 1)
                    flat = lambda x: x[:, bass.ds(t, 1), at].rearrange("p o n -> p (o n)")
                    nc.vector.scalar_tensor_tensor(flat(hs_lo), h_b[:, at], dinv[:, bass.ds(t, 1)], flat(hs_hi).bitcast(F32), ALU.mult, ALU.subtract).then_inc(lo_done, 1)

            with dve.Fori(0, NT // 2) as i:
                for b in range(2):
                    tile(2 * i + b, b)

        @block.tensor
        def _(pe):
            pe.sem_inc(hb_done, 4)
            pe.sem_inc(deg_ready, 1)
            pe.wait_ge(ones_ready, 1)
            wide = wide_counts(pe, scr)

            def degree(t):
                pe.wait_ge(deg_ready, t + 1)
                pe.wait_ge(at_in, 16 * t + 16)
                pe.matmul(pdeg[:, :], at_hi[:, 0:T], ones[:, :], start=True, stop=False)
                with pe.If(wide > 0):
                    pe.wait_ge(at_lo_in, 16 * t + 16)
                    for j in range(NT):
                        pe.matmul(pdeg[:, :], at_lo[:, j * T:(j + 1) * T], ones[:, :], start=False, stop=False)
                for j in range(1, NT):
                    m = pe.matmul(pdeg[:, :], at_hi[:, j * T:(j + 1) * T], ones[:, :], start=False, stop=j == NT - 1)
                m.then_inc(deg_mm, 1)

            def features(t, b, first=False):
                pe.wait_ge(x_in[b], 16 * (t - b) + 32)
                for h in range(2):
                    pe.wait_ge(hb_done, 2 * t + h + 1)
                    col = slice(h * HALF, (h + 1) * HALF)
                    for c in range(C):
                        if first and h == 0:
                            pe.wait_ge(w_lo_done, c + 1)
                        at = slice(c * T, (c + 1) * T)
                        m = mm3(pe, ph[2 * b + h][:, :], xT_hi[:, b, at], xT_lo[:, b, at], w_hi[:, c, col], w_lo[:, c, col], c == 0, c == C - 1)
                    m.then_inc(h_mm, 1)

            features(0, 0, first=True)
            degree(0)
            features(1, 1)
            degree(1)
            with pe.Fori(1, NT // 2) as i:
                for b in range(2):
                    features(2 * i + b, b)
                    degree(2 * i + b)


EXPERTS = 8


def aggregate_and_mix(nc, io, scr):
    with Phase(nc) as ctx:
        sb = lambda n, s, d: ctx.enter_context(nc.sbuf_tensor(n, s, d))
        ps = lambda n, s: ctx.enter_context(nc.psum_tensor(n, s, F32))
        sem = ctx.sem
        m_hi, m_lo = sb("p5_m_hi", [P, C, D], F32R), sb("p5_m_lo", [P, C, D], F32R)
        m_raw = before_split(nc, "p5_m_raw", m_lo)
        at_hi, at_lo = scr["at_hi"], sb("p5_at_lo", [T, NT * T], F32R)
        xT_hi, xT_lo = sb("p5_xT_hi", [P, 2, C * T], F32R), sb("p5_xT_lo", [P, C * T], F32R)
        x1, xn = sb("p5_x1", [T, 2, D], F32), sb("p5_xn", [T, D], F32)
        nT_hi, nT_lo = sb("p5_nT_hi", [P, C * T], F32R), sb("p5_nT_lo", [P, C * T], F32R)
        r_raw = sb("p5_r_raw", [P, C, EXPERTS], F32)
        r_parts = sb("p5_r_parts", [P, C, 2, EXPERTS], F32R)
        r_hi, r_lo = r_parts[:, :, 0, :], r_parts[:, :, 1, :]
        log_low = sb("p5_log_low", [T, EXPERTS], F32)
        stats, mv, small = sb("p5_stats", [T, 2, 6], F32), sb("p5_mv", [T, 2], F32), sb("p5_small", [T, 8], F32)
        hs_hi, hs_lo, dinv, logits = scr["hs_hi"], scr["hs_lo"], scr["dinv"], scr["logits"]
        pagg, pmix = [ps(f"p5_agg{h}", [T, HALF]) for h in range(2)], [ps(f"p5_mix{h}", [T, HALF]) for h in range(2)]
        pT = [ps(f"p5_T{h}", [P, 4 * T]) for h in range(2)]
        plog = ps("p5_log", [T, 2, EXPERTS])
        m_in, m_hi_done, m_lo_done, r_in = [sem(f"p5_m_in{c}") for c in range(C)], sem("p5_m_hi_done"), sem("p5_m_lo_done"), sem("p5_r_in")
        at_in, at_lo_in = scr["at_in"], sem("p5_at_lo_in")
        xT_in, xT_lo_in, x_in = [sem(f"p5_xT_in{b}") for b in range(2)], sem("p5_xT_lo_in"), [sem(f"p5_x_in{b}") for b in range(2)]
        agg_mm, mix_mm = sem("p5_agg_mm"), sem("p5_mix_mm")
        agg_added, mix_added, x1_stored = sem("p5_agg_added"), sem("p5_mix_added"), [sem(f"p5_x1_stored{b}") for b in range(2)]
        step, var_ready, std_ready, xn_ready, xn_stored = sem("p5_step"), sem("p5_var"), sem("p5_std"), sem("p5_xn"), sem("p5_xn_stored")
        nT_mm, nT_hi_done, nT_lo_done, nT_stored = sem("p5_nT_mm"), sem("p5_nT_hi_done"), sem("p5_nT_lo_done"), sem("p5_nT_stored")
        r_hi_done, r_lo_done, log_mm, log_done = sem("p5_r_hi_done"), sem("p5_r_lo_done"), sem("p5_log_mm"), sem("p5_log_done")
        low_taken = sem("p5_low_taken")
        block = ctx.block()
        x_dram = io["x"].rearrange("(t p) d -> t p d", p=T)

        @block.sync
        def _(sp):
            wide = wide_counts(sp, scr)

            def load_at_lo(t):
                with sp.If(wide > 0):
                    if not (isinstance(t, int) and t == 0):
                        sp.wait_ge(agg_mm, 2 * t)
                    load_tile(sp, at_lo[:, :].bitcast(F32), scr["AT_lo"], t, at_lo_in)

            def load_at_hi(t, b):
                load_tile(sp, at_hi[:, b, :].bitcast(F32), scr["AT_hi"], t, at_in[b])

            def load_xT_hi(t, b):
                load_tile(sp, xT_hi[:, b, :].bitcast(F32), scr["xT_hi"], t, xT_in[b])

            def load_x(t, b):
                load_tile(sp, x1[:, b, :], x_dram, t, x_in[b])

            load_at_lo(0)
            load_x(0, 0)
            load_xT_hi(0, 0)
            load_tile(sp, xT_lo[:, :].bitcast(F32), scr["xT_lo"], 0, xT_lo_in)
            for c in range(C):
                sp.dma_start(m_raw[:, c, :], scr["M"][c, :, :]).then_inc(m_in[c], 16)
            load_xT_hi(1, 1)
            load_x(1, 1)

            def rest(t, b, more):
                if more >= 1:
                    load_at_lo(t + 1)
                sp.wait_ge(mix_mm, 2 * t + 2)
                if more >= 1:
                    load_tile(sp, xT_lo[:, :].bitcast(F32), scr["xT_lo"], t + 1, xT_lo_in)
                if more >= 2:
                    load_at_hi(t + 2, b)
                    load_xT_hi(t + 2, b)
                sp.wait_ge(mix_added, 2 * t + 2)
                load_store = scr["x1"][bass.ds(t, 1), :, :].rearrange("o p d -> (o p) d")
                sp.dma_start(load_store, x1[:, b, :]).then_inc(x1_stored[b], 16)
                sp.wait_ge(xn_ready, t + 1)
                sp.dma_start(scr["xn2"][bass.ds(t * T, T), :], xn[:, :]).then_inc(xn_stored, 16)
                if more >= 2:
                    sp.wait_ge(x1_stored[b], 8 * (t - b) + 16)
                    load_x(t + 2, b)
                sp.wait_ge(nT_lo_done, 2 * t + 2)
                for name, t_ in (("nT_hi", nT_hi), ("nT_lo", nT_lo)):
                    sp.dma_start(scr[name][bass.ds(t, 1), :, :].rearrange("o p d -> (o p) d"), t_[:, :].bitcast(F32)).then_inc(nT_stored, 16)

            with sp.Fori(0, NT // 2 - 1) as i:
                for b in range(2):
                    rest(2 * i + b, b, 2)
            for b in range(2):
                rest(NT - 2 + b, b, 1 - b)
            for b in range(2):
                sp.wait_ge(x1_stored[b], 8 * NT)
            sp.wait_ge(xn_stored, 16 * NT)
            sp.wait_ge(nT_stored, 32 * NT)

        @block.gpsimd
        def _(pool):
            pool.dma_start(r_raw[:, :, :], io["router"].rearrange("(c p) e -> p c e", p=P)).then_inc(r_in, 16)

        @block.scalar
        def _(act):
            carrier = Carrier(nc, scr, act, "scalar")
            split(nc, act, None, r_raw[:, :, :], r_hi, None, r_in, 16, r_hi_done, None, 0)
            for c in range(C):
                split(nc, act, None, m_raw[:, c, :], m_hi[:, c, :], None, m_in[c], 16, m_hi_done, None, c)

            def tile(t, first=False):
                hold(carrier, var_ready, t + 1)
                nc.scalar.activation(small[:, 1:2], small[:, 0:1], ACT.Sqrt).then_inc(std_ready, 1)
                if not first:
                    act.wait_ge(nT_stored, 32 * t)
                    act.wait_ge(log_mm, t)
                for h in range(2):
                    act.wait_ge(nT_mm, 2 * t + h + 1)
                    nc.scalar.copy(nT_hi[:, h * 4 * T:(h + 1) * 4 * T], pT[h][:, :]).then_inc(nT_hi_done, 1)

            tile(0, True)
            with act.Fori(1, NT) as t:
                tile(t)

        @block.vector
        def _(dve):
            carrier = Carrier(nc, scr, dve, "vector")
            split(nc, None, dve, r_raw[:, :, :], r_hi, r_lo, None, 0, r_hi_done, r_lo_done, 0)

            def add_aggregated(t, b):
                dve.wait_ge(x_in[b], 8 * (t - b) + 16)
                for h in range(2):
                    at = slice(h * HALF, (h + 1) * HALF)
                    dve.wait_ge(agg_mm, 2 * t + h + 1)
                    nc.vector.scalar_tensor_tensor(x1[:, b, at], pagg[h][:, :], dinv[:, bass.ds(t, 1)], x1[:, b, at], ALU.mult, ALU.add).then_inc(agg_added, 1)

            def tile(t, b, first):
                if not first:
                    add_aggregated(t, b)
                for h in range(2):
                    at = slice(h * HALF, (h + 1) * HALF)
                    dve.wait_ge(agg_added, 2 * t + h + 1)
                    dve.wait_ge(mix_mm, 2 * t + h + 1)
                    nc.vector.tensor_tensor(x1[:, b, at], x1[:, b, at], pmix[h][:, :], ALU.add).then_inc(mix_added, 1)
                dve.wait_ge(mix_added, 2 * t + 2)
                if not first:
                    dve.wait_ge(xn_stored, 16 * t)
                    dve.wait_ge(nT_mm, 2 * t)
                layernorm(nc, carrier, x1[:, b, :], xn[:, :], stats, mv, small, step, 7 * t, var_ready, std_ready, xn_ready, t)
                for h in range(2):
                    dve.wait_ge(nT_hi_done, 2 * t + h + 1)
                    at = slice(h * 4 * T, (h + 1) * 4 * T)
                    nc.vector.tensor_tensor(nT_lo[:, at], pT[h][:, :], nT_hi[:, at].bitcast(F32), ALU.subtract).then_inc(nT_lo_done, 1)
                dve.wait_ge(log_mm, t + 1)
                nc.vector.tensor_copy(log_low[:, :], plog[:, 1, :]).then_inc(low_taken, 1)
                dve.wait_ge(low_taken, t + 1)
                nc.vector.tensor_tensor(logits[:, bass.ds(t, 1), :].rearrange("p o e -> p (o e)"), plog[:, 0, :], log_low[:, :], ALU.add).then_inc(log_done, 1)

            for b in range(2):
                if b == 0:
                    add_aggregated(0, 0)
                    for c in range(C):
                        split(nc, None, dve, m_raw[:, c, :], m_hi[:, c, :], m_lo[:, c, :], None, 0, m_hi_done, m_lo_done, c)
                tile(b, b, b == 0)
            with dve.Fori(1, NT // 2) as i:
                for b in range(2):
                    tile(2 * i + b, b, False)

        @block.tensor
        def _(pe):
            wide = wide_counts(pe, scr)

            def aggregate(t, b, h):
                if h == 0:
                    pe.wait_ge(at_in[b], 8 * (t - b) + 16)
                col = slice(h * HALF, (h + 1) * HALF)
                if not (isinstance(t, int) and t == 0):
                    pe.wait_ge(agg_added, 2 * t - 1 + h)
                counts = lambda x, j: x[:, j * T:(j + 1) * T]
                for j in range(NT):
                    pe.matmul(pagg[h][:, :], counts(at_hi[:, b, :], j), hs_lo[:, j, col], start=j == 0, stop=False)
                with pe.If(wide > 0):
                    pe.wait_ge(at_lo_in, 16 * t + 16)
                    for j in range(NT):
                        pe.matmul(pagg[h][:, :], counts(at_lo, j), hs_hi[:, j, col], start=False, stop=False)
                for j in range(NT):
                    m = pe.matmul(pagg[h][:, :], counts(at_hi[:, b, :], j), hs_hi[:, j, col], start=False, stop=j == NT - 1)
                m.then_inc(agg_mm, 1)

            def mix(t, b, first=False, halves=range(2)):
                for h in halves:
                    if h == 0:
                        pe.wait_ge(xT_in[b], 8 * (t - b) + 16)
                        pe.wait_ge(xT_lo_in, 16 * t + 16)
                    col = slice(h * HALF, (h + 1) * HALF)
                    if not first:
                        pe.wait_ge(mix_added, 2 * t - 1 + h)
                    for c in range(C):
                        if first and h == 0:
                            pe.wait_ge(m_lo_done, c + 1)
                        at = slice(c * T, (c + 1) * T)
                        m = mm3(pe, pmix[h][:, :], xT_hi[:, b, at], xT_lo[:, at], m_hi[:, c, col], m_lo[:, c, col], c == 0, c == C - 1)
                    m.then_inc(mix_mm, 1)

            def turn(t, first=False):
                pe.wait_ge(xn_ready, t + 1)
                if not first:
                    pe.wait_ge(nT_lo_done, 2 * t)
                for c in range(C):
                    m = pe.transpose(pT[c // 4][:, (c % 4) * T:(c % 4 + 1) * T], xn[:, c * P:(c + 1) * P], scr["ident"][0:T, 0:T])
                    if c % 4 == 3:
                        m.then_inc(nT_mm, 1)

            def route(t, first=False):
                if not first:
                    pe.wait_ge(log_done, t)
                pe.wait_ge(nT_lo_done, 2 * t + 2)
                for c in range(C):
                    at = slice(c * T, (c + 1) * T)
                    both = r_parts[:, c, :, :].rearrange("p k e -> p (k e)")
                    pe.matmul(plog[:, :, :].rearrange("p k e -> p (k e)"), nT_lo[:, at], both, start=c == 0, stop=False)
                    m = pe.matmul(plog[:, :, :].rearrange("p k e -> p (k e)"), nT_hi[:, at], both, start=False, stop=c == C - 1)
                m.then_inc(log_mm, 1)

            for t in range(2):
                for h in range(2):
                    aggregate(t, t, h)
            mix(0, 0, first=True)
            mix(1, 1)
            turn(0, first=True)
            pe.wait_ge(r_lo_done, 1)
            route(0, first=True)
            with pe.Fori(1, NT // 2) as i:
                for b in range(2):
                    t = 2 * i + b
                    aggregate(t, b, 0)
                    aggregate(t, b, 1)
                    turn(t - 1)
                    mix(t, b, halves=[0])
                    route(t - 1)
                    mix(t, b, halves=[1])
            turn(NT - 1)
            route(NT - 1)


TOP = 4
MOE = 512
SHARED = 256
SLOTS = 64
FAR = 1 << 20


def shared_and_routing(nc, io, scr, out):
    with Phase(nc) as ctx:
        sb = lambda n, s, d=F32: ctx.enter_context(nc.sbuf_tensor(n, s, d))
        ps = lambda n, s: ctx.enter_context(nc.psum_tensor(n, s, F32))
        sem = ctx.sem
        G = 2 * SHARED
        gu_hi, gu_lo = sb("p6_gu_hi", [P, C, G], F32R), sb("p6_gu_lo", [P, C, G], F32R)
        d_hi, d_lo = sb("p6_d_hi", [P, 2, D], F32R), sb("p6_d_lo", [P, 2, D], F32R)
        gu_raw, d_raw = before_split(nc, "p6_gu_raw", gu_lo), before_split(nc, "p6_d_raw", d_lo)
        nT_hi, nT_lo = sb("p6_nT_hi", [P, 2, C * T], F32R), sb("p6_nT_lo", [P, 2, C * T], F32R)
        y = sb("p6_y", [T, 2, D])
        sg, a = sb("p6_sg", [T, SHARED]), sb("p6_a", [T, SHARED])
        aT_hi, aT_lo = sb("p6_aT_hi", [P, 2 * T], F32R), sb("p6_aT_lo", [P, 2 * T], F32R)
        pgu, py = [ps(f"p6_gu{b}", [T, G]) for b in range(2)], [ps(f"p6_y{h}", [T, HALF]) for h in range(2)]
        paT = ps("p6_aT", [P, 2 * T])
        pcount = ps("p6_count", [T, 2, NT * EXPERTS])
        plist = ps("p6_list", [P, 2, SLOTS])
        gu_in, d_in = [sem(f"p6_gu_in{k}") for k in range(2)], sem("p6_d_in")
        nT_in, x1_in, stored = [sem(f"p6_nT_in{b}") for b in range(2)], [sem(f"p6_x1_in{b}") for b in range(2)], [sem(f"p6_stored{b}") for b in range(2)]
        gu_hi_done, gu_lo_done, d_hi_done, d_lo_done = sem("p6_gu_hi_done"), sem("p6_gu_lo_done"), sem("p6_d_hi_done"), sem("p6_d_lo_done")
        gu_mm, sg_done, a_done, aT_mm, aT_hi_done, aT_lo_done = sem("p6_gu_mm"), sem("p6_sg"), sem("p6_a"), sem("p6_aT_mm"), sem("p6_aT_hi_done"), sem("p6_aT_lo_done")
        y_mm, y_done = sem("p6_y_mm"), sem("p6_y_done")
        W = NT * EXPERTS
        sc, ez = sb("r_scores", [T, NT, EXPERTS]), sb("r_exp", [T, NT, EXPERTS])
        row_max, row_sum = sb("r_max", [T, NT]), sb("r_sum", [T, NT])
        bias = sb("r_bias", [T, 1])
        tri_i, tri = sb("r_tri_i", [T, EXPERTS, EXPERTS], I32), sb("r_tri", [T, EXPERTS, EXPERTS])
        full_i, full = sb("r_full_i", [T, EXPERTS, NT], I32), sb("r_full", [T, EXPERTS, NT])
        kth_i, kth = sb("r_kth_i", [T, TOP, EXPERTS], I32), sb("r_kth", [T, TOP, EXPERTS])
        below_i, below = sb("r_below_i", [T, T], I32), sb("r_below", [T, T], BF16)
        all_ones = sb("r_ones", [T, T], BF16)
        gt, eq = sb("r_gt", [T, NT, EXPERTS * EXPERTS]), sb("r_eq", [T, NT, EXPERTS * EXPERTS])
        rank, sel, sel_b = sb("r_rank", [T, NT, EXPERTS]), sb("r_sel", [T, NT, EXPERTS]), sb("r_sel_b", [T, NT, EXPERTS], BF16)
        wts, pos = sb("r_wts", [T, NT, EXPERTS]), sb("r_pos", [T, NT, EXPERTS])
        before, within = sb("r_before", [T, NT + 1, EXPERTS]), sb("r_within", [T, 2, W])
        over, tiles, base = sb("r_over", [T, EXPERTS, NT]), sb("r_tiles", [T, EXPERTS + 1]), sb("r_base", [T, EXPERTS])
        span = sb("r_span", [T, EXPERTS, EXPERTS])
        is_kth, picked = sb("r_is_kth", [T, NT, TOP * EXPERTS]), sb("r_picked", [T, NT, TOP * EXPERTS])
        row_of, row_i = sb("r_row", [T, NT, TOP]), sb("r_row_i", [T, NT * TOP], I32)
        token_i, entry = sb("r_token_i", [T, NT, TOP], I32), sb("r_entry", [T, NT, TOP, 2])
        blank = sb("r_blank", [P, SLOTS, 2])
        lists = sb("r_lists", [SLOTS, P, 2])
        consts, step, bias_in, exp_in, exp_done = sem("r_consts"), sem("r_step"), sem("r_bias_in"), sem("r_exp_in"), sem("r_exp_done")
        blank_set, blank_out, rows_ready, scattered = sem("r_blank_set"), sem("r_blank_out"), sem("r_rows_ready"), sem("r_scattered")
        sel_ready, counted, lists_in, lists_T, lists_done = sem("r_sel_ready"), sem("r_counted"), sem("r_lists_in"), sem("r_lists_T"), sem("r_lists_done")
        from_set = sem("r_from_set")
        block = ctx.block()
        y_dram = out.rearrange("(t p) d -> t p d", p=T)

        @block.sync
        def _(sp):
            def load_nT(t, b):
                load_tile(sp, nT_hi[:, b, :].bitcast(F32), scr["nT_hi"], t, nT_in[b])
                load_tile(sp, nT_lo[:, b, :].bitcast(F32), scr["nT_lo"], t, nT_in[b])

            def load_x1(t, b):
                load_tile(sp, y[:, b, :], scr["x1"], t, x1_in[b])

            sp.dma_start(bias[:, :], io["router_b"].to_broadcast([T, 1])).then_inc(bias_in, 16)
            for half in range(2):
                cs = slice(half * C // 2, (half + 1) * C // 2)
                for k, name in enumerate(("s_gate", "s_up")):
                    sp.dma_start(gu_raw[:, cs, k * SHARED:(k + 1) * SHARED],
                                 io[name].rearrange("(c p) n -> p c n", p=P)[:, cs, :]).then_inc(gu_in[half], 16)
                if half == 0:
                    load_nT(0, 0)
            sp.dma_start(d_raw[:, :, :], io["s_down"].rearrange("(c p) n -> p c n", p=P)).then_inc(d_in, 16)
            load_nT(1, 1)
            for b in range(2):
                load_x1(b, b)
            def load_expert(pieces):
                for k in pieces:
                    sp.dma_start(*scr["expert_pieces"](0)[k]).then_inc(scr["raw_in"][k], 16)

            def next_nT(t, b):
                sp.wait_ge(gu_mm, t + 1)
                load_nT(t + 2, b)

            def store_y(t, b, more):
                sp.wait_ge(y_done, 2 * t + 2)
                sp.dma_start(y_dram[bass.ds(t, 1), :, :].rearrange("o p d -> (o p) d"), y[:, b, :]).then_inc(stored[b], 16)
                if more:
                    sp.wait_ge(stored[b], 8 * (t - b) + 16)
                    load_x1(t + 2, b)

            next_nT(0, 0)
            next_nT(1, 1)
            load_expert(range(0, 3))
            store_y(0, 0, True)
            for t in range(2, 5):
                next_nT(t, t % 2)
                load_expert(range(3 * (t - 1), 3 * t))
                store_y(t - 1, (t - 1) % 2, True)
            next_nT(5, 1)
            store_y(4, 0, True)
            with sp.Fori(3, NT // 2 - 1) as i:
                for b in range(2):
                    next_nT(2 * i + b, b)
                    store_y(2 * i + b - 1, 1 - b, True)
            store_y(NT - 3, 1, True)
            for b in range(2):
                store_y(NT - 2 + b, b, False)
            for b in range(2):
                sp.wait_ge(stored[b], 8 * NT)

        @block.gpsimd
        def _(pool):
            nc.gpsimd.memset(blank[:, :, 0:1], float(FAR)).then_inc(blank_set, 1)
            nc.gpsimd.memset(blank[:, :, 1:2], 0.0).then_inc(blank_set, 1)
            pool.wait_ge(blank_set, 2)
            pool.dma_start(scr["lists"].rearrange("(p s) w -> p s w", p=P), blank[:, :, :]).then_inc(blank_out, 16)
            nc.gpsimd.iota(tri_i[:, :, :], pattern=[[1, EXPERTS], [-1, EXPERTS]], base=0, channel_multiplier=0).then_inc(consts, 1)
            nc.gpsimd.iota(full_i[:, :, :], pattern=[[0, EXPERTS], [P, NT]], base=0, channel_multiplier=0).then_inc(consts, 1)
            nc.gpsimd.iota(kth_i[:, :, :], pattern=[[1, TOP], [0, EXPERTS]], base=0, channel_multiplier=0).then_inc(consts, 1)
            nc.gpsimd.iota(below_i[:, :], pattern=[[1, T]], base=0, channel_multiplier=-1).then_inc(consts, 1)
            nc.gpsimd.iota(token_i[:, :, :], pattern=[[T, NT], [0, TOP]], base=0, channel_multiplier=1).then_inc(consts, 1)
            pool.wait_ge(rows_ready, 1)
            pool.wait_ge(blank_out, 16)
            for t in range(NT):
                for k in range(TOP):
                    n = t * TOP + k
                    pool.indirect_dma_start(out=scr["lists"], out_offset=bass.IndirectOffsetOnAxis(ap=row_i[:, n:n + 1].bitcast(U32), axis=0),
                                            in_=entry[:, t, k, :], in_offset=None).then_inc(scattered, 16)
            pool.wait_ge(scattered, 16 * NT * TOP)
            pool.dma_start(lists[:, :, :], scr["lists"].rearrange("(s r) w -> s r w", r=P)).then_inc(lists_in, 16)
            pool.wait_ge(lists_done, 1)
            nc.gpsimd.tensor_copy(scr["from_cell"][:, :], scr["from_rows"][:, 0:1]).then_inc(from_set, 1)
            pool.wait_ge(from_set, 1)
            gather_rows(pool, scr)

        @block.scalar
        def _(act):
            carrier = Carrier(nc, scr, act, "scalar")
            act.wait_ge(exp_in, 1)
            nc.scalar.activation(ez[:, :, :], sc[:, :, :], ACT.Exp).then_inc(exp_done, 1)
            for c in range(C):
                split(nc, act, None, gu_raw[:, c, :], gu_hi[:, c, :], None, gu_in[2 * c // C], 32, gu_hi_done, None, c)
            for c in range(2):
                split(nc, act, None, d_raw[:, c, :], d_hi[:, c, :], None, d_in, 16, d_hi_done, None, c)

            with act.Fori(0, NT // 2) as i:
                for b in range(2):
                    t = 2 * i + b
                    hold(carrier, gu_mm, t + 1)
                    nc.scalar.activation(sg[:, :], pgu[b][:, 0:SHARED], ACT.Silu).then_inc(sg_done, 1)
                    act.wait_ge(aT_mm, t + 1)
                    nc.scalar.copy(aT_hi[:, :], paT[:, :]).then_inc(aT_hi_done, 1)

        @block.vector
        def _(dve):
            n = [0]

            def link(ins):
                n[0] += 1
                ins.then_inc(step, 1)
                dve.wait_ge(step, n[0])

            inner = lambda t, shape: t.unsqueeze(len(t.shape)).to_broadcast(shape)
            every = lambda t, shape: t.unsqueeze(1).to_broadcast(shape)
            by_e = [T, NT, EXPERTS]
            logits = scr["logits"]
            def activate(t, b):
                dve.wait_ge(sg_done, t + 1)
                nc.vector.tensor_tensor(a[:, :], sg[:, :], pgu[b][:, SHARED:G], ALU.mult).then_inc(a_done, 1)

            def add_down(t, b):
                dve.wait_ge(x1_in[b], 8 * (t - b) + 16)
                for h in range(2):
                    at = slice(h * HALF, (h + 1) * HALF)
                    dve.wait_ge(y_mm, 2 * t + h + 1)
                    nc.vector.tensor_tensor(y[:, b, at], y[:, b, at], py[h][:, :], ALU.add).then_inc(y_done, 1)

            def low(t):
                dve.wait_ge(aT_hi_done, t + 1)
                nc.vector.tensor_tensor(aT_lo[:, :], paT[:, :], aT_hi[:, :].bitcast(F32), ALU.subtract).then_inc(aT_lo_done, 1)

            link(nc.vector.tensor_reduce(row_max[:, :], logits[:, :, :], AX, ALU.max))
            nc.vector.tensor_tensor(sc[:, :, :], logits[:, :, :], inner(row_max[:, :], by_e), ALU.subtract).then_inc(exp_in, 1)
            for c in range(C):
                split(nc, None, dve, gu_raw[:, c, :], gu_hi[:, c, :], gu_lo[:, c, :], None, 0, gu_hi_done, gu_lo_done, c)
            for c in range(2):
                split(nc, None, dve, d_raw[:, c, :], d_hi[:, c, :], d_lo[:, c, :], None, 0, d_hi_done, d_lo_done, c)

            dve.wait_ge(consts, 5)
            nc.vector.tensor_scalar(tri[:, :, :], tri_i[:, :, :], 0.0, None, ALU.is_gt)
            nc.vector.tensor_copy(full[:, :, :], full_i[:, :, :])
            nc.vector.tensor_copy(kth[:, :, :], kth_i[:, :, :])
            nc.vector.tensor_scalar(below[:, :], below_i[:, :], 0.0, None, ALU.is_gt)
            nc.vector.memset(all_ones[:, :], 1.0)
            nc.vector.tensor_copy(entry[:, :, :, 0], token_i[:, :, :])
            nc.vector.memset(before[:, 0, :], 0.0)
            dve.wait_ge(exp_done, 1)
            link(nc.vector.tensor_reduce(row_sum[:, :], ez[:, :, :], AX, ALU.add))
            link(nc.vector.reciprocal(row_max[:, :], row_sum[:, :]))
            link(nc.vector.tensor_tensor(ez[:, :, :], ez[:, :, :], inner(row_max[:, :], by_e), ALU.mult))
            dve.wait_ge(bias_in, 16)
            link(nc.vector.tensor_scalar(sc[:, :, :], ez[:, :, :], bias[:, 0:1], None, ALU.add))
            pair = [T, NT, EXPERTS, EXPERTS]
            view = lambda t: t[:, :, :].rearrange("p t (e f) -> p t e f", f=EXPERTS)
            own, other = sc[:, :, :].unsqueeze(3).to_broadcast(pair), sc[:, :, :].unsqueeze(2).to_broadcast(pair)
            nc.vector.tensor_tensor(view(gt), other, own, ALU.is_gt)
            link(nc.vector.tensor_tensor(view(eq), other, own, ALU.is_equal))
            flat_tri = tri[:, :, :].rearrange("p e f -> p (e f)")
            link(nc.vector.tensor_tensor(eq[:, :, :], eq[:, :, :], every(flat_tri, [T, NT, EXPERTS * EXPERTS]), ALU.mult))
            link(nc.vector.tensor_tensor(gt[:, :, :], gt[:, :, :], eq[:, :, :], ALU.add))
            link(nc.vector.tensor_reduce(rank[:, :, :], view(gt), AX, ALU.add))
            nc.vector.tensor_scalar(sel_b[:, :, :], rank[:, :, :], float(TOP), None, ALU.is_lt).then_inc(sel_ready, 1)
            link(nc.vector.tensor_scalar(sel[:, :, :], rank[:, :, :], float(TOP), None, ALU.is_lt))
            activate(0, 0)
            low(0)
            link(nc.vector.tensor_tensor(wts[:, :, :], ez[:, :, :], sel[:, :, :], ALU.mult))
            link(nc.vector.tensor_reduce(row_sum[:, :], wts[:, :, :], AX, ALU.add))
            link(nc.vector.tensor_scalar(row_sum[:, :], row_sum[:, :], 1e-20, None, ALU.add))
            link(nc.vector.reciprocal(row_max[:, :], row_sum[:, :]))
            link(nc.vector.tensor_tensor(wts[:, :, :], wts[:, :, :], inner(row_max[:, :], by_e), ALU.mult))
            dve.wait_ge(counted, 1)
            link(nc.vector.tensor_copy(within[:, :, :], pcount[:, :, :]))
            for t in range(NT):
                link(nc.vector.tensor_tensor(before[:, t + 1, :], before[:, t, :], within[:, 1, t * EXPERTS:(t + 1) * EXPERTS], ALU.add))
            link(nc.vector.tensor_tensor(over[:, :, :], inner(before[:, NT, :], [T, EXPERTS, NT]), full[:, :, :], ALU.is_gt))
            link(nc.vector.tensor_reduce(tiles[:, 0:EXPERTS], over[:, :, :], AX, ALU.add))
            link(nc.vector.tensor_scalar(tiles[:, 0:EXPERTS], tiles[:, 0:EXPERTS], 2.0, None, ALU.max))
            link(nc.vector.tensor_tensor(span[:, :, :], every(tiles[:, 0:EXPERTS], [T, EXPERTS, EXPERTS]), tri[:, :, :], ALU.mult))
            link(nc.vector.tensor_reduce(base[:, :], span[:, :, :], AX, ALU.add))
            link(nc.vector.tensor_tensor(tiles[:, EXPERTS:EXPERTS + 1], base[:, EXPERTS - 1:EXPERTS], tiles[:, EXPERTS - 1:EXPERTS], ALU.add))
            nc.vector.tensor_scalar(scr["tiles"][:, 0:EXPERTS], tiles[0:1, 0:EXPERTS], -2.0, None, ALU.add)
            nc.vector.tensor_scalar(scr["tiles"][:, EXPERTS:EXPERTS + 1], tiles[0:1, EXPERTS:EXPERTS + 1], -1.0, None, ALU.add)
            link(nc.vector.tensor_scalar(base[:, :], base[:, :], float(P), None, ALU.mult))
            link(nc.vector.tensor_tensor(pos[:, :, :], before[:, 0:NT, :], within[:, 0, :].rearrange("p (t e) -> p t e", e=EXPERTS), ALU.add))
            link(nc.vector.tensor_tensor(pos[:, :, :], pos[:, :, :], every(base[:, :], by_e), ALU.add))
            activate(1, 1)
            add_down(0, 0)
            low(1)
            four = [T, NT, TOP, EXPERTS]
            kview = lambda t: t[:, :, :].rearrange("p t (k e) -> p t k e", e=EXPERTS)
            over_k = lambda t: t[:, :, :].unsqueeze(2).to_broadcast(four)
            link(nc.vector.tensor_tensor(kview(is_kth), over_k(rank), kth[:, :, :].unsqueeze(1).to_broadcast(four), ALU.is_equal))
            link(nc.vector.tensor_tensor(kview(picked), kview(is_kth), over_k(pos), ALU.mult))
            link(nc.vector.tensor_reduce(row_of[:, :, :], kview(picked), AX, ALU.add))
            nc.vector.tensor_copy(row_i[:, :], row_of[:, :, :].rearrange("p t k -> p (t k)"))
            link(nc.vector.tensor_tensor(kview(picked), kview(is_kth), over_k(wts), ALU.mult))
            nc.vector.tensor_reduce(entry[:, :, :, 1], kview(picked), AX, ALU.add).then_inc(rows_ready, 1)

            def step_of(t, b):
                activate(t, b)
                add_down(t - 1, 1 - b)
                low(t)

            with dve.Fori(1, NT // 2 - 1) as i:
                for b in range(2):
                    step_of(2 * i + b, b)
            step_of(NT - 2, 0)
            dve.wait_ge(lists_T, 2)
            nc.vector.tensor_copy(scr["to_rows"][:, :], plist[:, 0, :])
            nc.vector.tensor_scalar(scr["from_rows"][:, :], plist[:, 0, :], float(N - 1), None, ALU.min)
            nc.vector.tensor_copy(scr["row_weights"][:, :], plist[:, 1, :]).then_inc(lists_done, 1)
            step_of(NT - 1, 1)
            add_down(NT - 1, 1)

        @block.tensor
        def _(pe):
            def gate_up(t, b, first=False):
                pe.wait_ge(nT_in[b], 16 * (t - b) + 32)
                for c in range(C):
                    if first:
                        pe.wait_ge(gu_lo_done, c + 1)
                    at = slice(c * T, (c + 1) * T)
                    m = mm3(pe, pgu[b][:, :], nT_hi[:, b, at], nT_lo[:, b, at], gu_hi[:, c, :], gu_lo[:, c, :], c == 0, c == C - 1)
                m.then_inc(gu_mm, 1)

            def down(t, first=False):
                if first:
                    pe.wait_ge(d_lo_done, 2)
                pe.wait_ge(aT_lo_done, t + 1)
                for h in range(2):
                    col = slice(h * HALF, (h + 1) * HALF)
                    if not first:
                        pe.wait_ge(y_done, 2 * t - 1 + h)
                    for c in range(2):
                        at = slice(c * T, (c + 1) * T)
                        m = mm3(pe, py[h][:, :], aT_hi[:, at], aT_lo[:, at], d_hi[:, c, col], d_lo[:, c, col], c == 0, c == 1)
                    m.then_inc(y_mm, 1)

            def turn(t):
                pe.wait_ge(a_done, t + 1)
                for c in range(2):
                    m = pe.transpose(paT[:, c * T:(c + 1) * T], a[:, c * P:(c + 1) * P], scr["ident"][0:T, 0:T])
                m.then_inc(aT_mm, 1)

            gate_up(0, 0, first=True)
            gate_up(1, 1)
            pe.wait_ge(sel_ready, 1)
            flat = sel_b[:, :, :].rearrange("p t e -> p (t e)")
            pe.matmul(pcount[:, 0, :], below[:, :], flat, start=True, stop=True)
            pe.matmul(pcount[:, 1, :], all_ones[:, :], flat, start=True, stop=True).then_inc(counted, 1)
            turn(0)
            down(0, first=True)
            turn(1)
            def step_of(t, b):
                gate_up(t, b)
                down(t - 1)
                turn(t)

            with pe.Fori(1, NT // 2 - 1) as i:
                for b in range(2):
                    step_of(2 * i + b, b)
            step_of(NT - 2, 0)
            pe.wait_ge(lists_in, 16)
            for w in range(2):
                pe.transpose(plist[:, w, :], lists[:, :, w], scr["ident"][0:SLOTS, 0:SLOTS]).then_inc(lists_T, 1)
            step_of(NT - 1, 1)
            down(NT - 1)


def gather_rows(pool, scr):
    pool.indirect_dma_start(out=scr["rows"][:, :], out_offset=None, in_=scr["xn2"],
                            in_offset=bass.IndirectOffsetOnAxis(ap=scr["from_cell"][:, 0:1].bitcast(U32), axis=0)).then_inc(scr["rows_in"], 16)


def experts(nc, scr, out):
    with Phase(nc) as ctx:
        sb = lambda n, s, d=F32: ctx.enter_context(nc.sbuf_tensor(n, s, d))
        ps = lambda n, s: ctx.enter_context(nc.psum_tensor(n, s, F32))
        sem = ctx.sem
        I4 = MOE // P
        gu_raw, d_raw, raw_in = scr["gu_raw"], scr["d_raw"], scr["raw_in"]
        gu_hi, gu_lo = sb("p7_gu_hi", [P, C, 2 * MOE], F32R), sb("p7_gu_lo", [P, C, 2 * MOE], F32R)
        d_hi, d_lo = sb("p7_d_hi", [P, I4, D], F32R), sb("p7_d_lo", [P, I4, D], F32R)
        x, y = scr["rows"], sb("p7_y", [P, D])
        xT_hi, xT_lo = sb("p7_xT_hi", [P, D], F32R), sb("p7_xT_lo", [P, D], F32R)
        sg, a = sb("p7_sg", [P, MOE]), sb("p7_a", [P, MOE])
        aT_hi, aT_lo = sb("p7_aT_hi", [P, MOE], F32R), sb("p7_aT_lo", [P, MOE], F32R)
        from_cell, to_cell = scr["from_cell"], sb("p7_to", [P, 1], I32)
        pg, pu, paT = ps("p7_g", [P, MOE]), ps("p7_u", [P, MOE]), ps("p7_aT", [P, MOE])
        pxT, py = [ps(f"p7_xT{h}", [P, HALF]) for h in range(2)], [ps(f"p7_y{h}", [P, HALF]) for h in range(2)]
        gu_hi_done, gu_lo_done, d_hi_done, d_lo_done = sem("p7_gu_hi_done"), sem("p7_gu_lo_done"), sem("p7_d_hi_done"), sem("p7_d_lo_done")
        x_in, xT_mm, xT_hi_done, xT_lo_done = scr["rows_in"], sem("p7_xT_mm"), sem("p7_xT_hi_done"), sem("p7_xT_lo_done")
        gu_mm, sg_done, a_done = sem("p7_gu_mm"), sem("p7_sg_done"), sem("p7_a_done")
        aT_mm, aT_hi_done, aT_lo_done = sem("p7_aT_mm"), sem("p7_aT_hi_done"), sem("p7_aT_lo_done")
        y_mm, y_act, y_dve, y_out, y_free = sem("p7_y_mm"), sem("p7_y_act"), sem("p7_y_dve"), sem("p7_y_out"), sem("p7_y_free")
        from_set, to_set = sem("p7_from_set"), sem("p7_to_set")
        block = ctx.block()

        def by_expert(eng, first, middle, last):
            with eng.register("p7_done") as done:
                eng.reg_mov(done, 0)

                def one(e, opening, more):
                    between = eng.value_load(scr["tiles"][0:1, bass.ds(e, 1)], min_val=0, max_val=NT - 2)
                    before = None if opening else eng.snap(done)
                    start = eng.snap(done) if opening else eng.snap(before + 1)
                    first(e, before, start)
                    with eng.If(between > 0):
                        with eng.Fori(0, between) as t:
                            middle(e, eng.snap(start + t), eng.snap(start + t + 1))
                    g = eng.snap(start + between + 1)
                    last(e, eng.snap(start + between), g, more)
                    eng.reg_add(done, done, between)
                    eng.reg_add(done, done, 1 if opening else 2)
                    return g
                one(0, True, True)
                with eng.Fori(1, EXPERTS - 1) as e:
                    one(e, False, True)
                return one(EXPERTS - 1, False, False)

        @block.sync
        def _(sp):
            with sp.Fori(0, EXPERTS - 1) as e:
                for k, (raw, src) in enumerate(scr["expert_pieces"](e + 1)):
                    if k < C:
                        sp.wait_ge(gu_lo_done, C * e + k + 1)
                    else:
                        sp.wait_ge(d_lo_done, I4 * e + k - C + 1)
                    sp.dma_start(raw, src).then_inc(raw_in[k], 16)

        @block.gpsimd
        def _(pool):
            others = pool.value_load(scr["tiles"][0:1, EXPERTS:EXPERTS + 1], min_val=2 * EXPERTS - 1, max_val=SLOTS - 4)
            for s in (y_act, y_dve, y_free):
                pool.sem_inc(s, 1)

            carrier = Carrier(nc, scr, pool, "gpsimd")

            def gather(g):
                pool.wait_ge(x_in, 16 * g)
                hold(carrier, xT_mm, 2 * g)
                nc.gpsimd.tensor_copy(from_cell[:, :], scr["from_rows"][:, bass.ds(g, 1)]).then_inc(from_set, 1)
                hold(carrier, from_set, g)
                gather_rows(pool, scr)

            def scatter(g):
                pool.wait_ge(y_act, g + 2)
                hold(carrier, y_dve, g + 2)
                nc.gpsimd.tensor_copy(to_cell[:, :], scr["to_rows"][:, bass.ds(g, 1)]).then_inc(to_set, 1)
                hold(carrier, to_set, g + 1)
                pool.indirect_dma_start(out=out, out_offset=bass.IndirectOffsetOnAxis(ap=to_cell[:, 0:1].bitcast(U32), axis=0),
                                        in_=y[:, :], in_offset=None, bounds_check=N - 1, oob_is_err=False, compute_op=ALU.add).then_inc(y_out, 16)
                hold(carrier, y_out, 16 * g + 16).then_inc(y_free, 1)

            gather(1)
            gather(2)
            with pool.Fori(0, others) as g:
                gather(pool.snap(g + 3))
                scatter(g)
            scatter(others)

        @block.scalar
        def _(act):
            carrier = Carrier(nc, scr, act, "scalar")

            def split_gu(e):
                for c in range(C):
                    act.wait_ge(raw_in[c], 16 * e + 16)
                    nc.scalar.copy(gu_hi[:, c, :], gu_raw[:, c, :]).then_inc(gu_hi_done, 1)

            def split_d(e):
                for c in range(I4):
                    act.wait_ge(raw_in[C + c], 16 * e + 16)
                    nc.scalar.copy(d_hi[:, c, :], d_raw[:, c, :]).then_inc(d_hi_done, 1)

            def x_high(g):
                for h in range(2):
                    act.wait_ge(xT_mm, 2 * g + h + 1)
                    nc.scalar.copy(xT_hi[:, h * HALF:(h + 1) * HALF], pxT[h][:, :]).then_inc(xT_hi_done, 1)

            def silu(g):
                hold(carrier, gu_mm, 2 * g + 1)
                nc.scalar.activation(sg[:, :], pg[:, :], ACT.Silu).then_inc(sg_done, 1)

            def weigh(g):
                act.wait_ge(y_free, g + 1)
                hold(carrier, y_mm, 2 * g + 1)
                nc.scalar.activation(y[:, 0:HALF], py[0][:, :], ACT.Copy, scale=scr["row_weights"][:, bass.ds(g, 1)]).then_inc(y_act, 1)

            def a_high(g):
                act.wait_ge(aT_mm, g + 1)
                nc.scalar.copy(aT_hi[:, :], paT[:, :]).then_inc(aT_hi_done, 1)

            def middle(e, before, g):
                silu(g)
                x_high(g + 1)
                if before is not None:
                    weigh(before)
                a_high(g)

            def first(e, before, g):
                middle(e, before, g)
                if before is not None:
                    split_d(e)

            def last(e, before, g, more):
                silu(g)
                x_high(g + 1)
                if more:
                    split_gu(e + 1)
                weigh(before)
                a_high(g)

            x_high(0)
            split_gu(0)
            split_d(0)
            weigh(by_expert(act, first, middle, last))

        @block.vector
        def _(dve):
            def split_gu(e):
                for c in range(C):
                    dve.wait_ge(gu_hi_done, C * e + c + 1)
                    nc.vector.tensor_tensor(gu_lo[:, c, :], gu_raw[:, c, :], gu_hi[:, c, :].bitcast(F32), ALU.subtract).then_inc(gu_lo_done, 1)

            def split_d(e):
                for c in range(I4):
                    dve.wait_ge(d_hi_done, I4 * e + c + 1)
                    nc.vector.tensor_tensor(d_lo[:, c, :], d_raw[:, c, :], d_hi[:, c, :].bitcast(F32), ALU.subtract).then_inc(d_lo_done, 1)

            def x_low(g):
                for h in range(2):
                    dve.wait_ge(xT_hi_done, 2 * g + h + 1)
                    at = slice(h * HALF, (h + 1) * HALF)
                    nc.vector.tensor_tensor(xT_lo[:, at], pxT[h][:, :], xT_hi[:, at].bitcast(F32), ALU.subtract).then_inc(xT_lo_done, 1)

            def multiply(g):
                dve.wait_ge(sg_done, g + 1)
                dve.wait_ge(gu_mm, 2 * g + 2)
                nc.vector.tensor_tensor(a[:, :], sg[:, :], pu[:, :], ALU.mult).then_inc(a_done, 1)

            def weigh(g):
                dve.wait_ge(y_free, g + 1)
                dve.wait_ge(y_mm, 2 * g + 2)
                nc.vector.tensor_scalar(y[:, HALF:D], py[1][:, :], scr["row_weights"][:, bass.ds(g, 1)], None, ALU.mult).then_inc(y_dve, 1)

            def a_low(g):
                dve.wait_ge(aT_hi_done, g + 1)
                nc.vector.tensor_tensor(aT_lo[:, :], paT[:, :], aT_hi[:, :].bitcast(F32), ALU.subtract).then_inc(aT_lo_done, 1)

            def middle(e, before, g):
                multiply(g)
                x_low(g + 1)
                if before is not None:
                    weigh(before)
                a_low(g)

            def first(e, before, g):
                middle(e, before, g)
                if before is not None:
                    split_d(e)

            def last(e, before, g, more):
                multiply(g)
                x_low(g + 1)
                if more:
                    split_gu(e + 1)
                weigh(before)
                a_low(g)

            x_low(0)
            split_gu(0)
            split_d(0)
            weigh(by_expert(dve, first, middle, last))

        @block.tensor
        def _(pe):
            def turn_x(g):
                pe.wait_ge(x_in, 16 * g + 16)
                for c in range(C):
                    m = pe.transpose(pxT[c // 4][:, (c % 4) * P:(c % 4 + 1) * P], x[:, c * P:(c + 1) * P], scr["ident"][:, :])
                    if c % 4 == 3:
                        m.then_inc(xT_mm, 1)

            def gate_up(e, g, first):
                pe.wait_ge(xT_lo_done, 2 * g + 2)
                for k, acc in enumerate((pg, pu)):
                    for c in range(C):
                        if first and k == 0:
                            pe.wait_ge(gu_lo_done, C * e + c + 1)
                        at, col = slice(c * P, (c + 1) * P), slice(k * MOE, (k + 1) * MOE)
                        m = mm3(pe, acc[:, :], xT_hi[:, at], xT_lo[:, at], gu_hi[:, c, col], gu_lo[:, c, col], c == 0, c == C - 1)
                    m.then_inc(gu_mm, 1)

            def down(e, g):
                pe.wait_ge(aT_lo_done, g + 1)
                pe.wait_ge(y_act, g + 1)
                pe.wait_ge(y_dve, g + 1)
                pe.wait_ge(d_lo_done, I4 * e + I4)
                for h in range(2):
                    col = slice(h * HALF, (h + 1) * HALF)
                    for c in range(I4):
                        at = slice(c * P, (c + 1) * P)
                        m = mm3(pe, py[h][:, :], aT_hi[:, at], aT_lo[:, at], d_hi[:, c, col], d_lo[:, c, col], c == 0, c == I4 - 1)
                    m.then_inc(y_mm, 1)

            def turn_a(g):
                pe.wait_ge(a_done, g + 1)
                for c in range(I4):
                    m = pe.transpose(paT[:, c * P:(c + 1) * P], a[:, c * P:(c + 1) * P], scr["ident"][:, :])
                m.then_inc(aT_mm, 1)

            def first(e, before, g):
                gate_up(e, g, True)
                turn_x(g + 1)
                if before is not None:
                    down(e - 1, before)
                turn_a(g)

            def middle(e, before, g):
                gate_up(e, g, False)
                turn_x(g + 1)
                down(e, before)
                turn_a(g)

            def last(e, before, g, more):
                middle(e, before, g)

            turn_x(0)
            down(EXPERTS - 1, by_expert(pe, first, middle, last))


def program(nc, io, out):
    with ExitStack() as ctx:
        sem = lambda n: ctx.enter_context(nc.semaphore(n))
        scr = {}
        for name in ("xT_hi", "xT_lo"):
            scr[name] = nc.dram_tensor(name, (NT, P, C * T), F32).ap()
        scr["M"] = nc.dram_tensor("M", (C, P, D), F32).ap()
        for name in ("AT_hi", "AT_lo"):
            scr[name] = nc.dram_tensor(name, (NT, T, NT, T), F32).ap()
        scr["zero"] = ctx.enter_context(nc.sbuf_tensor("zero", [P, P], BF16))
        scr["ident"] = ctx.enter_context(nc.sbuf_tensor("ident", [P, P], F32))
        scr["spare"] = ctx.enter_context(nc.sbuf_tensor("spare", [1, 96], F32))
        scr["spare_used"] = 1
        scr["go"] = sem("go")
        ident_zero = sem("ident_zero")
        with nc.Block() as block:
            @block.gpsimd
            def _(pool):
                nc.gpsimd.memset(scr["spare"][:, :], 0.0)
                nc.gpsimd.memset(scr["zero"][:, :], 0.0)
                nc.gpsimd.memset(scr["ident"][:, :], 0.0).then_inc(ident_zero, 1)
                pool.wait_ge(ident_zero, 1)
                nc.gpsimd.affine_select(out=scr["ident"][:, :], in_=scr["ident"][:, :], compare_op=ALU.not_equal, fill=1.0,
                                        base=0, pattern=[[-1, P]], channel_multiplier=1).then_inc(scr["go"], 1)
        scr["x1"] = nc.dram_tensor("x1", (NT, T, D), F32).ap()
        scr["xn2"] = nc.dram_tensor("xn2", (N, D), F32).ap()
        for name in ("nT_hi", "nT_lo"):
            scr[name] = nc.dram_tensor(name, (NT, P, C * T), F32).ap()
        scr["wide"] = ctx.enter_context(nc.sbuf_tensor("wide", [1, 1], I32))
        scr["dinv"] = ctx.enter_context(nc.sbuf_tensor("dinv", [T, NT], F32))
        scr["logits"] = ctx.enter_context(nc.sbuf_tensor("logits", [T, NT, EXPERTS], F32))
        matrix_scope = ExitStack()
        with ExitStack() as kv_scope:
            scr["kvT"] = kv_scope.enter_context(nc.sbuf_tensor("kvT", [P, D], F32))
            project_kv(nc, io, scr)
            for part in ("matrix_hi", "matrix_lo"):
                scr[part] = matrix_scope.enter_context(nc.sbuf_tensor(part, [P, C, D], F32R, side="right"))
            scr["matrix_raw"] = before_split(nc, "matrix_raw", scr["matrix_lo"])
            scr["wg_in"] = [sem(f"wg_in{c}") for c in range(C)]
            mixing_and_adjacency(nc, io, scr)
        with ExitStack() as hs_scope:
            scr["hs_hi"] = hs_scope.enter_context(nc.sbuf_tensor("hs_hi", [T, NT, D], F32R))
            scr["hs_lo"] = hs_scope.enter_context(nc.sbuf_tensor("hs_lo", [T, NT, D], F32R))
            scr["at_hi"] = hs_scope.enter_context(nc.sbuf_tensor("at_hi", [T, 2, NT * T], F32R))
            scr["at_in"] = [sem(f"at_in{b}") for b in range(2)]
            node_features(nc, io, scr)
            matrix_scope.close()
            aggregate_and_mix(nc, io, scr)
        scr["lists"] = nc.dram_tensor("lists", (SLOTS * P, 2), F32).ap()
        scr["tiles"] = ctx.enter_context(nc.sbuf_tensor("tiles", [1, EXPERTS + 1], I32))
        scr["to_rows"] = ctx.enter_context(nc.sbuf_tensor("to_rows", [P, SLOTS], I32))
        scr["from_rows"] = ctx.enter_context(nc.sbuf_tensor("from_rows", [P, SLOTS], I32))
        scr["row_weights"] = ctx.enter_context(nc.sbuf_tensor("row_weights", [P, SLOTS], F32))
        scr["rows"], scr["rows_in"] = ctx.enter_context(nc.sbuf_tensor("rows", [P, D], F32)), sem("rows_in")
        scr["from_cell"] = ctx.enter_context(nc.sbuf_tensor("from_cell", [P, 1], I32))
        gu_raw = scr["gu_raw"] = ctx.enter_context(nc.sbuf_tensor("gu_raw", [P, C, 2 * MOE], F32))
        d_raw = scr["d_raw"] = ctx.enter_context(nc.sbuf_tensor("d_raw", [P, MOE // P, D], F32))
        scr["raw_in"] = [sem(f"raw_in{k}") for k in range(C + MOE // P)]
        downs = io["down"].rearrange("e (c p) n -> e c p n", p=P)

        def expert_pieces(e):
            pick = lambda t, c: t[bass.ds(e, 1), c, :, :].rearrange("o p n -> (o p) n")
            out_ = [(gu_raw[:, c, :], pick(io["gate_up"].rearrange("e (c p) n -> e c p n", p=P), c)) for c in range(C)]
            return out_ + [(d_raw[:, c, :], pick(downs, c)) for c in range(MOE // P)]
        scr["expert_pieces"] = expert_pieces
        shared_and_routing(nc, io, scr, out)
        experts(nc, scr, out)


def kernel(**a):
    import numpy as np
    import concourse.bacc as bacc
    from concourse.bass_utils import run_bass_kernel_spmd as run

    lay = {k: np.asarray(v) for k, v in a.items()}
    arrays = {
        "x": lay["x"], "src": lay["src"].reshape(160, 125).T, "dst": lay["dst"].reshape(160, 125).T,
        "wgT": lay["L0_gnn_W"].T, "gb": lay["L0_gnn_b"].reshape(1, D),
        "wkT": lay["L0_mix_W_k"].T, "wvT": lay["L0_mix_W_v"].T, "wq": lay["L0_mix_W_q"], "woT": lay["L0_mix_W_o"].T,
        "router": lay["L0_ffn_router_w"], "router_b": lay["L0_ffn_router_bias"].reshape(1, 1),
        "gate_up": np.concatenate([lay["L0_ffn_gate_w"], lay["L0_ffn_up_w"]], axis=2), "down": lay["L0_ffn_down_w"],
        "s_gate": lay["L0_ffn_s_gate_w"], "s_up": lay["L0_ffn_s_up_w"], "s_down": lay["L0_ffn_s_down_w"],
    }
    nc = bacc.Bacc("TRN2", target_bir_lowering=False, num_devices=1)
    arrays = {f"in_{k}": np.ascontiguousarray(v) for k, v in arrays.items()}
    io = {k[3:]: nc.dram_tensor(k, v.shape, mybir.dt.from_np(v.dtype), kind="ExternalInput").ap() for k, v in arrays.items()}
    out = nc.dram_tensor("out_x", (N, D), F32, kind="ExternalOutput").ap()
    program(nc, io, out)
    r = run(nc, [arrays], core_ids=[0])
    return r.results[0]["out_x"]
```
